# Optimizing a Trainium2 kernel written in Bass

```python
import numpy as np
import jax
import jax.numpy as jnp

def _softmax(x, axis=-1):
    return jax.nn.softmax(x, axis=axis)

def _gelu(x):
    return jax.nn.gelu(x, approximate=True)

def _silu(x):
    return jax.nn.silu(x)

def _sigmoid(x):
    return jax.nn.sigmoid(x)

def _layernorm(x, axis=-1, eps=1e-05):
    m = jnp.mean(x, axis=axis, keepdims=True)
    v = jnp.var(x, axis=axis, keepdims=True)
    return (x - m) / jnp.sqrt(v + eps)

def _scatter_add(tgt, idx, src, axis=0):
    return tgt.at[idx].add(src)

def _segment_sum(src, seg, n):
    return jax.ops.segment_sum(src, seg, n)
kernel_name = 'mk_gnn_preln_d4_gnn_r64_4ec2b2'

def setup_inputs(seed: int=0):
    np.random.seed(seed)
    _w = jnp.asarray

    def _rec_inputs():
        import jax
        import jax.numpy as jnp
        _gk = jax.random.key(seed)
        x = -0.0005121 + 1.001 * jax.random.normal(jax.random.fold_in(_gk, 1), (100000, 32), jnp.float32)
        src = jax.random.randint(jax.random.fold_in(_gk, 2), (25000,), 0, 100000, jnp.int32)
        dst = jnp.minimum((100000 * jax.random.uniform(jax.random.fold_in(_gk, 3), (25000,)) ** 2.0).astype(jnp.int32), 99999)
        _o = jnp.argsort(dst, stable=True)
        src = src[_o]
        dst = dst[_o]
        edge_attr_16 = 0.000196303 + 1.00016 * jax.random.normal(jax.random.fold_in(_gk, 11), (25000, 16), jnp.float32)
        edge_attr_3 = jax.random.uniform(jax.random.fold_in(_gk, 12), (25000, 3), jnp.float32, 0.0, 1)
        return (x, src, dst, edge_attr_16, edge_attr_3)
    x, src, dst, edge_attr_16, edge_attr_3 = _rec_inputs()

    def _L0_gnn_setup():
        import jax, jax.numpy as jnp
        import numpy as np
        N, F, D, O, E = (100000, 32, 3, 32, 25000)
        key = jax.random.key(seed)
        k = jax.random.split(key, 7)
        x = jax.random.normal(k[0], (N, F), dtype=jnp.float32)
        edge_index = jax.random.randint(k[1], (2, E), 0, N, dtype=jnp.int64)
        pseudo = jax.random.uniform(k[2], (E, D), dtype=jnp.float32)
        bound = 1.0 / np.sqrt(F)
        mu = jax.random.uniform(k[3], (F, D), minval=-bound, maxval=bound, dtype=jnp.float32)
        sigma = jax.random.uniform(k[4], (F, D), minval=0.1, maxval=1.0, dtype=jnp.float32)
        W = jax.random.uniform(k[5], (O, F), minval=-bound, maxval=bound, dtype=jnp.float32)
        b = jax.random.uniform(k[6], (O,), minval=-bound, maxval=bound, dtype=jnp.float32)
        return {'x': x, 'edge_index': edge_index, 'pseudo': pseudo, 'mu': mu, 'sigma': sigma, 'W': W, 'b': b}
    _L0_gnn_all = _L0_gnn_setup()
    _L0_gnn_in = {k: v for k, v in _L0_gnn_all.items() if k in ('mu', 'sigma', 'W', 'b')}
    del _L0_gnn_all

    def _L1_gnn_setup():
        import jax, jax.numpy as jnp
        import numpy as np
        N = 50000
        E = 25000
        C = 32
        KS = 4
        DIM = 3
        K3 = KS ** DIM
        NEG = 0.01
        EPS = 1e-05
        _BITS = np.array([[s >> d & 1 for d in range(DIM)] for s in range(2 ** DIM)], dtype=np.int32)

        def _basis(edge_attr):
            v = edge_attr * (KS - 1)
            lo = jnp.floor(v)
            f = v - lo
            lo = lo.astype(jnp.int32)
            bits = jnp.asarray(_BITS)
            idx = jnp.clip(lo[:, None, :] + bits[None], 0, KS - 1)
            w = jnp.where(bits[None] == 1, f[:, None, :], 1.0 - f[:, None, :])
            basis = jnp.prod(w, axis=-1)
            wi = idx[..., 0] + KS * idx[..., 1] + KS * KS * idx[..., 2]
            return (basis, wi)

        def _sconv(x, src, dst, basis, wi, W, R, b):
            n = x.shape[0]
            z = jnp.einsum('nc,kco->nko', x, W)
            msg = jnp.zeros((src.shape[0], W.shape[2]), x.dtype)
            for s in range(basis.shape[1]):
                msg = msg + basis[:, s, None] * z[src, wi[:, s]]
            agg = jax.ops.segment_sum(msg, dst, num_segments=n)
            cnt = jax.ops.segment_sum(jnp.ones((dst.shape[0],), x.dtype), dst, num_segments=n)
            agg = agg / jnp.clip(cnt, 1.0)[:, None]
            return agg + x @ R + b

        def _bn(x, g, be):
            mu = x.mean(0)
            var = x.var(0)
            return (x - mu) * jax.lax.rsqrt(var + EPS) * g + be

        def _leaky(x):
            return jnp.where(x >= 0, x, NEG * x)
        key = jax.random.key(seed)
        ks = jax.random.split(key, 32)
        inp = {'patch_embs': jax.random.normal(ks[0], (N, C), jnp.float32), 'edge_index': jax.random.randint(ks[1], (2, E), 0, N, jnp.int32), 'edge_attr': jax.random.uniform(ks[2], (E, DIM), jnp.float32)}
        i = 3
        for l in (1, 2, 3):
            inp[f'W{l}'] = jax.random.normal(ks[i], (K3, C, C), jnp.float32) * 0.05
            i += 1
            inp[f'R{l}'] = jax.random.normal(ks[i], (C, C), jnp.float32) * 0.1
            i += 1
            inp[f'b{l}'] = jnp.zeros((C,), jnp.float32)
            inp[f'g{l}'] = jnp.ones((C,), jnp.float32)
            inp[f'be{l}'] = jnp.zeros((C,), jnp.float32)
        return inp
    _L1_gnn_all = _L1_gnn_setup()
    _L1_gnn_in = {k: v for k, v in _L1_gnn_all.items() if k in ('W1', 'R1', 'b1', 'g1', 'be1', 'W2', 'R2', 'b2', 'g2', 'be2', 'W3', 'R3', 'b3', 'g3', 'be3')}
    del _L1_gnn_all

    def _L2_gnn_setup():
        import jax, jax.numpy as jnp
        import numpy as np
        N_LAYERS = 3
        N_NODES = 500000
        N_EDGES = 2500000
        EMBED_DIM = 32
        key = jax.random.key(seed)
        k_w, k_e = jax.random.split(key)
        weight = jax.random.normal(k_w, (N_NODES, EMBED_DIM), dtype=jnp.float32) * 0.1
        edge_index = jax.random.randint(k_e, (2, N_EDGES), 0, N_NODES, dtype=jnp.int32)
        return {'weight': weight, 'edge_index': edge_index}
    _L2_gnn_all = _L2_gnn_setup()
    _L2_gnn_in = {k: v for k, v in _L2_gnn_all.items() if k in ()}
    del _L2_gnn_all

    def _L3_gnn_setup():
        import jax, jax.numpy as jnp
        import numpy as np
        N = 50000
        E = 25000
        DN = 32
        DE = 16
        DI = DN + DE
        DH = 2 * DI

        def _linear_params(key, fan_in, fan_out, dtype=jnp.float32):
            k1, k2 = jax.random.split(key)
            bound = 1.0 / np.sqrt(fan_in)
            w = jax.random.uniform(k1, (fan_in, fan_out), dtype, -bound, bound)
            b = jax.random.uniform(k2, (fan_out,), dtype, -bound, bound)
            return (w, b)
        key = jax.random.key(seed)
        ks = jax.random.split(key, 7)
        x = jax.random.normal(ks[0], (N, DN), dtype=jnp.float32)
        edge_index = jax.random.randint(ks[1], (2, E), 0, N, dtype=jnp.int64)
        edge_attr = jax.random.normal(ks[2], (E, DE), dtype=jnp.float32)
        w1a, b1a = _linear_params(ks[3], DI, DH)
        w1b, b1b = _linear_params(ks[4], DH, DH)
        w2a, b2a = _linear_params(ks[5], DN + DH, DI)
        w2b, b2b = _linear_params(ks[6], DI, DN)
        return {'x': x, 'edge_index': edge_index, 'edge_attr': edge_attr, 'w1a': w1a, 'b1a': b1a, 'w1b': w1b, 'b1b': b1b, 'w2a': w2a, 'b2a': b2a, 'w2b': w2b, 'b2b': b2b}
    _L3_gnn_all = _L3_gnn_setup()
    _L3_gnn_in = {k: v for k, v in _L3_gnn_all.items() if k in ('w1a', 'b1a', 'w1b', 'b1b', 'w2a', 'b2a', 'w2b', 'b2b')}
    del _L3_gnn_all
    return {'x': x, 'src': src, 'dst': dst, 'edge_attr_16': edge_attr_16, 'edge_attr_3': edge_attr_3, 'L0_gnn_mu': _L0_gnn_in['mu'], 'L0_gnn_sigma': _L0_gnn_in['sigma'], 'L0_gnn_W': _L0_gnn_in['W'], 'L0_gnn_b': _L0_gnn_in['b'], 'L1_gnn_W1': _L1_gnn_in['W1'], 'L1_gnn_R1': _L1_gnn_in['R1'], 'L1_gnn_b1': _L1_gnn_in['b1'], 'L1_gnn_g1': _L1_gnn_in['g1'], 'L1_gnn_be1': _L1_gnn_in['be1'], 'L1_gnn_W2': _L1_gnn_in['W2'], 'L1_gnn_R2': _L1_gnn_in['R2'], 'L1_gnn_b2': _L1_gnn_in['b2'], 'L1_gnn_g2': _L1_gnn_in['g2'], 'L1_gnn_be2': _L1_gnn_in['be2'], 'L1_gnn_W3': _L1_gnn_in['W3'], 'L1_gnn_R3': _L1_gnn_in['R3'], 'L1_gnn_b3': _L1_gnn_in['b3'], 'L1_gnn_g3': _L1_gnn_in['g3'], 'L1_gnn_be3': _L1_gnn_in['be3'], 'L3_gnn_w1a': _L3_gnn_in['w1a'], 'L3_gnn_b1a': _L3_gnn_in['b1a'], 'L3_gnn_w1b': _L3_gnn_in['w1b'], 'L3_gnn_b1b': _L3_gnn_in['b1b'], 'L3_gnn_w2a': _L3_gnn_in['w2a'], 'L3_gnn_b2a': _L3_gnn_in['b2a'], 'L3_gnn_w2b': _L3_gnn_in['w2b'], 'L3_gnn_b2b': _L3_gnn_in['b2b']}

def reference(x, src, dst, edge_attr_16, edge_attr_3, L0_gnn_mu, L0_gnn_sigma, L0_gnn_W, L0_gnn_b, L1_gnn_W1, L1_gnn_R1, L1_gnn_b1, L1_gnn_g1, L1_gnn_be1, L1_gnn_W2, L1_gnn_R2, L1_gnn_b2, L1_gnn_g2, L1_gnn_be2, L1_gnn_W3, L1_gnn_R3, L1_gnn_b3, L1_gnn_g3, L1_gnn_be3, L3_gnn_w1a, L3_gnn_b1a, L3_gnn_w1b, L3_gnn_b1b, L3_gnn_w2a, L3_gnn_b2a, L3_gnn_w2b, L3_gnn_b2b):
    import jax
    import jax.numpy as jnp

    def _L0_gnn_ref(x, edge_index, pseudo, mu, sigma, W, b):
        import jax, jax.numpy as jnp
        import numpy as np
        N, F, D, O, E = (100000, 32, 3, 32, 25000)
        row, col = (edge_index[0], edge_index[1])
        diff = pseudo[:, None, :] - mu[None, :, :]
        logw = jnp.sum(-0.5 * diff ** 2 / (1e-14 + sigma[None] ** 2), axis=-1)
        gaussian = jnp.exp(logw)
        msg = x[col] * gaussian
        out = jax.ops.segment_sum(msg, row, num_segments=x.shape[0])
        return out @ W.T + b

    def _L1_gnn_ref(patch_embs, edge_index, edge_attr, W1, R1, b1, g1, be1, W2, R2, b2, g2, be2, W3, R3, b3, g3, be3):
        import jax, jax.numpy as jnp
        import numpy as np
        N = 50000
        E = 25000
        C = 32
        KS = 4
        DIM = 3
        K3 = KS ** DIM
        NEG = 0.01
        EPS = 1e-05
        _BITS = np.array([[s >> d & 1 for d in range(DIM)] for s in range(2 ** DIM)], dtype=np.int32)

        def _basis(edge_attr):
            v = edge_attr * (KS - 1)
            lo = jnp.floor(v)
            f = v - lo
            lo = lo.astype(jnp.int32)
            bits = jnp.asarray(_BITS)
            idx = jnp.clip(lo[:, None, :] + bits[None], 0, KS - 1)
            w = jnp.where(bits[None] == 1, f[:, None, :], 1.0 - f[:, None, :])
            basis = jnp.prod(w, axis=-1)
            wi = idx[..., 0] + KS * idx[..., 1] + KS * KS * idx[..., 2]
            return (basis, wi)

        def _sconv(x, src, dst, basis, wi, W, R, b):
            n = x.shape[0]
            z = jnp.einsum('nc,kco->nko', x, W)
            msg = jnp.zeros((src.shape[0], W.shape[2]), x.dtype)
            for s in range(basis.shape[1]):
                msg = msg + basis[:, s, None] * z[src, wi[:, s]]
            agg = jax.ops.segment_sum(msg, dst, num_segments=n)
            cnt = jax.ops.segment_sum(jnp.ones((dst.shape[0],), x.dtype), dst, num_segments=n)
            agg = agg / jnp.clip(cnt, 1.0)[:, None]
            return agg + x @ R + b

        def _bn(x, g, be):
            mu = x.mean(0)
            var = x.var(0)
            return (x - mu) * jax.lax.rsqrt(var + EPS) * g + be

        def _leaky(x):
            return jnp.where(x >= 0, x, NEG * x)
        src, dst = (edge_index[0], edge_index[1])
        basis, wi = _basis(edge_attr)
        x = _bn(_leaky(_sconv(patch_embs, src, dst, basis, wi, W1, R1, b1)) + patch_embs, g1, be1)
        x = _bn(_leaky(_sconv(x, src, dst, basis, wi, W2, R2, b2)) + x, g2, be2)
        x = _bn(_sconv(x, src, dst, basis, wi, W3, R3, b3) + x, g3, be3)
        return x

    def _L2_gnn_ref(weight, edge_index):
        import jax, jax.numpy as jnp
        import numpy as np
        N_LAYERS = 3
        N_NODES = 500000
        N_EDGES = 2500000
        EMBED_DIM = 32
        src, dst = (edge_index[0], edge_index[1])
        n = weight.shape[0]
        deg = jax.ops.segment_sum(jnp.ones(src.shape, dtype=weight.dtype), dst, num_segments=n)
        deg_inv_sqrt = jnp.where(deg > 0, jax.lax.rsqrt(deg), jnp.zeros((), weight.dtype))
        norm = deg_inv_sqrt[src] * deg_inv_sqrt[dst]
        x = weight
        acc = weight
        for _ in range(N_LAYERS):
            msgs = norm[:, None] * x[src]
            x = jax.ops.segment_sum(msgs, dst, num_segments=n)
            acc = acc + x
        return acc / (N_LAYERS + 1)

    def _L3_gnn_ref(x, edge_index, edge_attr, w1a, b1a, w1b, b1b, w2a, b2a, w2b, b2b):
        import jax, jax.numpy as jnp
        import numpy as np
        N = 50000
        E = 25000
        DN = 32
        DE = 16
        DI = DN + DE
        DH = 2 * DI

        def _linear_params(key, fan_in, fan_out, dtype=jnp.float32):
            k1, k2 = jax.random.split(key)
            bound = 1.0 / np.sqrt(fan_in)
            w = jax.random.uniform(k1, (fan_in, fan_out), dtype, -bound, bound)
            b = jax.random.uniform(k2, (fan_out,), dtype, -bound, bound)
            return (w, b)
        row = edge_index[0]
        col = edge_index[1]
        h = jnp.concatenate([x[row], edge_attr], axis=1)
        h = jnp.maximum(h @ w1a + b1a, 0.0)
        h = h @ w1b + b1b
        s = jax.ops.segment_sum(h, col, num_segments=x.shape[0])
        cnt = jax.ops.segment_sum(jnp.ones((col.shape[0],), x.dtype), col, num_segments=x.shape[0])
        agg = s / jnp.maximum(cnt, 1.0)[:, None]
        h2 = jnp.concatenate([x, agg], axis=1)
        h2 = jnp.maximum(h2 @ w2a + b2a, 0.0)
        return h2 @ w2b + b2b
    edge_index = jnp.stack([src, dst])
    h = jnp.maximum(_layernorm(x, axis=-1), 0.0)
    x = x + _L0_gnn_ref(h, edge_index, edge_attr_3, L0_gnn_mu, L0_gnn_sigma, L0_gnn_W, L0_gnn_b)
    h = jnp.maximum(_layernorm(x, axis=-1), 0.0)
    x = x + _L1_gnn_ref(h, edge_index, edge_attr_3, L1_gnn_W1, L1_gnn_R1, L1_gnn_b1, L1_gnn_g1, L1_gnn_be1, L1_gnn_W2, L1_gnn_R2, L1_gnn_b2, L1_gnn_g2, L1_gnn_be2, L1_gnn_W3, L1_gnn_R3, L1_gnn_b3, L1_gnn_g3, L1_gnn_be3)
    h = jnp.maximum(_layernorm(x, axis=-1), 0.0)
    x = x + _L2_gnn_ref(h, edge_index)
    h = jnp.maximum(_layernorm(x, axis=-1), 0.0)
    x = x + _L3_gnn_ref(h, edge_index, edge_attr_16, L3_gnn_w1a, L3_gnn_b1a, L3_gnn_w1b, L3_gnn_b1b, L3_gnn_w2a, L3_gnn_b2a, L3_gnn_w2b, L3_gnn_b2b)
    return x

_drawn_inputs = setup_inputs


def setup_inputs(seed=0):
    import zlib

    import numpy as np

    out = dict(_drawn_inputs(seed))
    spreads = {'L1_gnn_b1': (0.0, 0.583),
     'L1_gnn_g1': (1.0, 0.6),
     'L1_gnn_be1': (0.0, 1.893),
     'L1_gnn_b2': (0.0, 0.918),
     'L1_gnn_g2': (1.0, 0.582),
     'L1_gnn_be2': (0.0, 2.0),
     'L1_gnn_b3': (0.0, 2.0),
     'L1_gnn_g3': (1.0, 0.2),
     'L1_gnn_be3': (0.0, 0.33)}
    factors = {'edge_attr_16': 8.0,
     'L0_gnn_mu': 10.277,
     'L3_gnn_w1a': 7.787,
     'L3_gnn_b1a': 8.0,
     'L3_gnn_w1b': 7.178,
     'L3_gnn_b1b': 50.984,
     'L3_gnn_b2a': 17.377,
     'L0_gnn_sigma': 2.939,
     'L1_gnn_W1': 5.497,
     'L1_gnn_W2': 5.519,
     'L1_gnn_W3': 3.55,
     'L3_gnn_b2b': 4.397}
    for name, (base, spread) in spreads.items():
        noise = np.random.default_rng([zlib.crc32(name.encode()), seed]).standard_normal(out[name].shape)
        drawn = base * np.exp(spread * noise) if base else spread * noise
        out[name] = jnp.asarray(drawn.astype(out[name].dtype))
    for name, factor in factors.items():
        out[name] = (out[name] * factor).astype(out[name].dtype)
    return out
```

```python
from contextlib import ExitStack

import concourse.bass as bass
from concourse import mybir

F32, BF16, I32 = mybir.dt.float32, mybir.dt.bfloat16, mybir.dt.int32
ACT, ALU, AX = mybir.ActivationFunctionType, mybir.AluOpType, mybir.AxisListType

N, F, E = 100000, 32, 25000
P, Q = 128, 4
BLOCKS = 50
EC = BLOCKS * P
EP = Q * EC
ROWS = EP // P
HR = ROWS // 2
FULL = E // P
REST = E - FULL * P
NB = N // Q // BLOCKS
NP = NB // 4
TW = F + 2
PADROW = N + Q * P
TN = N + Q * P + 32
SLOTS = TN * TW // 2
KS, K3 = 4, 64
DE, DH, DI = 16, 96, 48
LN_EPS = BN_EPS = 1e-5
SLOPE = 0.01
CH = 10
XP = 125
NT = N // XP // CH

BDS = ["W0", "R1", "R2", "R3"] + [f"w1x{j}" for j in range(3)] + [f"w1e{j}" for j in range(3)] \
    + [f"wcA{j}" for j in range(3)] + [f"wcB{j}" for j in range(3)] + ["w2aA", "w2aB", "w2bA", "w2bB"]
VECS = ["b0", "b1", "b2", "b3", "g1", "g2", "g3", "be1", "be2", "be3", "mu0", "mu1", "mu2", "sg0", "sg1", "sg2",
        "b2aA", "b2aB", "b2b", "bcA", "bcB", "eps", "a0", "c0", "a1", "c1", "a2", "c2", "a3", "c3"]
CONSTS = ["ident", "centre", "mean", "groups", "shift"]


def after(e, sem, n):
    if not isinstance(n, int) or n > 0:
        e.wait_ge(sem, n)


def each_block(e, step):
    for j in (1, 2):
        step(2 * j - 2, 0, j)
        step(2 * j - 1, 1, j)
    with e.Fori(3, BLOCKS // 2 + 1) as j:
        step(2 * j - 2, 0, j)
        step(2 * j - 1, 1, j)


def each_block_ahead(e, head, body):
    head(0, 0, 1)
    for j in (1, 2):
        head(2 * j - 1, 1, j)
        body(2 * j - 2, 0, j)
        head(2 * j, 0, j + 1)
        body(2 * j - 1, 1, j)
    with e.Fori(3, BLOCKS // 2) as j:
        head(2 * j - 1, 1, j)
        body(2 * j - 2, 0, j)
        head(2 * j, 0, j + 1)
        body(2 * j - 1, 1, j)
    head(BLOCKS - 1, 1, BLOCKS // 2)
    body(BLOCKS - 2, 0, BLOCKS // 2)
    body(BLOCKS - 1, 1, BLOCKS // 2)


def bc(ap, n):
    return ap.unsqueeze(len(ap.shape)).broadcast_to(list(ap.shape) + [n])


def bc_mid(ap, n):
    p, a, b = ap.shape
    return ap.unsqueeze(2).broadcast_to([p, a, n, b])


def bc_first(ap, n):
    p, a = ap.shape
    return ap.unsqueeze(1).broadcast_to([p, n, a])


def sems(c, nc, phase, names):
    names = names.split()
    kept = {n: nc.alloc_semaphore(f"{phase}_{n}") for n in names if n[:3] == "got" or n[:4] == "sent"}
    s = {n: c.enter_context(nc.semaphore(f"{phase}_{n}")) for n in names if n not in kept}

    def zero():
        with nc.Block() as block:
            @block.gpsimd
            def _(e):
                for sem in s.values():
                    e.sem_clear(sem)
    c.callback(zero)
    return s | kept


def at(t, i, n=P):
    return t[:, bass.ds(i * n, n)]


def tiles(t, i):
    return t[:, :].rearrange("p (q b) -> p q b", q=Q)[:, :, bass.ds(i, 1)].rearrange("p q b -> p (q b)")


def copy(e, out, in_):
    return e.tensor_scalar(out, in_, 0.0, None, ALU.add)



LN = "x cen sq var sd rs h"


def ln_sems(n):
    return " ".join(a + n for a in LN.split())


def ln_tensor(pe, s, n, t, i, g):
    after(pe, s["x" + n], i + 1)
    after(pe, s["h" + n], i)
    pe.matmul(t["cen"], g["centre"], t["x"], start=True, stop=True).then_inc(s["cen" + n], 1)
    after(pe, s["sq" + n], i + 1)
    pe.matmul(t["var"], g["mean"], t["sq"], start=True, stop=True).then_inc(s["var" + n], 1)


def ln_scalar(act, s, n, t, i, g):
    after(act, s["cen" + n], i + 1)
    act.activation(t["sq"], t["cen"], ACT.Square).then_inc(s["sq" + n], 1)
    after(act, s["var" + n], i + 1)
    act.activation(t["sd"], t["var"], ACT.Sqrt, bias=g["V"]["eps"]).then_inc(s["sd" + n], 1)


def ln_vector(dve, s, n, t, i):
    after(dve, s["sd" + n], i + 1)
    dve.reciprocal(t["rs"], t["sd"]).then_inc(s["rs" + n], 1)
    after(dve, s["rs" + n], i + 1)
    dve.scalar_tensor_tensor(t["h"], t["cen"], 0.0, t["rs"], ALU.max, ALU.mult).then_inc(s["h" + n], 1)


def stage_indices(e, s, st, k, j, table, i):
    e.tensor_copy(st[:, k, :], tiles(table, i)).then_inc(s[f"stg{k}"], 1)
    e.wait_ge(s[f"stg{k}"], 1)
    after(e, s[f"stg{k}"], j)


def gather(e, s, st, k, j, i, table, src, dst, used):
    after(e, used, i - 1)
    stage_indices(e, s, st, k, j, table, i)
    for q in range(Q):
        e.indirect_dma_start(dst[:, k, q, :], None, src, bass.IndirectOffsetOnAxis(ap=st[:, k, q:q + 1], axis=0)).then_inc(s[f"got{k}"], 16)


GATHER = "stg0 stg1 got0 got1"


def scan_phase(nc, g, tag, arrays):
    same, first, carry = g["same"], g["first"], g["carry"]
    n = len(arrays)
    with ExitStack() as c:
        s = sems(c, nc, tag, "scan x c copied")
        x = g["sb"](c, tag + "_x", [P, n])
        pc = g["psum"](c, tag + "_pc", [P, n])
        block = c.enter_context(nc.Block())

        @block.vector
        def _(e):
            e.memset(carry[:, :], 0.0).then_inc(s["copied"], 1)
            for m, t in enumerate(arrays):
                e.tensor_tensor_scan(t[:, :], same[:, :], t[:, :], 0.0, ALU.mult, ALU.add).then_inc(s["scan"], 1)
            e.wait_ge(s["scan"], n)
            e.wait_ge(s["copied"], 1)
            for r in range(Q - 1):
                for m, t in enumerate(arrays):
                    e.scalar_tensor_tensor(x[:, m:m + 1], first[:, EC - 1:EC], carry[:, m:m + 1], t[:, EC - 1:EC],
                                           ALU.mult, ALU.add).then_inc(s["x"], 1)
                e.wait_ge(s["c"], r + 1)
                e.tensor_copy(carry[:, 0:n], pc[:, :]).then_inc(s["copied"], 1)
                e.wait_ge(s["copied"], r + 2)

        @block.tensor
        def _(e):
            for r in range(Q - 1):
                e.wait_ge(s["x"], n * (r + 1))
                e.matmul(pc[:, :], g["shift"], x[:, :], start=True, stop=True).then_inc(s["c"], 1)


def setup(nc, g):
    a, V, BD, sb, psum = g["a"], g["V"], g["BD"], g["sb"], g["psum"]
    same, last, first, MSG, ident = g["same"], g["last"], g["first"], g["MSG"], g["ident"]
    srcflat, sameflat, lastflat = g["srcflat"], g["sameflat"], g["lastflat"]
    HS, HDW = g["HS"], g["HDW"][:, :, :, :].rearrange("p b w c -> p (b w c)")
    with ExitStack() as c:
        s = sems(c, nc, "in", "const clear zero idx idxw wts vec tails attr wide table pads xin0 xin1 xcp xout0 xout1 rowsf "
                              "shf flags lastf lastb tr trc slot p3t p3 base bk flat bcast wT wTc wc wcc wcd sg first done")
        zero = sb(c, "zero", [P, P])
        w1b, w1bT, w2bot = sb(c, "w1b", [DH, DH]), sb(c, "w1bT", [DH, DH]), sb(c, "w2bot", [DH, DI])
        wc, bcv, b1bc = sb(c, "wc", [DH, DI]), sb(c, "bcv", [DI, 1]), sb(c, "b1bc", [DH, 1])
        ri = sb(c, "ri", [HR, 2, 2, P], I32)
        hb = sb(c, "hb", [HR, 2, 2], I32)
        rf = sb(c, "rf", [HR, 5, 2, P])
        fb = sb(c, "fb", [HR, 2, 2, P], BF16)
        real = sb(c, "real", [HR, 2, P])
        p3r = sb(c, "p3r", [HR, 2, 3 * P])
        et = sb(c, "et", [P, ROWS])
        p3 = HS[:, 0:3 * ROWS].rearrange("p (d r) -> p d r", d=3)
        bt = HS[:, 3 * ROWS:9 * ROWS].rearrange("p (w d r) -> p w d r", w=2, d=3)
        xr = HDW[0:XP, 0:2 * NT * F].rearrange("p (k n f) -> p k n f", k=2, f=F)
        xw = HDW[0:XP, 2 * NT * F:2 * NT * (F + TW)].rearrange("p (k n f) -> p k n f", k=2, f=TW)
        pt = psum(c, "pt", [P, 2, P])
        pd = psum(c, "pd", [P, 3, P])
        pd2 = psum(c, "pd2", [P, 3, P])
        pw = psum(c, "pw", [P, 2, P])
        block = c.enter_context(nc.Block())
        halves = [(0, 0, HR), (1, HR, FULL - HR)]

        def column(v):
            return v.rearrange("(p o) -> p o", o=1)

        placed = []
        for q in range(Q):
            p = slice(32 * q, 32 * q + 32)
            h = slice(32 * q, 32 * q + 16)
            placed += [(BD["W0"][p, p], a["W0T"])] + [(BD[f"R{l}"][p, p], a[f"R{l}"]) for l in (1, 2, 3)]
            for j in range(3):
                o = slice(32 * j, 32 * j + 32)
                placed += [(BD[f"w1x{j}"][p, p], a["w1a"][0:F, o]), (BD[f"w1e{j}"][h, p], a["w1a"][F:F + DE, o]),
                           (BD[f"w1e{j}"][32 * q + DE:32 * q + DE + 1, p], a["b1a"][o].rearrange("(o n) -> o n", o=1))]
            placed += [(BD["w2aA"][p, p], a["w2a"][0:F, 0:32]), (BD["w2aB"][p, h], a["w2a"][0:F, 32:DI]),
                       (BD["w2bA"][p, p], a["w2b"][0:32, :]), (BD["w2bB"][h, p], a["w2b"][32:DI, :])]
            placed += [(V[n][p], column(a[n])) for n in ["b0", "b1", "b2", "b3", "g1", "g2", "g3", "be1", "be2", "be3", "b2b"]]
            placed += [(V["b2aA"][p], column(a["b2a"][0:32])), (V["b2aB"][h], column(a["b2a"][32:DI]))]
            placed += [(V[f"{n}{d}"][p], a[n][:, d:d + 1]) for n in ("mu", "sg") for d in range(3)]
        placed += [(b1bc[:, :], column(a["b1b"])), (w1b[:, :], a["w1b"]), (w2bot[:, :], a["w2a"][F:F + DH, :])]
        folded = []
        for q in range(Q):
            p = slice(32 * q, 32 * q + 32)
            h = slice(32 * q, 32 * q + 16)
            for j in range(3):
                o = slice(32 * j, 32 * j + 32)
                folded += [(BD[f"wcA{j}"][p, p], wc[o, 0:32]), (BD[f"wcB{j}"][p, h], wc[o, 32:DI])]
            folded += [(V["bcA"][p], bcv[0:32, :]), (V["bcB"][h], bcv[32:DI, :])]

        @block.sync
        def _(e):
            e.dma_start(g["consts"][:, :, :], a["consts"]).then_inc(s["const"], 16)
            e.dma_start(g["trashE"][:, :], a["trash"]).then_inc(s["const"], 16)
            e.wait_ge(s["clear"], 2)
            for w, n in enumerate(("src", "dst")):
                for h, r0, m in halves:
                    e.dma_start(ri[0:m, w, h, :], a[n][r0 * P:(r0 + m) * P].rearrange("(r c) -> r c", c=P)).then_inc(s["idx"], 16)
                e.dma_start(ri[FULL - HR:FULL - HR + 1, w, 1, 0:REST], a[n][FULL * P:E].rearrange("(o n) -> o n", o=1)).then_inc(s["idx"], 16)
            with nc.allow_non_contiguous_dma(reason="one word per tile or feature"):
                before, behind = column(a["dst"][P - 1:FULL * P:P]), column(a["dst"][P:E:P])
                e.dma_start(hb[1:HR, 0, 0:1], before[0:HR - 1]).then_inc(s["idx"], 16)
                e.dma_start(hb[0:FULL - HR + 1, 0, 1:2], before[HR - 1:FULL]).then_inc(s["idx"], 16)
                e.dma_start(hb[0:HR, 1, 0:1], behind[0:HR]).then_inc(s["idx"], 16)
                e.dma_start(hb[0:FULL - HR, 1, 1:2], behind[HR:FULL]).then_inc(s["idx"], 16)
                e.wait_ge(s["wts"], 3)
                for dst, src in placed:
                    e.dma_start(dst, src).then_inc(s["vec"], 16)
                e.wait_ge(s["flags"], 1)
                e.wait_ge(s["lastb"], 1)
                for h in range(2):
                    span = slice(h * HR * P, (h + 1) * HR * P)
                    for flat, t in ((sameflat, fb[:, 0, h, :]), (lastflat, fb[:, 1, h, :]), (srcflat, rf[:, 0, h, :])):
                        e.dma_start(flat[span].rearrange("(r c) -> r c", c=P), t).then_inc(s["flat"], 16)
                e.wait_ge(s["flat"], 96)
                for flat, t in ((sameflat, same), (lastflat, last)):
                    for q in range(Q):
                        e.dma_start(t[32 * q:32 * q + 32, :], flat[q * EC:(q + 1) * EC].partition_broadcast(32)).then_inc(s["bcast"], 16)
                e.wait_ge(s["wcc"], 2)
                for dst, src in folded:
                    e.dma_start(dst, src).then_inc(s["wcd"], 16)
            e.wait_ge(s["bcast"], 16 * 8)
            e.wait_ge(s["wcd"], 16 * len(folded))

        @block.scalar
        def _(e):
            x = a["x"].rearrange("(p n) f -> p n f", p=XP)
            t = g["table"][0:N, :].rearrange("(p n) f -> p n f", p=XP)
            e.wait_ge(s["zero"], 1)
            e.dma_start(g["table"][N:TN, :].rearrange("(p n) f -> p n f", p=32),
                        zero[0:32, 0:TW].unsqueeze(1).broadcast_to([32, (TN - N) // 32, TW])).then_inc(s["pads"], 16)
            e.dma_start(g["runs"][EP:EP + P, :], zero[:, 0:F]).then_inc(s["pads"], 16)
            e.dma_start(g["attr3"][E:EP, :].rearrange("(p n) f -> p (n f)", p=120), zero[0:120, 0:15]).then_inc(s["pads"], 16)
            e.dma_start(g["attr16"][E:EP, :].rearrange("(p n) f -> p (n f)", p=120), zero[0:120, 0:80]).then_inc(s["pads"], 16)
            for n in ("attr3", "attr16"):
                e.dma_start(g[n][0:E, :].rearrange("(p n) f -> p (n f)", p=100), a[n].rearrange("(p n) f -> p (n f)", p=100)).then_inc(s["attr"], 16)
            for m in range(CH + 1):
                k = m % 2
                if m < CH:
                    after(e, s["xcp"], m - 1)
                    e.dma_start(xr[:, k], x[:, m * NT:(m + 1) * NT, :]).then_inc(s[f"xin{k}"], 16)
                if m:
                    e.wait_ge(s["xcp"], m)
                    e.dma_start(t[:, (m - 1) * NT:m * NT, :], xw[:, 1 - k]).then_inc(s[f"xout{1 - k}"], 16)
            e.wait_ge(s["attr"], 32)
            e.wait_ge(s["pads"], 64)
            for h in range(2):
                e.dma_start(p3r[:, h, :], g["attr3"][h * HR * P:(h + 1) * HR * P, :].rearrange("(r c) d -> r (c d)", c=P)).then_inc(s["tails"], 16)
            for k in range(2):
                e.wait_ge(s[f"xout{k}"], 16 * (CH // 2))
            e.wait_ge(s["vec"], 16 * len(placed))
            sg = g["vecs"][:, VECS.index("sg0"):VECS.index("sg0") + 3]
            e.wait_ge(s["sg"], 3)
            e.activation(sg, sg, ACT.Sqrt).then_inc(s["sg"], 1)

        @block.gpsimd
        def _(e):
            e.memset(zero[:, :], 0.0).then_inc(s["zero"], 1)
            e.memset(xw[:, :, :, F:F + 1], float(EP)).then_inc(s["wide"], 1)
            e.memset(xw[:, :, :, F + 1:TW], 0.0).then_inc(s["wide"], 1)
            e.wait_ge(s["wide"], 2)
            for m in range(CH):
                k = m % 2
                e.wait_ge(s[f"xin{k}"], 16 * (m // 2 + 1))
                after(e, s[f"xout{k}"], 16 * (m // 2))
                e.tensor_copy(xw[:, k, :, 0:F], xr[:, k]).then_inc(s["xcp"], 1)

        @block.tensor
        def _(e):
            e.wait_ge(s["const"], 32)
            e.wait_ge(s["lastf"], 3)
            for n, w in enumerate((0, 1, 4)):
                after(e, s["trc"], n)
                for h in range(2):
                    mm = e.transpose(pt[:, h, 0:HR], rf[:, w, h, :], ident[0:HR, 0:HR])
                mm.then_inc(s["tr"], 1)
            e.wait_ge(s["tails"], 32)
            for h, p in ((0, pd), (1, pd2)):
                for d in range(3):
                    mm = e.transpose(p[:, d, 0:HR], p3r[:, h, :].rearrange("r (c d) -> r c d", d=3)[:, :, d], ident[0:HR, 0:HR])
            mm.then_inc(s["p3t"], 1)
            e.wait_ge(s["vec"], 16 * len(placed))
            e.transpose(pw[0:DH, 0, 0:DH], w1b[:, :], ident[0:DH, 0:DH]).then_inc(s["wT"], 1)
            e.wait_ge(s["wTc"], 1)
            e.matmul(pw[0:DH, 1, 0:DI], w1bT[:, :], w2bot[:, :], start=True, stop=True).then_inc(s["wc"], 1)
            e.wait_ge(s["wcc"], 1)
            e.matmul(pw[0:DI, 0, 0:1], w2bot[:, :], b1bc[:, :], start=True, stop=True).then_inc(s["wc"], 1)

        @block.vector
        def _(e):
            e.memset(ri[:, 0], PADROW)
            e.memset(ri[:, 1], N)
            e.memset(hb[:, :, :], N).then_inc(s["clear"], 1)
            e.wait_ge(s["clear"], 1)
            e.memset(hb[0:1, 0, 0:1], -1).then_inc(s["clear"], 1)
            e.memset(g["bds"][:, :, :], 0.0).then_inc(s["wts"], 1)
            e.memset(g["vecs"][:, :], 0.0).then_inc(s["wts"], 1)
            e.wait_ge(s["wts"], 2)
            e.memset(V["eps"], LN_EPS)
            e.memset(V["a0"], 1.0).then_inc(s["wts"], 1)
            e.memset(MSG[:, :], 1.0)
            e.wait_ge(s["idx"], 16 * 10)
            e.tensor_copy(rf[:, 0:2], ri[:, :]).then_inc(s["rowsf"], 1)
            e.wait_ge(s["rowsf"], 1)
            e.tensor_copy(rf[:, 2, :, 1:P], rf[:, 1, :, 0:P - 1])
            e.tensor_copy(rf[:, 3, :, 0:P - 1], rf[:, 1, :, 1:P])
            e.tensor_copy(rf[:, 2, :, 0:1], hb[:, 0].unsqueeze(2))
            e.tensor_copy(rf[:, 3, :, P - 1:P], hb[:, 1].unsqueeze(2)).then_inc(s["shf"], 1)
            e.wait_ge(s["shf"], 1)
            e.tensor_tensor(fb[:, 0], rf[:, 1], rf[:, 2], ALU.is_equal).then_inc(s["flags"], 1)
            e.tensor_scalar(real[:, :, :], rf[:, 1], float(N), None, ALU.is_lt).then_inc(s["lastf"], 1)
            e.tensor_tensor(rf[:, 4], rf[:, 1], rf[:, 3], ALU.not_equal).then_inc(s["lastf"], 1)
            e.wait_ge(s["lastf"], 2)
            e.tensor_tensor(rf[:, 4], rf[:, 4], real[:, :, :], ALU.mult).then_inc(s["lastf"], 1)
            e.wait_ge(s["lastf"], 3)
            e.tensor_copy(fb[:, 1], rf[:, 4]).then_inc(s["lastb"], 1)
            for n, t in enumerate((g["srcE"], g["dstE"], g["lastE"])):
                e.wait_ge(s["tr"], n + 1)
                e.tensor_copy(t[:, :].rearrange("p (h r) -> p h r", h=2), pt[:, :, 0:HR]).then_inc(s["trc"], 1)
            e.wait_ge(s["trc"], 3)
            e.tensor_copy(g["srcI"][:, :], g["srcE"][:, :])
            e.tensor_copy(g["dstI"][:, :], g["dstE"][:, :])
            e.tensor_scalar(g["inI"][:, :], g["dstE"][:, :], float(N - 1), None, ALU.min)
            for n, (t, scale, add, far) in enumerate(((g["slotI"], TW // 2, F // 2, SLOTS + 8), (g["outI"], 1, 0, N + 8))):
                e.tensor_scalar(et[:, :], g["dstE"][:, :], float(scale), float(add - far), ALU.mult, ALU.add).then_inc(s["slot"], 1)
                e.wait_ge(s["slot"], 3 * n + 1)
                e.tensor_tensor(et[:, :], et[:, :], g["lastE"][:, :], ALU.mult).then_inc(s["slot"], 1)
                e.wait_ge(s["slot"], 3 * n + 2)
                e.tensor_scalar(t[:, :], et[:, :], float(far), None, ALU.add).then_inc(s["slot"], 1)
                e.wait_ge(s["slot"], 3 * n + 3)
            e.wait_ge(s["p3t"], 1)
            for h, p in ((0, pd), (1, pd2)):
                e.tensor_scalar(p3[:, :, h * HR:(h + 1) * HR], p[:, :, 0:HR], float(KS - 1), 0.0, ALU.mult, ALU.max).then_inc(s["p3"], 1)
            e.wait_ge(s["p3"], 2)
            for k in range(KS):
                after(e, s["bk"], k)
                e.tensor_scalar(bt[:, 0], p3, float(KS - 1), float(-k), ALU.min, ALU.add).then_inc(s["base"], 1)
                e.wait_ge(s["base"], 3 * k + 1)
                e.scalar_tensor_tensor(bt[:, 1], bt[:, 0], -1.0, bt[:, 0], ALU.mult, ALU.max).then_inc(s["base"], 1)
                e.wait_ge(s["base"], 3 * k + 2)
                e.tensor_scalar(bt[:, 0], bt[:, 1], -1.0, 1.0, ALU.mult, ALU.add).then_inc(s["base"], 1)
                e.wait_ge(s["base"], 3 * k + 3)
                e.tensor_scalar(g["basis"][:, :, :, k], bt[:, 0], 0.0, None, ALU.max).then_inc(s["bk"], 1)
            e.wait_ge(s["wT"], 1)
            e.tensor_copy(w1bT[:, :], pw[0:DH, 0, 0:DH]).then_inc(s["wTc"], 1)
            e.wait_ge(s["wc"], 1)
            e.tensor_copy(wc[:, :], pw[0:DH, 1, 0:DI]).then_inc(s["wcc"], 1)
            e.wait_ge(s["wc"], 2)
            e.tensor_copy(bcv[:, :], pw[0:DI, 0, 0:1]).then_inc(s["wcc"], 1)
            sg, mu = (g["vecs"][:, VECS.index(n):VECS.index(n) + 3] for n in ("sg0", "mu0"))
            e.wait_ge(s["vec"], 16 * len(placed))
            e.tensor_tensor(sg, sg, sg, ALU.mult).then_inc(s["sg"], 1)
            e.wait_ge(s["sg"], 1)
            e.tensor_scalar(sg, sg, 1e-14, 2.0, ALU.add, ALU.mult).then_inc(s["sg"], 1)
            e.wait_ge(s["sg"], 2)
            e.reciprocal(sg, sg).then_inc(s["sg"], 1)
            e.wait_ge(s["sg"], 4)
            e.scalar_tensor_tensor(mu, mu, -1.0, sg, ALU.mult, ALU.mult)
            e.wait_ge(s["bcast"], 16 * 8)
            e.tensor_tensor_scan(first[:, :], same[:, :], same[:, :], 1.0, ALU.mult, ALU.min)


def degrees(nc, g):
    a, sb, psum, MSG, ident = g["a"], g["sb"], g["psum"], g["MSG"], g["ident"]
    scan_phase(nc, g, "cnt", [MSG])
    with ExitStack() as c:
        s = sems(c, nc, "deg", "fix eidx flat rows tr cnt pairs sd rd stg0 stg1 sent0 sent1")
        cr = sb(c, "cr", [HR, 2, P])
        pt = psum(c, "pt", [P, 2, P])
        sd, eidx = sb(c, "sdc", [P, ROWS]), sb(c, "eidx", [P, ROWS])
        pairs = sb(c, "pairs", [P, BLOCKS, Q, 2])
        st, pv = sb(c, "st", [P, 2, Q], I32), sb(c, "pv", [P, 2, Q, 2])
        block = c.enter_context(nc.Block())

        @block.sync
        def _(e):
            e.dma_start(eidx[:, :], a["eidx"]).then_inc(s["eidx"], 16)
            e.wait_ge(s["fix"], 1)
            for q in range(Q):
                e.dma_start(g["cntflat"][q * EC:(q + 1) * EC].rearrange("(o n) -> o n", o=1), MSG[32 * q:32 * q + 1, :]).then_inc(s["flat"], 16)
            e.wait_ge(s["flat"], 16 * Q)
            for h in range(2):
                e.dma_start(cr[:, h, :], g["cntflat"][h * HR * P:(h + 1) * HR * P].rearrange("(r c) -> r c", c=P)).then_inc(s["rows"], 16)

        @block.scalar
        def _(e):
            e.wait_ge(s["cnt"], 1)
            e.activation(sd[:, :], g["cntE"][:, :], ACT.Sqrt).then_inc(s["sd"], 1)

        @block.tensor
        def _(e):
            e.wait_ge(s["rows"], 32)
            for h in range(2):
                mm = e.transpose(pt[:, h, 0:HR], cr[:, h, :], ident[0:HR, 0:HR])
            mm.then_inc(s["tr"], 1)

        @block.vector
        def _(e):
            e.scalar_tensor_tensor(MSG[:, :], g["first"][:, :], g["carry"][:, 0:1], MSG[:, :], ALU.mult, ALU.add).then_inc(s["fix"], 1)
            e.wait_ge(s["tr"], 1)
            e.tensor_scalar(g["cntE"][:, :].rearrange("p (h r) -> p h r", h=2), pt[:, :, 0:HR], 1.0, None, ALU.max).then_inc(s["cnt"], 1)
            e.wait_ge(s["cnt"], 1)
            e.reciprocal(g["rcE"][:, :], g["cntE"][:, :])
            e.wait_ge(s["eidx"], 16)
            byblock = pairs[:, :, :, :].rearrange("p b q w -> p w q b")
            e.tensor_copy(byblock[:, 0], eidx[:, :].rearrange("p (q b) -> p q b", q=Q)).then_inc(s["pairs"], 1)
            e.tensor_copy(byblock[:, 1], g["cntE"][:, :].rearrange("p (q b) -> p q b", q=Q)).then_inc(s["pairs"], 1)
            e.wait_ge(s["sd"], 1)
            e.reciprocal(g["dinvD"][:, :], sd[:, :])

        @block.gpsimd
        def _(e):
            slots = g["table"].rearrange("n (h w) -> (n h) w", w=2)
            e.wait_ge(s["pairs"], 2)

            def step(i, k, j):
                after(e, s[f"sent{k}"], 64 * (j - 1))
                e.tensor_copy(pv[:, k], pairs[:, bass.ds(i, 1)].rearrange("p b q w -> p (b q) w")).then_inc(s[f"stg{k}"], 1)
                e.tensor_copy(st[:, k, :], tiles(g["slotI"], i)).then_inc(s[f"stg{k}"], 1)
                e.wait_ge(s[f"stg{k}"], 1)
                after(e, s[f"stg{k}"], 2 * j)
                for q in range(Q):
                    e.indirect_dma_start(slots, bass.IndirectOffsetOnAxis(ap=st[:, k, q:q + 1], axis=0), pv[:, k, q, :], None,
                                         bounds_check=SLOTS - 1, oob_is_err=False).then_inc(s[f"sent{k}"], 16)
            each_block(e, step)
            for k in range(2):
                e.wait_ge(s[f"sent{k}"], 64 * (BLOCKS // 2))


def layer0(nc, g):
    a, V, BD, sb, psum, ident = g["a"], g["V"], g["BD"], g["sb"], g["psum"], g["ident"]
    with ExitStack() as c:
        s = sems(c, nc, "l0", "const " + GATHER + " stf0 stf1 sts0 sts1 sent row0 row1 att0 att1 " + ln_sems("e")
                 + " xt gau g2 g3 ex m mw mwc sc eq cb ld ld2 ld3 addi sum av pad zi")
        xd = psum(c, "xd", [P, P])
        cen, var, pw = psum(c, "cen", [P, P]), psum(c, "var", [P, P]), psum(c, "pw", [P, P])
        pe_ = psum(c, "pe", [P, Q, F])
        cols, pos = sb(c, "cols", [P, Q * P]), sb(c, "pos", [P, Q])
        gx, st, ss = sb(c, "gx", [P, 2, Q, F]), sb(c, "st", [P, 2, Q], I32), sb(c, "ss", [P, 2, Q], I32)
        x, sq, sd, h, m = (sb(c, n, [P, P]) for n in ("x", "sq", "sd", "h", "m"))
        att, gq, gs = sb(c, "att", [P, 2, P, 3]), sb(c, "gq", [P, 3, P]), sb(c, "gs", [P, P])
        row, S = sb(c, "row", [P, 2, Q * P]), sb(c, "S", [P, Q, Q * P])
        junk, sc, cb, ld = sb(c, "junk", [P, Q * P]), sb(c, "sc", [P, Q]), sb(c, "cb", [P, Q]), sb(c, "ld", [P, Q])
        mw, av, ai = sb(c, "mw", [P, Q, F]), sb(c, "av", [P, 2, Q, TW]), sb(c, "ai", [P, 2, Q], I32)
        zi = sb(c, "zi", [P, Q], I32)
        t = {"x": x[:, :], "cen": cen[:, :], "sq": sq[:, :], "var": var[:, :], "sd": sd[:, :], "rs": sd[:, :], "h": h[:, :]}
        block = c.enter_context(nc.Block())

        @block.sync
        def _(e):
            e.dma_start(cols[:, :], a["cols"]).then_inc(s["const"], 16)
            e.dma_start(pos[:, :], a["pos"]).then_inc(s["const"], 16)

            def load(i, k, j):
                after(e, s["addi"], i - 1)
                after(e, s["gau"], i - 1)
                for q in range(Q):
                    e.dma_start(row[:, k, q * P:(q + 1) * P], g["srcflat"][bass.ds(i * P + q * EC, P)].partition_broadcast(P)).then_inc(s[f"row{k}"], 16)
                for q in range(Q):
                    e.dma_start(att[32 * q:32 * q + 32, k, :, :].rearrange("p c d -> p (c d)"),
                                g["attr3"][bass.ds(i * P + q * EC, P), :].rearrange("c d -> (c d)").partition_broadcast(32)).then_inc(s[f"att{k}"], 16)
            each_block(e, load)

        @block.gpsimd
        def _(e):
            def fetch(i, k, sem, n):
                after(e, s["xt"], i - 1)
                e.tensor_copy(st[:, k, :], tiles(g["inI"], i)).then_inc(sem, 1)
                e.wait_ge(sem, 1)
                after(e, sem, n)
                for q in range(Q):
                    e.indirect_dma_start(gx[:, k, q, :], None, a["x"], bass.IndirectOffsetOnAxis(ap=st[:, k, q:q + 1], axis=0)).then_inc(s[f"got{k}"], 16)

            def add(i, k, j):
                after(e, s["sent"], 64 * i)
                after(e, s["av"], i + 1)
                after(e, s["addi"], i + 1)
                e.tensor_tensor(ss[:, k, :], ai[:, k, :], zi[:, :], ALU.add).then_inc(s[f"sts{k}"], 1)
                e.wait_ge(s[f"sts{k}"], 1)
                after(e, s[f"sts{k}"], j)
                for q in range(Q):
                    e.indirect_dma_start(g["table"], bass.IndirectOffsetOnAxis(ap=ss[:, k, q:q + 1], axis=0), av[:, k, q, :], None,
                                         compute_op=ALU.add).then_inc(s["sent"], 16)

            e.memset(zi[:, :], 0).then_inc(s["zi"], 1)
            e.wait_ge(s["zi"], 1)
            for k in range(2):
                fetch(k, k, s[f"stf{k}"], 1)
            for k in range(2):
                add(k, k, 1)
                fetch(k + 2, k, s[f"stg{k}"], 1)
            with e.Fori(2, BLOCKS // 2) as j:
                for k in range(2):
                    add(2 * j - 2 + k, k, j)
                    fetch(2 * j + k, k, s[f"stg{k}"], j)
            for k in range(2):
                add(BLOCKS - 2 + k, k, BLOCKS // 2)
            e.wait_ge(s["sent"], 64 * BLOCKS)

        @block.tensor
        def _(e):
            def head(i, k, j):
                after(e, s[f"got{k}"], 64 * j)
                after(e, s["xe"], i)
                e.transpose(xd[:, :], gx[:, k, :, :], ident).then_inc(s["xt"], 1)
                ln_tensor(e, s, "e", t, i, g)

            def body(i, k, j):
                after(e, s["m"], i + 1)
                e.matmul(pw[:, :], m[:, :], BD["W0"], start=True, stop=True).then_inc(s["mw"], 1)
                after(e, s["mwc"], i + 1)
                after(e, s["eq"], Q * (i + 1))
                after(e, s["av"], i)
                for r in range(Q):
                    for q in range(Q):
                        mm = e.matmul(pe_[:, r, :], S[:, q, r * P:(r + 1) * P], mw[:, q, :], start=(q == 0), stop=(q == Q - 1))
                mm.then_inc(s["sum"], 1)
            each_block_ahead(e, head, body)

        @block.scalar
        def _(e):
            def head(i, k, j):
                after(e, s["xt"], i + 1)
                after(e, s["cene"], i)
                e.copy(x[:, :], xd[:, :]).then_inc(s["xe"], 1)
                ln_scalar(e, s, "e", t, i, g)
                after(e, s[f"att{k}"], 64 * j)
                after(e, s["g3"], i)
                for d in range(3):
                    mm = e.activation(gq[:, d, :], att[:, k, :, d], ACT.Square, bias=V[f"mu{d}"], scale=V[f"sg{d}"])
                mm.then_inc(s["gau"], 1)
                after(e, s["g3"], i + 1)
                e.activation(gs[:, :], gq[:, 0, :], ACT.Exp, scale=-1.0).then_inc(s["ex"], 1)

            def body(i, k, j):
                after(e, s["mw"], i + 1)
                after(e, s["sum"], i)
                e.copy(mw[:, :, :], pw[:, :].rearrange("p (q f) -> p q f", q=Q)).then_inc(s["mwc"], 1)
                after(e, s["sum"], i + 1)
                after(e, s["sent"], 64 * (i - 1))
                e.wait_ge(s["pad"], 1)
                e.copy(av[:, k, :, 0:F], pe_[:, :, :]).then_inc(s["av"], 1)
            each_block_ahead(e, head, body)

        @block.vector
        def _(e):
            e.memset(av[:, :, :, :], 0.0).then_inc(s["pad"], 1)
            e.wait_ge(s["const"], 32)

            def head(i, k, j):
                after(e, s["gau"], i + 1)
                after(e, s["ex"], i)
                e.tensor_tensor(gq[:, 1, :], gq[:, 0, :], gq[:, 1, :], ALU.add).then_inc(s["g2"], 1)
                after(e, s["g2"], i + 1)
                e.tensor_tensor(gq[:, 0, :], gq[:, 1, :], gq[:, 2, :], ALU.add).then_inc(s["g3"], 1)
                ln_vector(e, s, "e", t, i)
                after(e, s["ex"], i + 1)
                after(e, s["he"], i + 1)
                after(e, s["mw"], i)
                e.tensor_tensor(m[:, :], h[:, :], gs[:, :], ALU.mult).then_inc(s["m"], 1)

            def body(i, k, j):
                after(e, s["ld3"], i)
                copy(e, sc[:, :], tiles(g["srcE"], i)).then_inc(s["sc"], 1)
                after(e, s[f"row{k}"], 64 * j)
                after(e, s["sc"], i + 1)
                after(e, s["sum"], i)
                for q in range(Q):
                    e.tensor_scalar(S[:, q, :], row[:, k, :], sc[:, q:q + 1], None, ALU.is_equal).then_inc(s["eq"], 1)
                for q in range(Q):
                    after(e, s["eq"], Q * i + q + 1)
                    e.scalar_tensor_tensor(junk[:, :], cols[:, :], pos[:, q:q + 1], S[:, q, :], ALU.is_lt, ALU.mult,
                                           accum_out=cb[:, q:q + 1]).then_inc(s["cb"], 1)
                    after(e, s["cb"], Q * i + q + 1)
                e.tensor_scalar(ld[:, :], cb[:, :], 0.5, None, ALU.is_lt).then_inc(s["ld"], 1)
                e.tensor_tensor(sc[:, :], sc[:, :], g["trashE"][:, :], ALU.subtract).then_inc(s["ld2"], 1)
                after(e, s["ld"], i + 1)
                after(e, s["ld2"], i + 1)
                e.tensor_tensor(ld[:, :], sc[:, :], ld[:, :], ALU.mult).then_inc(s["ld3"], 1)
                after(e, s["ld3"], i + 1)
                after(e, s["sent"], 64 * (i - 1))
                e.tensor_tensor(ai[:, k, :], ld[:, :], g["trashE"][:, :], ALU.add).then_inc(s["addi"], 1)
            each_block_ahead(e, head, body)


def place(nc, g):
    V, sb, psum, ident, HS, HDW = g["V"], g["sb"], g["psum"], g["ident"], g["HS"], g["HDW"]
    with ExitStack() as c:
        s = sems(c, nc, "pl", GATHER + " stgd0 stgd1 tb0 tb1 xs0 xs1 xo0 xo1 yo0 yo1 et zt tc gc ptr hc " + ln_sems("e") + " " + ln_sems("z"))
        pxe, pxz = psum(c, "pxe", [P, 2, P]), psum(c, "pxz", [P, NB])
        cene, vare = psum(c, "cene", [P, 2 * P]), psum(c, "vare", [P, 2 * P])
        cenz, varz = psum(c, "cenz", [P, NB]), psum(c, "varz", [P, NB])
        gx, st = sb(c, "gx", [P, 2, 2, Q, TW]), sb(c, "st", [P, 2, 2, Q], I32)
        gc = sb(c, "gc", [P, 2, Q, F])
        tb, tc = sb(c, "tb", [NP, 2, Q, 4, TW]), sb(c, "tc", [NP, 4, Q, F])
        xe, sqe, sde, he = sb(c, "xe", [P, 2, 2 * P]), sb(c, "sqe", [P, 2 * P]), sb(c, "sde", [P, 2 * P]), sb(c, "he", [P, 2 * P])
        xz, sqz, sdz, hz = sb(c, "xz", [P, 2, NB]), sb(c, "sqz", [P, NB]), sb(c, "sdz", [P, NB]), sb(c, "hz", [P, 2, NB])
        tab = g["table"][0:N, :].rearrange("(q b p n) w -> b p q (n w)", q=Q, b=BLOCKS, p=NP)

        def te(k):
            return {"x": xe[:, k], "cen": cene[:, :], "sq": sqe[:, :], "var": vare[:, :], "sd": sde[:, :], "rs": sde[:, :], "h": he[:, :]}

        def tz(k):
            return {"x": xz[:, k], "cen": cenz[:, :], "sq": sqz[:, :], "var": varz[:, :], "sd": sdz[:, :], "rs": sdz[:, :], "h": hz[:, k]}
        block = c.enter_context(nc.Block())

        @block.gpsimd
        def _(e):
            def step(i, k, j):
                after(e, s["ptr"], i - 1)
                e.tensor_copy(st[:, k, 0, :], tiles(g["srcI"], i)).then_inc(s[f"stg{k}"], 1)
                e.tensor_copy(st[:, k, 1, :], tiles(g["dstI"], i)).then_inc(s[f"stg{k}"], 1)
                e.wait_ge(s[f"stg{k}"], 1)
                after(e, s[f"stg{k}"], 2 * j)
                for w in range(2):
                    for q in range(Q):
                        e.indirect_dma_start(gx[:, k, w, q, :], None, g["table"],
                                             bass.IndirectOffsetOnAxis(ap=st[:, k, w, q:q + 1], axis=0)).then_inc(s[f"got{k}"], 16)
            each_block(e, step)

        @block.sync
        def _(e):
            def load(i, k, j):
                after(e, s["tc"], i - 1)
                e.dma_start(tb[:, k].rearrange("p q n w -> p q (n w)"), tab[bass.ds(i, 1)].rearrange("b p q w -> (b p) q w")).then_inc(s[f"tb{k}"], 16)

            def store(i, k, j):
                after(e, s["xe"], i + 1)
                e.dma_start(g["xsd"][bass.ds(i, 1)].rearrange("b p c -> (b p) c"), xe[:, k]).then_inc(s[f"xs{k}"], 16)
                after(e, s["xz"], i + 1)
                e.dma_start(g["x0f"][bass.ds(i, 1)].rearrange("b p c -> (b p) c"), xz[:, k]).then_inc(s[f"xo{k}"], 16)
                after(e, s["hz"], i + 1)
                e.dma_start(g["yf"][bass.ds(i, 1)].rearrange("b p c -> (b p) c"), hz[:, k]).then_inc(s[f"yo{k}"], 16)
            each_block_ahead(e, load, store)
            for k in range(2):
                for n in ("xs", "xo", "yo"):
                    e.wait_ge(s[f"{n}{k}"], 16 * (BLOCKS // 2))

        @block.tensor
        def _(e):
            def step(i, k, j):
                after(e, s["tc"], i + 1)
                after(e, s["xz"], i)
                for n in range(4):
                    mm = e.transpose(pxz[:, n * NP:(n + 1) * NP], tc[:, n, :, :], ident[0:NP, 0:NP])
                mm.then_inc(s["zt"], 1)
                ln_tensor(e, s, "z", tz(k), i, g)
                after(e, s["gc"], i + 1)
                after(e, s["xe"], i)
                for w in range(2):
                    mm = e.transpose(pxe[:, w, :], gc[:, w, :, :], ident)
                mm.then_inc(s["et"], 1)
                ln_tensor(e, s, "e", te(k), i, g)
            each_block(e, step)

        @block.scalar
        def _(e):
            def step(i, k, j):
                after(e, s[f"tb{k}"], 16 * j)
                after(e, s["zt"], i)
                e.copy(tc[:, :, :, :], tb[:, k, :, :, 0:F].rearrange("p q n f -> p n q f")).then_inc(s["tc"], 1)
                after(e, s["zt"], i + 1)
                after(e, s[f"xo{k}"], 16 * (j - 1))
                after(e, s["cenz"], i - 1)
                e.activation(xz[:, k], pxz[:, :], ACT.Identity, bias=V["b0"]).then_inc(s["xz"], 1)
                ln_scalar(e, s, "z", tz(k), i, g)
                after(e, s["et"], i + 1)
                after(e, s[f"xs{k}"], 16 * (j - 1))
                e.activation(xe[:, k].rearrange("p (w c) -> p w c", w=2), pxe[:, :, :], ACT.Identity, bias=V["b0"]).then_inc(s["xe"], 1)
                ln_scalar(e, s, "e", te(k), i, g)
            each_block(e, step)

        @block.vector
        def _(e):
            def step(i, k, j):
                after(e, s[f"got{k}"], 128 * j)
                after(e, s["et"], i)
                e.tensor_copy(gc[:, :, :, :], gx[:, k, :, :, 0:F]).then_inc(s["gc"], 1)
                after(e, s[f"yo{k}"], 16 * (j - 1))
                ln_vector(e, s, "z", tz(k), i)
                copy(e, tiles(g["ptrI"], i), gx[:, k, 0, :, F])
                after(e, s["gc"], i + 1)
                copy(e, tiles(g["cntS"], i), gx[:, k, 0, :, F + 1]).then_inc(s["ptr"], 1)
                after(e, s["hc"], i)
                ln_vector(e, s, "e", te(k), i)
                after(e, s["he"], i + 1)
                copy(e, at(HS, i), he[:, 0:P])
                copy(e, HDW[:, bass.ds(i, 1)].rearrange("p b w c -> p (b w) c"), bc_first(he[:, P:2 * P], 2)).then_inc(s["hc"], 1)
            each_block(e, step)

    with ExitStack() as c:
        s = sems(c, nc, "ds", "m z sd r")
        z = sb(c, "z", [P, 2, ROWS])
        block = c.enter_context(nc.Block())

        @block.vector
        def _(e):
            e.tensor_scalar(z[:, 0], g["cntS"][:, :], 1.0, None, ALU.max).then_inc(s["m"], 1)
            e.tensor_scalar(z[:, 1], g["cntS"][:, :], 0.5, None, ALU.is_gt).then_inc(s["z"], 1)
            e.wait_ge(s["sd"], 1)
            e.reciprocal(z[:, 0], z[:, 0]).then_inc(s["r"], 1)
            e.wait_ge(s["z"], 1)
            e.wait_ge(s["r"], 1)
            e.tensor_tensor(g["dinvS"][:, :], z[:, 0], z[:, 1], ALU.mult)

        @block.scalar
        def _(e):
            e.wait_ge(s["m"], 1)
            e.activation(z[:, 0], z[:, 0], ACT.Sqrt).then_inc(s["sd"], 1)


def spline(nc, g, l):
    a, V, BD, sb, psum, ident = g["a"], g["V"], g["BD"], g["sb"], g["psum"], g["ident"]
    HS, MSG, basis = g["HS"], g["MSG"], g["basis"]
    with ExitStack() as c:
        s = sems(c, nc, f"sp{l}", "w " + GATHER + " yi0 yi1 yo0 yo1 ex ev lk ey hs hsd t1 t4 cf tt ttc y prod red m mw "
                 "zh zr zv zl zy st ag")
        px, pt = psum(c, "px", [P, P]), psum(c, "ptm", [P, P])
        ptt = psum(c, "ptt", [P, Q, P])
        py = [psum(c, f"py{n}", [P, 512]) for n in range(2)]
        pm, pz = psum(c, "pm", [P, P]), psum(c, "pz", [P, NB])
        Wl = sb(c, "Wl", [P, 16, F])
        gx, st = sb(c, "gx", [P, 2, Q, F]), sb(c, "st", [P, 2, Q], I32)
        v, lk, hs = sb(c, "v", [P, P]), sb(c, "lk", [P, P]), sb(c, "hs", [P, P])
        T4, cf = sb(c, "T4", [P, Q, KS, F]), sb(c, "cf", [P, 2, Q, KS, KS])
        TT, prod, msg = sb(c, "TT", [P, 2, Q, P]), sb(c, "prod", [P, 2, 16, F]), sb(c, "msg", [P, Q, F])
        yz, zv = sb(c, "yz", [P, 2, NB]), sb(c, "zv", [P, 2, NB])
        A, C = V[f"a{l - 1}"], V[f"c{l - 1}"]
        block = c.enter_context(nc.Block())

        @block.gpsimd
        def _(e):
            if l > 1:
                each_block(e, lambda i, k, j: gather(e, s, st, k, j, i, g["ptrI"], g["runs"], gx, s["ex"]))

        @block.sync
        def _(e):
            Ws = a[f"W{l}"]
            for k2 in range(KS):
                e.dma_start(Wl[32 * k2:32 * k2 + 32], Ws[16 * k2:16 * k2 + 16].rearrange("k c o -> c k o")).then_inc(s["w"], 16)

            def load(i, k, j):
                after(e, s["zy"], i - 1)
                e.dma_start(yz[:, k], g["yf"][bass.ds(i + (l - 1) * BLOCKS, 1)].rearrange("b p c -> (b p) c")).then_inc(s[f"yi{k}"], 16)

            def store(i, k, j):
                after(e, s["zy"], i + 1)
                e.dma_start(g["yf"][bass.ds(i + l * BLOCKS, 1)].rearrange("b p c -> (b p) c"), zv[:, k]).then_inc(s[f"yo{k}"], 16)
            each_block_ahead(e, load, store)
            for k in range(2):
                e.wait_ge(s[f"yo{k}"], 16 * (BLOCKS // 2))

        @block.tensor
        def _(e):
            e.wait_ge(s["w"], 64)

            def head(i, k, j):
                if l > 1:
                    after(e, s[f"got{k}"], 64 * j)
                    after(e, s["ev"], i)
                    e.matmul(px[:, :], BD[f"R{l - 1}"], at(HS, i), start=True, stop=False)
                    e.matmul(px[:, :], gx[:, k, :, :], ident, start=False, stop=True).then_inc(s["ex"], 1)
                after(e, s["zh"], i + 1)
                after(e, s["zv"], i)
                e.matmul(pz[:, :], BD[f"R{l}"], yz[:, k], start=True, stop=True).then_inc(s["zr"], 1)
                after(e, s["hs"], i + 1)
                after(e, s["t4"], i)
                e.transpose(pt[:, :], hs[:, :], ident).then_inc(s["t1"], 1)
                after(e, s["t4"], i + 1)
                for q in range(Q):
                    mm = e.transpose(ptt[:, q, :], T4[:, q].rearrange("p k f -> p (k f)"), ident)
                mm.then_inc(s["tt"], 1)

            def body(i, k, j):
                after(e, s["ttc"], i + 1)
                for q in range(Q):
                    after(e, s["prod"], Q * i + q - 1)
                    e.matmul(py[q % 2][:, :], TT[:, k, q, :], Wl[:, :, :], start=True, stop=True).then_inc(s["y"], 1)
                after(e, s["red"], Q * (i + 1))
                after(e, s["mw"], i)
                e.transpose(pm[:, :], msg[:, :, :], ident).then_inc(s["m"], 1)
            each_block_ahead(e, head, body)

        @block.scalar
        def _(e):
            def head(i, k, j):
                after(e, s[f"yi{k}"], 16 * j)
                e.activation(yz[:, k], yz[:, k], ACT.Identity, bias=C, scale=A).then_inc(s["zh"], 1)
                if l > 1:
                    after(e, s["ex"], i + 1)
                    after(e, s["ey"], i)
                    e.activation(v[:, :], px[:, :], ACT.Identity, bias=V[f"b{l - 1}"]).then_inc(s["ev"], 1)
                after(e, s["zr"], i + 1)
                after(e, s["st"], i - 1)
                after(e, s[f"yo{k}"], 16 * (j - 1))
                e.activation(zv[:, k], pz[:, :], ACT.Identity, bias=V[f"b{l}"]).then_inc(s["zv"], 1)
                if l > 1:
                    after(e, s["ey"], i + 1)
                    after(e, s["t1"], i)
                    after(e, s["hsd"], i)
                    e.activation(hs[:, :], lk[:, :], ACT.Identity, bias=C, scale=A).then_inc(s["hs"], 1)
                after(e, s["tt"], i + 1)
                after(e, s["y"], Q * (i - 1))
                e.copy(TT[:, k], ptt[:, :, :]).then_inc(s["ttc"], 1)
            each_block(e, head)

        @block.vector
        def _(e):
            def head(i, k, j):
                if l > 1:
                    after(e, s["ev"], i + 1)
                    after(e, s["hs"], i)
                    e.scalar_tensor_tensor(lk[:, :], v[:, :], SLOPE, v[:, :], ALU.mult, ALU.max).then_inc(s["lk"], 1)
                    after(e, s["lk"], i + 1)
                    e.tensor_tensor(lk[:, :], lk[:, :], at(HS, i), ALU.add).then_inc(s["ey"], 1)
                else:
                    after(e, s["t1"], i)
                    copy(e, hs[:, :], at(HS, i)).then_inc(s["hs"], 1)
                b0, b1, b2 = (basis[:, d].rearrange("p (q b) k -> p q b k", q=Q)[:, :, bass.ds(i, 1)].rearrange("p q b k -> p (q b) k") for d in range(3))
                after(e, s["prod"], Q * (i - 1))
                e.tensor_tensor(cf[:, k], bc(b1, KS), bc_mid(b0, KS), ALU.mult).then_inc(s["cf"], 1)
                if l > 1:
                    after(e, s["hs"], i + 1)
                    copy(e, at(HS, i), hs[:, :]).then_inc(s["hsd"], 1)
                after(e, s["t1"], i + 1)
                after(e, s["tt"], i)
                e.tensor_tensor(T4[:, :, :, :], bc_mid(pt[:, :].rearrange("p (q f) -> p q f", q=Q), KS), bc(b2, F), ALU.mult).then_inc(s["t4"], 1)
                after(e, s["zv"], i + 1)
                if l < 3:
                    e.scalar_tensor_tensor(zv[:, k], zv[:, k], SLOPE, zv[:, k], ALU.mult, ALU.max).then_inc(s["zl"], 1)
                    after(e, s["zl"], i + 1)
                e.tensor_tensor(zv[:, k], zv[:, k], yz[:, k], ALU.add).then_inc(s["zy"], 1)
                after(e, s["zy"], i + 1)
                e.bn_stats(g["stats"][:, bass.ds(i, 1), :].rearrange("p b c -> p (b c)"), zv[:, k]).then_inc(s["st"], 1)

            def body(i, k, j):
                after(e, s["cf"], i + 1)
                after(e, s["m"], i)
                for q in range(Q):
                    n = Q * i + q + 1
                    after(e, s["y"], n)
                    after(e, s["red"], n - 2)
                    e.tensor_tensor(prod[:, q % 2], py[q % 2][:, :].rearrange("p (k f) -> p k f", f=F),
                                    bc(cf[:, k, q].rearrange("p a b -> p (a b)"), F), ALU.mult).then_inc(s["prod"], 1)
                    after(e, s["prod"], n)
                    e.tensor_reduce(msg[:, q, :], prod[:, q % 2].rearrange("p k f -> p f k"), AX.X, ALU.add).then_inc(s["red"], 1)
                after(e, s["m"], i + 1)
                copy(e, at(MSG, i), pm[:, :]).then_inc(s["mw"], 1)
            each_block_ahead(e, head, body)
            e.wait_ge(s["st"], BLOCKS)
            e.bn_aggr(g["agg"][:, 0:2], g["stats"][:, :, :].rearrange("p b (t c) -> p (b t) c", c=3)).then_inc(s["ag"], 1)


def run_end(nc, g, l):
    V, BD, sb, psum, ident = g["V"], g["BD"], g["sb"], g["psum"], g["ident"]
    HDW, MSG, agg = g["HDW"], g["MSG"], g["agg"]
    with ExitStack() as c:
        s = sems(c, nc, f"re{l}", "zero mt t ag r0 r1 x v lk y ym r sq r2 a1 a2 norm p q f n")
        pt, px, pg = psum(c, "pt", [P, Q, F]), psum(c, "px", [P, 2, P]), psum(c, "pg", [P, 2])
        mt, ag = sb(c, "mt", [P, P]), sb(c, "ag", [P, 2, Q, F])
        v, ym, sq = sb(c, "v", [P, 2, P]), sb(c, "ym", [P, 2, P]), sb(c, "sq", [P, 2, P])
        r1, r2, acc = sb(c, "r1", [P, 2]), sb(c, "r2", [P, 2]), sb(c, "acc", [P, 2, 2])
        f = sb(c, "f", [P, 8])
        block = c.enter_context(nc.Block())

        def hdw(i):
            return HDW[:, bass.ds(i, 1)].rearrange("p b w c -> p (b w) c")

        @block.sync
        def _(e):
            def store(i, k, j):
                after(e, s["ag"], i + 1)
                e.dma_start(g["runs"][0:EP, :].rearrange("(q b p) f -> b p q f", q=Q, b=BLOCKS)[bass.ds(i, 1)].rearrange("b p q f -> (b p) q f"),
                            ag[:, k]).then_inc(s[f"r{k}"], 16)
            each_block(e, store)
            for k in range(2):
                e.wait_ge(s[f"r{k}"], 16 * (BLOCKS // 2))

        @block.tensor
        def _(e):
            def head(i, k, j):
                after(e, s["mt"], i + 1)
                after(e, s["ag"], i)
                e.transpose(pt[:, :, :].rearrange("p q f -> p (q f)"), mt[:, :], ident).then_inc(s["t"], 1)

            def body(i, k, j):
                after(e, s["ag"], i + 1)
                after(e, s["v"], i)
                e.matmul(px[:, :, :], BD[f"R{l}"], hdw(i), start=True, stop=False, skip_group_check=True)
                e.matmul(px[:, 0, :], ag[:, k, :, :], ident, start=False, stop=True, skip_group_check=True).then_inc(s["x"], 1)
            each_block_ahead(e, head, body)
            e.wait_ge(s["f"], 3)
            e.matmul(pg[:, :], g["groups"], f[:, 0:2], start=True, stop=True).then_inc(s["p"], 1)

        @block.scalar
        def _(e):
            def body(i, k, j):
                after(e, s["x"], i + 1)
                after(e, s["y"], i)
                e.activation(v[:, :, :], px[:, :, :], ACT.Identity, bias=V[f"b{l}"]).then_inc(s["v"], 1)
                after(e, s["ym"], i + 1)
                after(e, s["r2"], i)
                e.activation(sq[:, :, :], ym[:, :, :], ACT.Square).then_inc(s["sq"], 1)
            each_block(e, body)
            e.wait_ge(s["q"], 3)
            e.activation(f[:, 4:5], f[:, 4:5], ACT.Sqrt, bias=V["eps"]).then_inc(s["q"], 1)

        @block.vector
        def _(e):
            e.memset(acc[:, :, :], 0.0).then_inc(s["zero"], 1)
            e.wait_ge(s["zero"], 1)

            def head(i, k, j):
                after(e, s["t"], i)
                e.scalar_tensor_tensor(mt[:, :], at(g["first"], i), g["carry"][:, 0:1], at(MSG, i), ALU.mult, ALU.add).then_inc(s["mt"], 1)
                after(e, s["t"], i + 1)
                after(e, s[f"r{k}"], 16 * (j - 1))
                after(e, s["x"], i - 1)
                e.tensor_tensor(ag[:, k], pt[:, :, :], bc(tiles(g["rcE"], i), F), ALU.mult).then_inc(s["ag"], 1)

            def body(i, k, j):
                after(e, s["v"], i + 1)
                if l < 3:
                    e.scalar_tensor_tensor(v[:, :, :], v[:, :, :], SLOPE, v[:, :, :], ALU.mult, ALU.max).then_inc(s["lk"], 1)
                    after(e, s["lk"], i + 1)
                e.tensor_tensor(hdw(i), v[:, :, :], hdw(i), ALU.add).then_inc(s["y"], 1)
                after(e, s["y"], i + 1)
                after(e, s["sq"], i)
                after(e, s["r"], i)
                e.tensor_tensor(ym[:, :, :], hdw(i), bc_first(at(g["last"], i), 2), ALU.mult).then_inc(s["ym"], 1)
                after(e, s["ym"], i + 1)
                after(e, s["a1"], i)
                e.tensor_reduce(r1[:, :], ym[:, :, :], AX.X, ALU.add).then_inc(s["r"], 1)
                after(e, s["r"], i + 1)
                e.tensor_tensor(acc[:, 0, :], acc[:, 0, :], r1[:, :], ALU.add).then_inc(s["a1"], 1)
                after(e, s["sq"], i + 1)
                after(e, s["a2"], i)
                e.tensor_reduce(r2[:, :], sq[:, :, :], AX.X, ALU.add).then_inc(s["r2"], 1)
                after(e, s["r2"], i + 1)
                e.tensor_tensor(acc[:, 1, :], acc[:, 1, :], r2[:, :], ALU.add).then_inc(s["a2"], 1)
            each_block_ahead(e, head, body)
            e.wait_ge(s["a1"], BLOCKS)
            e.wait_ge(s["a2"], BLOCKS)
            e.tensor_tensor(f[:, 2:4], acc[:, :, 0], acc[:, :, 1], ALU.subtract).then_inc(s["n"], 1)
            e.scalar_tensor_tensor(f[:, 1:2], agg[:, 0:1], agg[:, 0:1], agg[:, 1:2], ALU.mult, ALU.add).then_inc(s["f"], 1)
            e.tensor_copy(f[:, 0:1], agg[:, 0:1]).then_inc(s["f"], 1)
            e.wait_ge(s["f"], 2)
            e.wait_ge(s["n"], 1)
            e.scalar_tensor_tensor(f[:, 0:2], f[:, 0:2], float(N // Q), f[:, 2:4], ALU.mult, ALU.add).then_inc(s["f"], 1)
            e.wait_ge(s["p"], 1)
            e.tensor_scalar(f[:, 4:6], pg[:, :], 1.0 / N, None, ALU.mult).then_inc(s["q"], 1)
            e.wait_ge(s["q"], 1)
            e.tensor_tensor(f[:, 6:7], f[:, 4:5], f[:, 4:5], ALU.mult).then_inc(s["n"], 1)
            e.tensor_copy(f[:, 7:8], f[:, 4:5]).then_inc(s["q"], 1)
            e.wait_ge(s["n"], 2)
            e.wait_ge(s["q"], 2)
            e.tensor_tensor(f[:, 4:5], f[:, 5:6], f[:, 6:7], ALU.subtract).then_inc(s["q"], 1)
            e.wait_ge(s["q"], 4)
            e.reciprocal(f[:, 5:6], f[:, 4:5]).then_inc(s["n"], 1)
            e.wait_ge(s["n"], 3)
            e.tensor_tensor(V[f"a{l}"], V[f"g{l}"], f[:, 5:6], ALU.mult).then_inc(s["n"], 1)
            e.wait_ge(s["n"], 4)
            e.tensor_tensor(f[:, 6:7], f[:, 7:8], V[f"a{l}"], ALU.mult).then_inc(s["n"], 1)
            e.wait_ge(s["n"], 5)
            e.tensor_tensor(V[f"c{l}"], V[f"be{l}"], f[:, 6:7], ALU.subtract).then_inc(s["n"], 1)
            e.wait_ge(s["n"], 6)
            flat = HDW[:, :, :, :].rearrange("p b w c -> p (b w c)")
            e.tensor_scalar(flat, flat, V[f"a{l}"], V[f"c{l}"], ALU.mult, ALU.add).then_inc(s["norm"], 1)


def xsd_block(g, i):
    return g["xsd"][bass.ds(i, 1)].rearrange("b p c -> (b p) c")


def hops_start(nc, g):
    V, BD, sb, psum, ident, HS, HDW, MSG = g["V"], g["BD"], g["sb"], g["psum"], g["ident"], g["HS"], g["HDW"], g["MSG"]
    with ExitStack() as c:
        s = sems(c, nc, "hp", GATHER + " xi0 xi1 xo0 xo1 ex ev ey hn xd hc hd t1 hm m mw " + ln_sems("e"))
        px, pt, pm = psum(c, "px", [P, P]), psum(c, "pt", [P, P]), psum(c, "pm", [P, P])
        cen, var = psum(c, "cen", [P, 2 * P]), psum(c, "var", [P, 2 * P])
        gx, st = sb(c, "gx", [P, 2, Q, F]), sb(c, "st", [P, 2, Q], I32)
        v, hn, hm = sb(c, "v", [P, P]), sb(c, "hn", [P, P]), sb(c, "hm", [P, Q, F])
        x, sq, sd, h = sb(c, "x", [P, 2, 2 * P]), sb(c, "sq", [P, 2 * P]), sb(c, "sd", [P, 2 * P]), sb(c, "h", [P, 2 * P])
        xi = sb(c, "xi", [P, 2, 2 * P])

        def te(k):
            return {"x": x[:, k], "cen": cen[:, :], "sq": sq[:, :], "var": var[:, :], "sd": sd[:, :], "rs": sd[:, :], "h": h[:, :]}
        block = c.enter_context(nc.Block())

        @block.gpsimd
        def _(e):
            each_block(e, lambda i, k, j: gather(e, s, st, k, j, i, g["ptrI"], g["runs"], gx, s["ex"]))

        @block.sync
        def _(e):
            def load(i, k, j):
                after(e, s["xe"], 2 * (i - 1))
                e.dma_start(xi[:, k], xsd_block(g, i)).then_inc(s[f"xi{k}"], 16)

            def store(i, k, j):
                after(e, s["xe"], 2 * (i + 1))
                after(e, s["cene"], i + 1)
                e.dma_start(xsd_block(g, i), x[:, k]).then_inc(s[f"xo{k}"], 16)
            each_block_ahead(e, load, store)
            for k in range(2):
                e.wait_ge(s[f"xo{k}"], 16 * (BLOCKS // 2))

        @block.tensor
        def _(e):
            def step(i, k, j):
                after(e, s[f"got{k}"], 64 * j)
                after(e, s["ev"], i)
                e.matmul(px[:, :], BD["R3"], at(HS, i), start=True, stop=False)
                e.matmul(px[:, :], gx[:, k, :, :], ident, start=False, stop=True).then_inc(s["ex"], 1)
                after(e, s["xe"], 2 * (i + 1))
                ln_tensor(e, s, "e", te(k), i, g)
                after(e, s["he"], i + 1)
                after(e, s["hm"], i)
                e.transpose(pt[:, :], h[:, 0:P], ident).then_inc(s["t1"], 1)
                after(e, s["hm"], i + 1)
                after(e, s["mw"], i)
                e.transpose(pm[:, :], hm[:, :, :], ident).then_inc(s["m"], 1)
            each_block(e, step)

        @block.scalar
        def _(e):
            def step(i, k, j):
                after(e, s["ex"], i + 1)
                after(e, s["ey"], i)
                e.activation(v[:, :], px[:, :], ACT.Identity, bias=V["b3"]).then_inc(s["ev"], 1)
                after(e, s["ey"], i + 1)
                e.activation(hn[:, :], v[:, :], ACT.Identity, bias=V["c3"], scale=V["a3"]).then_inc(s["hn"], 1)
                ln_scalar(e, s, "e", te(k), i, g)
            each_block(e, step)

        @block.vector
        def _(e):
            def step(i, k, j):
                after(e, s[f"xi{k}"], 16 * j)
                after(e, s[f"xo{k}"], 16 * (j - 1))
                e.tensor_tensor(x[:, k, P:2 * P], xi[:, k, P:2 * P], HDW[:, bass.ds(i, 1), 0, :].rearrange("p b c -> p (b c)"), ALU.add).then_inc(s["xe"], 1)
                after(e, s["ev"], i + 1)
                after(e, s["hn"], i)
                e.tensor_tensor(v[:, :], v[:, :], at(HS, i), ALU.add).then_inc(s["ey"], 1)
                after(e, s["hn"], i + 1)
                e.tensor_tensor(x[:, k, 0:P], xi[:, k, 0:P], hn[:, :], ALU.add).then_inc(s["xe"], 1)
                after(e, s["t1"], i)
                after(e, s["hc"], i)
                ln_vector(e, s, "e", te(k), i)
                after(e, s["he"], i + 1)
                copy(e, at(HS, i), h[:, 0:P])
                copy(e, HDW[:, bass.ds(i, 1), 0, :].rearrange("p b c -> p (b c)"), h[:, P:2 * P]).then_inc(s["hc"], 1)
                after(e, s["t1"], i + 1)
                after(e, s["m"], i)
                e.tensor_tensor(hm[:, :, :], pt[:, :].rearrange("p (q f) -> p q f", q=Q), bc(tiles(g["dinvS"], i), F), ALU.mult).then_inc(s["hm"], 1)
                after(e, s["m"], i + 1)
                copy(e, at(MSG, i), pm[:, :]).then_inc(s["mw"], 1)
            each_block(e, step)


def hop_end(nc, g, n):
    sb, psum, ident, HDW, MSG = g["sb"], g["psum"], g["ident"], g["HDW"], g["MSG"]
    with ExitStack() as c:
        s = sems(c, nc, f"he{n}", "mt t ag r0 r1 x y")
        pt, px = psum(c, "pt", [P, Q, F]), psum(c, "px", [P, P])
        mt, ag = sb(c, "mt", [P, 2, P]), sb(c, "ag", [P, 2, Q, F])
        block = c.enter_context(nc.Block())

        @block.sync
        def _(e):
            def store(i, k, j):
                after(e, s["ag"], i + 1)
                e.dma_start(g["runs"][0:EP, :].rearrange("(q b p) f -> b p q f", q=Q, b=BLOCKS)[bass.ds(i, 1)].rearrange("b p q f -> (b p) q f"),
                            ag[:, k]).then_inc(s[f"r{k}"], 16)
            each_block(e, store)
            for k in range(2):
                e.wait_ge(s[f"r{k}"], 16 * (BLOCKS // 2))

        @block.tensor
        def _(e):
            def head(i, k, j):
                after(e, s["mt"], i + 1)
                after(e, s["ag"], i)
                e.transpose(pt[:, :, :].rearrange("p q f -> p (q f)"), mt[:, k], ident).then_inc(s["t"], 1)

            def body(i, k, j):
                after(e, s["ag"], i + 1)
                after(e, s["y"], i)
                e.transpose(px[:, :], ag[:, k, :, :], ident).then_inc(s["x"], 1)
            each_block_ahead(e, head, body)

        @block.vector
        def _(e):
            def mt_block(i, k):
                after(e, s["t"], i - 1)
                e.scalar_tensor_tensor(mt[:, k], at(g["first"], i), g["carry"][:, 0:1], at(MSG, i), ALU.mult, ALU.add).then_inc(s["mt"], 1)

            def head(i, k, j):
                mt_block(i, k)
                after(e, s["t"], i + 1)
                after(e, s[f"r{k}"], 16 * (j - 1))
                after(e, s["x"], i - 1)
                e.tensor_tensor(ag[:, k], pt[:, :, :], bc(tiles(g["dinvD"], i), F), ALU.mult).then_inc(s["ag"], 1)

            def body(i, k, j):
                after(e, s["x"], i + 1)
                d = HDW[:, bass.ds(i, 1), 0, :].rearrange("p b c -> p (b c)")
                e.tensor_tensor(d, px[:, :], d, ALU.add).then_inc(s["y"], 1)
            each_block_ahead(e, head, body)


def hop_gather(nc, g, n):
    sb, psum, ident, HS, MSG = g["sb"], g["psum"], g["ident"], g["HS"], g["MSG"]
    with ExitStack() as c:
        s = sems(c, nc, f"hg{n}", GATHER + " t hs hm m mw")
        pt, pm = psum(c, "pt", [P, P]), psum(c, "pm", [P, P])
        gx, st, hm = sb(c, "gx", [P, 2, Q, F]), sb(c, "st", [P, 2, Q], I32), sb(c, "hm", [P, Q, F])
        block = c.enter_context(nc.Block())

        @block.gpsimd
        def _(e):
            def step(i, k, j):
                after(e, s["hm"], i - 1)
                gather(e, s, st, k, j, i, g["ptrI"], g["runs"], gx, s["t"])
            each_block(e, step)

        @block.tensor
        def _(e):
            def step(i, k, j):
                after(e, s[f"got{k}"], 64 * j)
                after(e, s["hs"], i)
                e.transpose(pt[:, :], gx[:, k, :, :], ident).then_inc(s["t"], 1)
                after(e, s["hm"], i + 1)
                after(e, s["mw"], i)
                e.transpose(pm[:, :], hm[:, :, :], ident).then_inc(s["m"], 1)
            each_block(e, step)

        @block.vector
        def _(e):
            def step(i, k, j):
                after(e, s[f"got{k}"], 64 * j)
                after(e, s["m"], i)
                e.tensor_tensor(hm[:, :, :], gx[:, k], bc(tiles(g["dinvS"], i), F), ALU.mult).then_inc(s["hm"], 1)
                after(e, s["t"], i + 1)
                e.tensor_tensor(at(HS, i), pt[:, :], at(HS, i), ALU.add).then_inc(s["hs"], 1)
                after(e, s["m"], i + 1)
                copy(e, at(MSG, i), pm[:, :]).then_inc(s["mw"], 1)
            each_block(e, step)


def dense_end(nc, g):
    V, BD, sb, psum, ident = g["V"], g["BD"], g["sb"], g["psum"], g["ident"]
    with ExitStack() as c:
        s = sems(c, nc, "de", "yi0 yi1 xi0 xi1 oo0 oo1 y3 ab ga gb o ov o2 ot oc " + ln_sems("1") + " " + ln_sems("2"))
        cen, var = psum(c, "cen", [P, NB]), psum(c, "var", [P, NB])
        pa, pb, po = psum(c, "pa", [P, NB]), psum(c, "pb", [P, NB]), psum(c, "po", [P, NB])
        pt = psum(c, "pt", [NP, 4, P])
        y, x = sb(c, "y", [P, 2, NB]), sb(c, "x", [P, 2, NB])
        sq, sd, h = sb(c, "sq", [P, NB]), sb(c, "sd", [P, NB]), sb(c, "h", [P, NB])
        ot = sb(c, "ot", [NP, 2, Q, 4, F])

        def tz(k):
            return {"x": x[:, k], "cen": cen[:, :], "sq": sq[:, :], "var": var[:, :], "sd": sd[:, :], "rs": sd[:, :], "h": h[:, :]}
        block = c.enter_context(nc.Block())
        outv = g["out"].rearrange("(q b p n) f -> b p q (n f)", q=Q, b=BLOCKS, p=NP)

        @block.sync
        def _(e):
            def load(i, k, j):
                after(e, s["o2"], i - 1)
                after(e, s["ot"], i - 1)
                e.dma_start(y[:, k], g["yf"][bass.ds(i + 3 * BLOCKS, 1)].rearrange("b p c -> (b p) c")).then_inc(s[f"yi{k}"], 16)
                e.dma_start(x[:, k], g["x0f"][bass.ds(i, 1)].rearrange("b p c -> (b p) c")).then_inc(s[f"xi{k}"], 16)

            def store(i, k, j):
                after(e, s["oc"], i + 1)
                e.dma_start(outv[bass.ds(i, 1)].rearrange("b p q w -> (b p) q w"), ot[:, k].rearrange("p q n f -> p q (n f)")).then_inc(s[f"oo{k}"], 16)
            each_block_ahead(e, load, store)
            for k in range(2):
                e.wait_ge(s[f"oo{k}"], 16 * (BLOCKS // 2))

        @block.tensor
        def _(e):
            def step(i, k, j):
                after(e, s["h2"], i)
                ln_tensor(e, s, "1", tz(k), i, g)
                after(e, s["h1"], i + 1)
                ln_tensor(e, s, "2", tz(k), i, g)
                after(e, s["h2"], i + 1)
                after(e, s["gb"], i)
                e.matmul(pa[:, :], BD["w2aA"], h[:, :], start=True, stop=True)
                e.matmul(pb[:, :], BD["w2aB"], h[:, :], start=True, stop=True).then_inc(s["ab"], 1)
                after(e, s["ga"], i + 1)
                after(e, s["gb"], i + 1)
                after(e, s["ov"], i)
                e.matmul(po[:, :], BD["w2bA"], sq[:, :], start=True, stop=False)
                e.matmul(po[:, :], BD["w2bB"], sd[:, :], start=False, stop=True).then_inc(s["o"], 1)
                after(e, s["o2"], i + 1)
                after(e, s["oc"], i)
                for n in range(4):
                    mm = e.transpose(pt[:, n, :], y[:, k, n * NP:(n + 1) * NP], ident)
                mm.then_inc(s["ot"], 1)
            each_block(e, step)

        @block.scalar
        def _(e):
            def step(i, k, j):
                after(e, s[f"yi{k}"], 16 * j)
                e.activation(y[:, k], y[:, k], ACT.Identity, bias=V["c3"], scale=V["a3"]).then_inc(s["y3"], 1)
                after(e, s["o"], i)
                ln_scalar(e, s, "1", tz(k), i, g)
                after(e, s["h1"], i + 1)
                ln_scalar(e, s, "2", tz(k), i, g)
                after(e, s["ab"], i + 1)
                e.activation(sq[:, :], pa[:, :], ACT.Relu, bias=V["b2aA"]).then_inc(s["ga"], 1)
                e.activation(sd[:, :], pb[:, :], ACT.Relu, bias=V["b2aB"]).then_inc(s["gb"], 1)
                after(e, s["o"], i + 1)
                e.activation(y[:, k], po[:, :], ACT.Identity, bias=V["b2b"]).then_inc(s["ov"], 1)
                after(e, s["ot"], i + 1)
                after(e, s[f"oo{k}"], 16 * (j - 1))
                e.copy(ot[:, k].rearrange("p q n f -> p n q f"), pt[:, :, :].rearrange("p n (q f) -> p n q f", q=Q)).then_inc(s["oc"], 1)
            each_block(e, step)

        @block.vector
        def _(e):
            def step(i, k, j):
                after(e, s[f"xi{k}"], 16 * j)
                after(e, s["y3"], i + 1)
                e.tensor_tensor(x[:, k], x[:, k], y[:, k], ALU.add).then_inc(s["x1"], 1)
                ln_vector(e, s, "1", tz(k), i)
                after(e, s["h1"], i + 1)
                e.scalar_tensor_tensor(x[:, k], h[:, :], 0.25, x[:, k], ALU.mult, ALU.add).then_inc(s["x2"], 1)
                after(e, s["x2"], i + 1)
                ln_vector(e, s, "2", tz(k), i)
                after(e, s["ov"], i + 1)
                e.tensor_tensor(y[:, k], y[:, k], x[:, k], ALU.add).then_inc(s["o2"], 1)
            each_block(e, step)


def edge_mlp(nc, g):
    V, BD, sb, psum, ident, HS, HDW, MSG = g["V"], g["BD"], g["sb"], g["psum"], g["ident"], g["HS"], g["HDW"], g["MSG"]
    with ExitStack() as c:
        s = sems(c, nc, "em", GATHER + " xi0 xi1 xo0 xo1 at0 at1 pad t hs xd hc att atc j h1 m mw " + ln_sems("e"))
        px, pat = psum(c, "px", [P, P]), psum(c, "pat", [P, P])
        cen, var = psum(c, "cen", [P, 2 * P]), psum(c, "var", [P, 2 * P])
        pj, pm = psum(c, "pj", [P, 3, P]), psum(c, "pm", [P, 2, P])
        gx, st = sb(c, "gx", [P, 2, Q, F]), sb(c, "st", [P, 2, Q], I32)
        hs, x, xi = sb(c, "hs", [P, P]), sb(c, "x", [P, 2, 2 * P]), sb(c, "xi", [P, 2, 2 * P])
        sq, sd, h = sb(c, "sq", [P, 2 * P]), sb(c, "sd", [P, 2 * P]), sb(c, "h", [P, 2 * P])
        atr, atf, h1 = sb(c, "atr", [P, 2, Q, F]), sb(c, "atf", [P, P]), sb(c, "h1", [P, 3, P])

        def te(k):
            return {"x": x[:, k], "cen": cen[:, :], "sq": sq[:, :], "var": var[:, :], "sd": sd[:, :], "rs": sd[:, :], "h": h[:, :]}
        block = c.enter_context(nc.Block())

        @block.gpsimd
        def _(e):
            each_block(e, lambda i, k, j: gather(e, s, st, k, j, i, g["ptrI"], g["runs"], gx, s["t"]))

        @block.sync
        def _(e):
            e.wait_ge(s["pad"], 2)

            def load(i, k, j):
                after(e, s["xe"], 2 * (i - 1))
                e.dma_start(xi[:, k], xsd_block(g, i)).then_inc(s[f"xi{k}"], 16)
                after(e, s["att"], i - 1)
                e.dma_start(atr[:, k, :, 0:DE], g["attr16"].rearrange("(q b p) d -> b p q d", q=Q, b=BLOCKS)[bass.ds(i, 1)]
                            .rearrange("b p q d -> (b p) q d")).then_inc(s[f"at{k}"], 16)

            def store(i, k, j):
                after(e, s["xe"], 2 * (i + 1))
                after(e, s["cene"], i + 1)
                e.dma_start(xsd_block(g, i), x[:, k]).then_inc(s[f"xo{k}"], 16)
            each_block_ahead(e, load, store)
            for k in range(2):
                e.wait_ge(s[f"xo{k}"], 16 * (BLOCKS // 2))

        @block.tensor
        def _(e):
            def step(i, k, j):
                after(e, s[f"at{k}"], 16 * j)
                after(e, s["atc"], i)
                e.transpose(pat[:, :], atr[:, k, :, :], ident).then_inc(s["att"], 1)
                after(e, s[f"got{k}"], 64 * j)
                after(e, s["hs"], i)
                e.transpose(px[:, :], gx[:, k, :, :], ident).then_inc(s["t"], 1)
                after(e, s["xe"], 2 * (i + 1))
                ln_tensor(e, s, "e", te(k), i, g)
                after(e, s["he"], i + 1)
                after(e, s["atc"], i + 1)
                after(e, s["h1"], i)
                for n in range(3):
                    e.matmul(pj[:, n, :], BD[f"w1x{n}"], h[:, 0:P], start=True, stop=False)
                    mm = e.matmul(pj[:, n, :], BD[f"w1e{n}"], atf[:, :], start=False, stop=True)
                mm.then_inc(s["j"], 1)
                after(e, s["h1"], i + 1)
                after(e, s["mw"], i)
                for w, name in enumerate(("wcA", "wcB")):
                    for n in range(3):
                        mm = e.matmul(pm[:, w, :], BD[f"{name}{n}"], h1[:, n, :], start=(n == 0), stop=(n == 2))
                mm.then_inc(s["m"], 1)
            each_block(e, step)

        @block.scalar
        def _(e):
            def step(i, k, j):
                after(e, s["att"], i + 1)
                after(e, s["j"], i)
                e.copy(atf[:, :], pat[:, :]).then_inc(s["atc"], 1)
                ln_scalar(e, s, "e", te(k), i, g)
                after(e, s["j"], i + 1)
                after(e, s["m"], i)
                e.activation(h1[:, :, :], pj[:, :, :], ACT.Relu).then_inc(s["h1"], 1)
            each_block(e, step)

        @block.vector
        def _(e):
            e.memset(atr[:, :, :, :], 0.0).then_inc(s["pad"], 1)
            e.wait_ge(s["pad"], 1)
            e.memset(atr[:, :, :, DE:DE + 1], 1.0).then_inc(s["pad"], 1)

            def step(i, k, j):
                d = HDW[:, bass.ds(i, 1), 0, :].rearrange("p b c -> p (b c)")
                after(e, s[f"xi{k}"], 16 * j)
                after(e, s[f"xo{k}"], 16 * (j - 1))
                e.scalar_tensor_tensor(x[:, k, P:2 * P], d, 0.25, xi[:, k, P:2 * P], ALU.mult, ALU.add).then_inc(s["xe"], 1)
                after(e, s["t"], i + 1)
                e.tensor_tensor(hs[:, :], px[:, :], at(HS, i), ALU.add).then_inc(s["hs"], 1)
                after(e, s["hs"], i + 1)
                e.scalar_tensor_tensor(x[:, k, 0:P], hs[:, :], 0.25, xi[:, k, 0:P], ALU.mult, ALU.add).then_inc(s["xe"], 1)
                after(e, s["j"], i)
                after(e, s["hc"], i)
                ln_vector(e, s, "e", te(k), i)
                after(e, s["he"], i + 1)
                copy(e, d, h[:, P:2 * P]).then_inc(s["hc"], 1)
                after(e, s["m"], i + 1)
                copy(e, at(MSG, i), pm[:, 0, :])
                copy(e, at(HS, i), pm[:, 1, :]).then_inc(s["mw"], 1)
            each_block(e, step)


def node_mlp(nc, g):
    V, BD, sb, psum, ident, HDW = g["V"], g["BD"], g["sb"], g["psum"], g["ident"], g["HDW"]
    with ExitStack() as c:
        s = sems(c, nc, "nm", "bias xi0 xi1 mt t ag p g0 o ov o2 ot oc stg0 stg1 sent0 sent1")
        pt, ph = psum(c, "pt", [P, 2, P]), psum(c, "ph", [P, 2, P])
        po, pr = psum(c, "po", [P, P]), psum(c, "pr", [P, P])
        mt, ag, x = sb(c, "mt", [P, 2, P]), sb(c, "ag", [P, 2, Q, F]), sb(c, "x", [P, 2, 2 * P])
        gh, o, o2 = sb(c, "gh", [P, 2, P]), sb(c, "o", [P, P]), sb(c, "o2", [P, P])
        ot, st, bias = sb(c, "ot", [P, 2, Q, F]), sb(c, "st", [P, 2, Q], I32), sb(c, "bias", [P, 2])
        block = c.enter_context(nc.Block())

        @block.sync
        def _(e):
            def load(i, k, j):
                after(e, s["o2"], i - 1)
                e.dma_start(x[:, k], xsd_block(g, i)).then_inc(s[f"xi{k}"], 16)
            each_block(e, load)

        @block.gpsimd
        def _(e):
            def step(i, k, j):
                after(e, s["oc"], i + 1)
                after(e, s[f"sent{k}"], 64 * (j - 1))
                stage_indices(e, s, st, k, j, g["outI"], i)
                for q in range(Q):
                    e.indirect_dma_start(g["out"], bass.IndirectOffsetOnAxis(ap=st[:, k, q:q + 1], axis=0), ot[:, k, q, :], None,
                                         bounds_check=N - 1, oob_is_err=False).then_inc(s[f"sent{k}"], 16)
            each_block(e, step)
            for k in range(2):
                e.wait_ge(s[f"sent{k}"], 64 * (BLOCKS // 2))

        @block.tensor
        def _(e):
            def step(i, k, j):
                after(e, s["mt"], 2 * (i + 1))
                after(e, s["ag"], i)
                for w in range(2):
                    mm = e.transpose(pt[:, w, :], mt[:, w, :], ident)
                mm.then_inc(s["t"], 1)
                after(e, s["ag"], i + 1)
                after(e, s["g0"], 2 * i)
                d = HDW[:, bass.ds(i, 1), 0, :].rearrange("p b c -> p (b c)")
                for w, name in enumerate(("w2aA", "w2aB")):
                    e.matmul(ph[:, w, :], BD[name], d, start=True, stop=False)
                    mm = e.matmul(ph[:, w, :], ag[:, w, :, :], ident, start=False, stop=True)
                mm.then_inc(s["p"], 1)
                after(e, s["g0"], 2 * (i + 1))
                after(e, s["ov"], i)
                e.matmul(po[:, :], BD["w2bA"], gh[:, 0, :], start=True, stop=False)
                e.matmul(po[:, :], BD["w2bB"], gh[:, 1, :], start=False, stop=True).then_inc(s["o"], 1)
                after(e, s["o2"], i + 1)
                after(e, s["oc"], i)
                e.transpose(pr[:, :], o2[:, :], ident).then_inc(s["ot"], 1)
            each_block(e, step)

        @block.scalar
        def _(e):
            e.wait_ge(s["bias"], 2)

            def step(i, k, j):
                after(e, s["p"], i + 1)
                after(e, s["o"], i)
                for w in range(2):
                    e.activation(gh[:, w, :], ph[:, w, :], ACT.Relu, bias=bias[:, w:w + 1]).then_inc(s["g0"], 1)
                after(e, s["o"], i + 1)
                after(e, s["o2"], i)
                e.activation(o[:, :], po[:, :], ACT.Identity, bias=V["b2b"]).then_inc(s["ov"], 1)
                after(e, s["ot"], i + 1)
                after(e, s[f"sent{k}"], 64 * (j - 1))
                e.copy(ot[:, k], pr[:, :].rearrange("p (q f) -> p q f", q=Q)).then_inc(s["oc"], 1)
            each_block(e, step)

        @block.vector
        def _(e):
            e.tensor_tensor(bias[:, 0:1], V["b2aA"], V["bcA"], ALU.add).then_inc(s["bias"], 1)
            e.tensor_tensor(bias[:, 1:2], V["b2aB"], V["bcB"], ALU.add).then_inc(s["bias"], 1)

            def step(i, k, j):
                after(e, s["t"], i)
                for w, m in enumerate((g["MSG"], g["HS"])):
                    e.scalar_tensor_tensor(mt[:, w, :], at(g["first"], i), g["carry"][:, w:w + 1], at(m, i), ALU.mult, ALU.add).then_inc(s["mt"], 1)
                after(e, s["t"], i + 1)
                after(e, s["p"], i)
                r = tiles(g["rcE"], i)
                for w in range(2):
                    ins = e.tensor_tensor(ag[:, w], pt[:, w, :].rearrange("p (q f) -> p q f", q=Q), bc(r, F), ALU.mult)
                ins.then_inc(s["ag"], 1)
                after(e, s["ov"], i + 1)
                after(e, s[f"xi{k}"], 16 * j)
                after(e, s["ot"], i)
                e.tensor_tensor(o2[:, :], o[:, :], x[:, k, P:2 * P], ALU.add).then_inc(s["o2"], 1)
            each_block(e, step)


def build(nc, a, out):
    top = ExitStack()
    with top:
        def dram(name, shape, dt=F32):
            return nc.dram_tensor(name, shape, dt, kind="Internal").ap()

        used = {}

        def unique(name):
            used[name] = used.get(name, 0) + 1
            return name if used[name] == 1 else f"{name}_{used[name]}"

        def sb(c, name, shape, dt=F32):
            return c.enter_context(nc.sbuf_tensor(unique(name), shape, dt))

        def psum(c, name, shape):
            return c.enter_context(nc.psum_tensor(unique(name), shape, F32))

        g = {"a": a, "out": out, "sb": sb, "psum": psum,
             "table": dram("table", [TN, TW]),
             "runs": dram("runs", [EP + P, F]),
             "srcflat": dram("srcflat", [EP]), "cntflat": dram("cntflat", [EP]),
             "sameflat": dram("sameflat", [EP], BF16), "lastflat": dram("lastflat", [EP], BF16),
             "attr3": dram("attr3", [EP, 3]), "attr16": dram("attr16", [EP, DE]),
             "x0f": dram("x0f", [BLOCKS, P, NB]),
             "yf": dram("yf", [4 * BLOCKS, P, NB]),
             "xsd": dram("xsd", [BLOCKS, P, 2 * P])}
        for n in ("same", "last", "first"):
            g[n] = sb(top, n, [P, EC], BF16)
        g["HS"], g["MSG"] = sb(top, "HS", [P, EC]), sb(top, "MSG", [P, EC])
        g["HDW"] = sb(top, "HDW", [P, BLOCKS, 2, P])
        g["basis"] = sb(top, "basis", [P, 3, ROWS, KS])
        for n in ("srcE", "dstE", "lastE", "cntE", "cntS", "rcE", "dinvD", "dinvS"):
            g[n] = sb(top, n, [P, ROWS])
        for n in ("srcI", "dstI", "inI", "ptrI", "slotI", "outI"):
            g[n] = sb(top, n, [P, ROWS], I32)
        g["consts"] = sb(top, "consts", [P, len(CONSTS), P])
        for j, n in enumerate(CONSTS):
            g[n] = g["consts"][:, j, :]
        g["trashE"], g["carry"] = sb(top, "trashE", [P, Q]), sb(top, "carry", [P, 2])
        g["stats"], g["agg"] = sb(top, "stats", [P, BLOCKS, 6]), sb(top, "agg", [P, 2])
        g["bds"], g["vecs"] = sb(top, "bds", [P, len(BDS), P]), sb(top, "vecs", [P, len(VECS)])
        g["BD"] = {n: g["bds"][:, j, :] for j, n in enumerate(BDS)}
        g["V"] = {n: g["vecs"][:, j:j + 1] for j, n in enumerate(VECS)}

        setup(nc, g)
        degrees(nc, g)
        layer0(nc, g)
        place(nc, g)
        for l in (1, 2, 3):
            spline(nc, g, l)
            scan_phase(nc, g, f"scan{l}", [g["MSG"]])
            run_end(nc, g, l)
        hops_start(nc, g)
        dense_end(nc, g)
        for n in (1, 2, 3):
            scan_phase(nc, g, f"hscan{n}", [g["MSG"]])
            hop_end(nc, g, n)
            if n < 3:
                hop_gather(nc, g, n)
        edge_mlp(nc, g)
        scan_phase(nc, g, "mscan", [g["MSG"], g["HS"]])
        node_mlp(nc, g)


_NAMES = {"x": "x", "src": "src", "dst": "dst", "attr16": "edge_attr_16", "attr3": "edge_attr_3",
          "mu": "L0_gnn_mu", "sg": "L0_gnn_sigma", "b0": "L0_gnn_b"}
_NAMES |= {f"{n}{l}": f"L1_gnn_{n}{l}" for n in ("W", "R", "b", "g", "be") for l in (1, 2, 3)}
_NAMES |= {n: f"L3_gnn_{n}" for n in ("w1a", "b1a", "w1b", "b1b", "w2a", "b2a", "w2b", "b2b")}


def constants():
    import numpy as np
    p, q = np.arange(P)[:, None], np.arange(P)[None, :]
    eye, group = (p == q), (p // F == q // F)
    mean = np.where(group, np.float32(1 / F), np.float32(0))
    consts = np.stack([eye, eye - mean, mean, p % F == q % F, q == p + F], axis=1).astype(np.float32)
    pos = (np.arange(Q)[None, :] * P + p).astype(np.float32)
    eidx = (np.arange(ROWS)[None, :] * P + p).astype(np.float32)
    cols = np.ascontiguousarray(np.broadcast_to(np.arange(Q * P, dtype=np.float32), (P, Q * P)))
    return {"consts": consts, "pos": pos, "trash": pos + np.float32(N), "eidx": eidx, "cols": cols}


def kernel(**inputs):
    import numpy as np
    import concourse.bacc as bacc
    from concourse.bass_utils import run_bass_kernel_spmd as run

    nc = bacc.Bacc("TRN2", target_bir_lowering=False, num_devices=1)
    arrays = {n: np.ascontiguousarray(inputs[full]) for n, full in _NAMES.items()}
    arrays["W0T"] = np.ascontiguousarray(np.asarray(inputs["L0_gnn_W"]).T)
    arrays |= constants()
    args = {n: nc.dram_tensor(f"in_{n}", v.shape, mybir.dt.from_np(v.dtype), kind="ExternalInput").ap() for n, v in arrays.items()}
    out = nc.dram_tensor("out_x", (N, F), F32, kind="ExternalOutput").ap()
    build(nc, args, out)
    r = run(nc, [{f"in_{n}": v for n, v in arrays.items()}], core_ids=[0])
    return r.results[0]["out_x"]
```

```python
from contextlib import ExitStack

import concourse.bass as bass
from concourse import mybir

F32, BF16, I32 = mybir.dt.float32, mybir.dt.bfloat16, mybir.dt.int32
ACT, ALU, AX = mybir.ActivationFunctionType, mybir.AluOpType, mybir.AxisListType

N, F, E = 100000, 32, 25000
P, Q = 128, 4
BLOCKS = 50
EC = BLOCKS * P
EP = Q * EC
ROWS = EP // P
HR = ROWS // 2
FULL = E // P
REST = E - FULL * P
NB = N // Q // BLOCKS
NP = NB // 4
TW = F + 2
PADROW = N + Q * P
TN = N + Q * P + 32
SLOTS = TN * TW // 2
KS, K3 = 4, 64
DE, DH, DI = 16, 96, 48
LN_EPS = BN_EPS = 1e-5
SLOPE = 0.01
BANK = 512
CH = 10
XP = 125
NT = N // XP // CH

BDS = ["W0", "R1", "R2", "R3"] + [f"w1x{j}" for j in range(3)] + [f"w1e{j}" for j in range(3)] \
    + [f"wcA{j}" for j in range(3)] + [f"wcB{j}" for j in range(3)] + ["w2aA", "w2aB", "w2bA", "w2bB"]
VECS = ["b0", "b1", "b2", "b3", "g1", "g2", "g3", "be1", "be2", "be3", "mu0", "mu1", "mu2", "sg0", "sg1", "sg2",
        "b2aA", "b2aB", "b2b", "bcA", "bcB", "eps", "a0", "c0", "a1", "c1", "a2", "c2", "a3", "c3"]
CONSTS = ["ident", "centre", "mean", "groups", "shift"]


def after(e, sem, n):
    if not isinstance(n, int) or n > 0:
        e.wait_ge(sem, n)


def each_block(e, step):
    for j in (1, 2):
        step(2 * j - 2, 0, j)
        step(2 * j - 1, 1, j)
    with e.Fori(3, BLOCKS // 2 + 1) as j:
        step(2 * j - 2, 0, j)
        step(2 * j - 1, 1, j)


def each_block_ahead(e, head, body):
    head(0, 0, 1)
    for j in (1, 2):
        head(2 * j - 1, 1, j)
        body(2 * j - 2, 0, j)
        head(2 * j, 0, j + 1)
        body(2 * j - 1, 1, j)
    with e.Fori(3, BLOCKS // 2) as j:
        head(2 * j - 1, 1, j)
        body(2 * j - 2, 0, j)
        head(2 * j, 0, j + 1)
        body(2 * j - 1, 1, j)
    head(BLOCKS - 1, 1, BLOCKS // 2)
    body(BLOCKS - 2, 0, BLOCKS // 2)
    body(BLOCKS - 1, 1, BLOCKS // 2)


def staged(e, *stages):
    most = max(lag for lag, _ in stages)
    start = (most + 5) // 2 * 2

    def single(n):
        for lag, step in stages:
            i = n - lag
            if 0 <= i < BLOCKS:
                step(i, i % 2, i // 2 + 1)
    for n in range(start):
        single(n)
    with e.Fori(start // 2 + 1, BLOCKS // 2 + 1) as r:
        for odd in (0, 1):
            for lag, step in stages:
                k = (odd - lag) % 2
                j = r if odd - lag == k else r - (k + lag - odd) // 2
                step(2 * j - 2 + k, k, j)
    for n in range(BLOCKS, BLOCKS + most):
        single(n)


def ln_centre(pe, s, n, t, i, g, banks=1):
    after(pe, s["x" + n], i + 1)
    after(pe, s["h" + n], i + 1 - banks)
    pe.matmul(t["cen"], g["centre"], t["x"], start=True, stop=True).then_inc(s["cen" + n], 1)


def ln_square(act, s, n, t, i):
    after(act, s["cen" + n], i + 1)
    act.activation(t["sq"], t["cen"], ACT.Square).then_inc(s["sq" + n], 1)


def ln_mean(pe, s, n, t, i, g):
    after(pe, s["sq" + n], i + 1)
    pe.matmul(t["var"], g["mean"], t["sq"], start=True, stop=True).then_inc(s["var" + n], 1)


def ln_root(act, s, n, t, i, g):
    after(act, s["var" + n], i + 1)
    act.activation(t["sd"], t["var"], ACT.Sqrt, bias=g["V"]["eps"]).then_inc(s["sd" + n], 1)


def bc(ap, n):
    return ap.unsqueeze(len(ap.shape)).broadcast_to(list(ap.shape) + [n])


def bc_mid(ap, n):
    p, a, b = ap.shape
    return ap.unsqueeze(2).broadcast_to([p, a, n, b])


def bc_first(ap, n):
    p, a = ap.shape
    return ap.unsqueeze(1).broadcast_to([p, n, a])


def sems(c, nc, phase, names):
    names = names.split()
    kept = {n: nc.alloc_semaphore(f"{phase}_{n}") for n in names if n[:3] == "got" or n[:4] == "sent"}
    s = {n: c.enter_context(nc.semaphore(f"{phase}_{n}")) for n in names if n not in kept}

    def zero():
        with nc.Block() as block:
            @block.gpsimd
            def _(e):
                for sem in s.values():
                    e.sem_clear(sem)
    c.callback(zero)
    return s | kept


def at(t, i, n=P):
    return t[:, bass.ds(i * n, n)]


def tiles(t, i):
    return t[:, :].rearrange("p (q b) -> p q b", q=Q)[:, :, bass.ds(i, 1)].rearrange("p q b -> p (q b)")


def copy(e, out, in_):
    return e.tensor_scalar(out, in_, 0.0, None, ALU.add)



LN = "x cen sq var sd rs h"


def ln_sems(n):
    return " ".join(a + n for a in LN.split())


def ln_vector(dve, s, n, t, i):
    after(dve, s["sd" + n], i + 1)
    dve.reciprocal(t["rs"], t["sd"]).then_inc(s["rs" + n], 1)
    after(dve, s["rs" + n], i + 1)
    dve.scalar_tensor_tensor(t["h"], t["cen"], 0.0, t["rs"], ALU.max, ALU.mult).then_inc(s["h" + n], 1)


def stage_indices(e, s, st, k, j, table, i):
    e.tensor_copy(st[:, k, :], tiles(table, i)).then_inc(s[f"stg{k}"], 1)
    e.wait_ge(s[f"stg{k}"], 1)
    after(e, s[f"stg{k}"], j)


def gather(e, s, st, k, j, i, table, src, dst, used):
    after(e, used, i - 1)
    stage_indices(e, s, st, k, j, table, i)
    for q in range(Q):
        e.indirect_dma_start(dst[:, k, q, :], None, src, bass.IndirectOffsetOnAxis(ap=st[:, k, q:q + 1], axis=0)).then_inc(s[f"got{k}"], 16)


GATHER = "stg0 stg1 got0 got1"


def scan_phase(nc, g, tag, arrays):
    same, first, carry = g["same"], g["first"], g["carry"]
    n = len(arrays)
    with ExitStack() as c:
        s = sems(c, nc, tag, "scan x c copied")
        x = g["sb"](c, tag + "_x", [P, n])
        pc = g["psum"](c, tag + "_pc", [P, n])
        block = c.enter_context(nc.Block())

        @block.vector
        def _(e):
            e.memset(carry[:, :], 0.0).then_inc(s["copied"], 1)
            for m, t in enumerate(arrays):
                e.tensor_tensor_scan(t[:, :], same[:, :], t[:, :], 0.0, ALU.mult, ALU.add).then_inc(s["scan"], 1)
            e.wait_ge(s["scan"], n)
            e.wait_ge(s["copied"], 1)
            for r in range(Q - 1):
                for m, t in enumerate(arrays):
                    e.scalar_tensor_tensor(x[:, m:m + 1], first[:, EC - 1:EC], carry[:, m:m + 1], t[:, EC - 1:EC],
                                           ALU.mult, ALU.add).then_inc(s["x"], 1)
                e.wait_ge(s["c"], r + 1)
                e.tensor_copy(carry[:, 0:n], pc[:, :]).then_inc(s["copied"], 1)
                e.wait_ge(s["copied"], r + 2)

        @block.tensor
        def _(e):
            for r in range(Q - 1):
                e.wait_ge(s["x"], n * (r + 1))
                e.matmul(pc[:, :], g["shift"], x[:, :], start=True, stop=True).then_inc(s["c"], 1)


def setup(nc, g):
    a, V, BD, sb, psum = g["a"], g["V"], g["BD"], g["sb"], g["psum"]
    same, last, first, MSG, ident = g["same"], g["last"], g["first"], g["MSG"], g["ident"]
    srcflat, sameflat, lastflat = g["srcflat"], g["sameflat"], g["lastflat"]
    HS, HDW = g["HS"], g["HDW"][:, :, :, :].rearrange("p b w c -> p (b w c)")
    with ExitStack() as c:
        s = sems(c, nc, "in", "const clear zero idx idxw wts vec tails attr wide table pads xin0 xin1 xcp xout0 xout1 rowsf "
                              "shf flags lastf lastb tr trc slot p3t p3 base bk flat bcast wT wTc wc wcc wcd sg first done")
        zero = sb(c, "zero", [P, P])
        w1b, w1bT, w2bot = sb(c, "w1b", [DH, DH]), sb(c, "w1bT", [DH, DH]), sb(c, "w2bot", [DH, DI])
        wc, bcv, b1bc = sb(c, "wc", [DH, DI]), sb(c, "bcv", [DI, 1]), sb(c, "b1bc", [DH, 1])
        ri = sb(c, "ri", [HR, 2, 2, P], I32)
        hb = sb(c, "hb", [HR, 2, 2], I32)
        rf = sb(c, "rf", [HR, 5, 2, P])
        fb = sb(c, "fb", [HR, 2, 2, P], BF16)
        real = sb(c, "real", [HR, 2, P])
        p3r = sb(c, "p3r", [HR, 2, 3 * P])
        et = sb(c, "et", [P, ROWS])
        p3 = HS[:, 0:3 * ROWS].rearrange("p (d r) -> p d r", d=3)
        bt = HS[:, 3 * ROWS:9 * ROWS].rearrange("p (w d r) -> p w d r", w=2, d=3)
        xr = HDW[0:XP, 0:2 * NT * F].rearrange("p (k n f) -> p k n f", k=2, f=F)
        xw = HDW[0:XP, 2 * NT * F:2 * NT * (F + TW)].rearrange("p (k n f) -> p k n f", k=2, f=TW)
        pt = psum(c, "pt", [P, 2, P])
        pd = psum(c, "pd", [P, 3, P])
        pd2 = psum(c, "pd2", [P, 3, P])
        pw = psum(c, "pw", [P, 2, P])
        block = c.enter_context(nc.Block())
        halves = [(0, 0, HR), (1, HR, FULL - HR)]

        def column(v):
            return v.rearrange("(p o) -> p o", o=1)

        placed = []
        for q in range(Q):
            p = slice(32 * q, 32 * q + 32)
            h = slice(32 * q, 32 * q + 16)
            placed += [(BD["W0"][p, p], a["W0T"])] + [(BD[f"R{l}"][p, p], a[f"R{l}"]) for l in (1, 2, 3)]
            for j in range(3):
                o = slice(32 * j, 32 * j + 32)
                placed += [(BD[f"w1x{j}"][p, p], a["w1a"][0:F, o]), (BD[f"w1e{j}"][h, p], a["w1a"][F:F + DE, o]),
                           (BD[f"w1e{j}"][32 * q + DE:32 * q + DE + 1, p], a["b1a"][o].rearrange("(o n) -> o n", o=1))]
            placed += [(BD["w2aA"][p, p], a["w2a"][0:F, 0:32]), (BD["w2aB"][p, h], a["w2a"][0:F, 32:DI]),
                       (BD["w2bA"][p, p], a["w2b"][0:32, :]), (BD["w2bB"][h, p], a["w2b"][32:DI, :])]
            placed += [(V[n][p], column(a[n])) for n in ["b0", "b1", "b2", "b3", "g1", "g2", "g3", "be1", "be2", "be3", "b2b"]]
            placed += [(V["b2aA"][p], column(a["b2a"][0:32])), (V["b2aB"][h], column(a["b2a"][32:DI]))]
            placed += [(V[f"{n}{d}"][p], a[n][:, d:d + 1]) for n in ("mu", "sg") for d in range(3)]
        placed += [(b1bc[:, :], column(a["b1b"])), (w1b[:, :], a["w1b"]), (w2bot[:, :], a["w2a"][F:F + DH, :])]
        folded = []
        for q in range(Q):
            p = slice(32 * q, 32 * q + 32)
            h = slice(32 * q, 32 * q + 16)
            for j in range(3):
                o = slice(32 * j, 32 * j + 32)
                folded += [(BD[f"wcA{j}"][p, p], wc[o, 0:32]), (BD[f"wcB{j}"][p, h], wc[o, 32:DI])]
            folded += [(V["bcA"][p], bcv[0:32, :]), (V["bcB"][h], bcv[32:DI, :])]

        @block.sync
        def _(e):
            e.dma_start(g["consts"][:, :, :], a["consts"]).then_inc(s["const"], 16)
            e.dma_start(g["trashE"][:, :], a["trash"]).then_inc(s["const"], 16)
            e.wait_ge(s["clear"], 2)
            for w, n in enumerate(("src", "dst")):
                for h, r0, m in halves:
                    e.dma_start(ri[0:m, w, h, :], a[n][r0 * P:(r0 + m) * P].rearrange("(r c) -> r c", c=P)).then_inc(s["idx"], 16)
                e.dma_start(ri[FULL - HR:FULL - HR + 1, w, 1, 0:REST], a[n][FULL * P:E].rearrange("(o n) -> o n", o=1)).then_inc(s["idx"], 16)
            with nc.allow_non_contiguous_dma(reason="one word per tile or feature"):
                before, behind = column(a["dst"][P - 1:FULL * P:P]), column(a["dst"][P:E:P])
                e.dma_start(hb[1:HR, 0, 0:1], before[0:HR - 1]).then_inc(s["idx"], 16)
                e.dma_start(hb[0:FULL - HR + 1, 0, 1:2], before[HR - 1:FULL]).then_inc(s["idx"], 16)
                e.dma_start(hb[0:HR, 1, 0:1], behind[0:HR]).then_inc(s["idx"], 16)
                e.dma_start(hb[0:FULL - HR, 1, 1:2], behind[HR:FULL]).then_inc(s["idx"], 16)
                e.wait_ge(s["wts"], 3)
                for dst, src in placed:
                    e.dma_start(dst, src).then_inc(s["vec"], 16)
                e.wait_ge(s["flags"], 1)
                e.wait_ge(s["lastb"], 1)
                for h in range(2):
                    span = slice(h * HR * P, (h + 1) * HR * P)
                    for flat, t in ((sameflat, fb[:, 0, h, :]), (lastflat, fb[:, 1, h, :]), (srcflat, rf[:, 0, h, :])):
                        e.dma_start(flat[span].rearrange("(r c) -> r c", c=P), t).then_inc(s["flat"], 16)
                e.wait_ge(s["flat"], 96)
                for flat, t in ((sameflat, same), (lastflat, last)):
                    for q in range(Q):
                        e.dma_start(t[32 * q:32 * q + 32, :], flat[q * EC:(q + 1) * EC].partition_broadcast(32)).then_inc(s["bcast"], 16)
                e.wait_ge(s["wcc"], 2)
                for dst, src in folded:
                    e.dma_start(dst, src).then_inc(s["wcd"], 16)
            e.wait_ge(s["bcast"], 16 * 8)
            e.wait_ge(s["wcd"], 16 * len(folded))

        @block.scalar
        def _(e):
            x = a["x"].rearrange("(p n) f -> p n f", p=XP)
            t = g["table"][0:N, :].rearrange("(p n) f -> p n f", p=XP)
            e.wait_ge(s["zero"], 1)
            e.dma_start(g["table"][N:TN, :].rearrange("(p n) f -> p n f", p=32),
                        zero[0:32, 0:TW].unsqueeze(1).broadcast_to([32, (TN - N) // 32, TW])).then_inc(s["pads"], 16)
            e.dma_start(g["runs"][EP:EP + P, :], zero[:, 0:F]).then_inc(s["pads"], 16)
            e.dma_start(g["attr3"][E:EP, :].rearrange("(p n) f -> p (n f)", p=120), zero[0:120, 0:15]).then_inc(s["pads"], 16)
            e.dma_start(g["attr16"][E:EP, :].rearrange("(p n) f -> p (n f)", p=120), zero[0:120, 0:80]).then_inc(s["pads"], 16)
            for n in ("attr3", "attr16"):
                e.dma_start(g[n][0:E, :].rearrange("(p n) f -> p (n f)", p=100), a[n].rearrange("(p n) f -> p (n f)", p=100)).then_inc(s["attr"], 16)
            for m in range(CH + 1):
                k = m % 2
                if m < CH:
                    after(e, s["xcp"], m - 1)
                    e.dma_start(xr[:, k], x[:, m * NT:(m + 1) * NT, :]).then_inc(s[f"xin{k}"], 16)
                if m:
                    e.wait_ge(s["xcp"], m)
                    e.dma_start(t[:, (m - 1) * NT:m * NT, :], xw[:, 1 - k]).then_inc(s[f"xout{1 - k}"], 16)
            e.wait_ge(s["attr"], 32)
            e.wait_ge(s["pads"], 64)
            for h in range(2):
                e.dma_start(p3r[:, h, :], g["attr3"][h * HR * P:(h + 1) * HR * P, :].rearrange("(r c) d -> r (c d)", c=P)).then_inc(s["tails"], 16)
            for k in range(2):
                e.wait_ge(s[f"xout{k}"], 16 * (CH // 2))
            e.wait_ge(s["vec"], 16 * len(placed))
            sg = g["vecs"][:, VECS.index("sg0"):VECS.index("sg0") + 3]
            e.wait_ge(s["sg"], 3)
            e.activation(sg, sg, ACT.Sqrt).then_inc(s["sg"], 1)

        @block.gpsimd
        def _(e):
            e.memset(zero[:, :], 0.0).then_inc(s["zero"], 1)
            e.memset(xw[:, :, :, F:F + 1], float(EP)).then_inc(s["wide"], 1)
            e.memset(xw[:, :, :, F + 1:TW], 0.0).then_inc(s["wide"], 1)
            e.wait_ge(s["wide"], 2)
            for m in range(CH):
                k = m % 2
                e.wait_ge(s[f"xin{k}"], 16 * (m // 2 + 1))
                after(e, s[f"xout{k}"], 16 * (m // 2))
                e.tensor_copy(xw[:, k, :, 0:F], xr[:, k]).then_inc(s["xcp"], 1)

        @block.tensor
        def _(e):
            e.wait_ge(s["const"], 32)
            e.wait_ge(s["lastf"], 3)
            for n, w in enumerate((0, 1, 4)):
                after(e, s["trc"], n)
                for h in range(2):
                    mm = e.transpose(pt[:, h, 0:HR], rf[:, w, h, :], ident[0:HR, 0:HR])
                mm.then_inc(s["tr"], 1)
            e.wait_ge(s["tails"], 32)
            for h, p in ((0, pd), (1, pd2)):
                for d in range(3):
                    mm = e.transpose(p[:, d, 0:HR], p3r[:, h, :].rearrange("r (c d) -> r c d", d=3)[:, :, d], ident[0:HR, 0:HR])
            mm.then_inc(s["p3t"], 1)
            e.wait_ge(s["vec"], 16 * len(placed))
            e.transpose(pw[0:DH, 0, 0:DH], w1b[:, :], ident[0:DH, 0:DH]).then_inc(s["wT"], 1)
            e.wait_ge(s["wTc"], 1)
            e.matmul(pw[0:DH, 1, 0:DI], w1bT[:, :], w2bot[:, :], start=True, stop=True).then_inc(s["wc"], 1)
            e.wait_ge(s["wcc"], 1)
            e.matmul(pw[0:DI, 0, 0:1], w2bot[:, :], b1bc[:, :], start=True, stop=True).then_inc(s["wc"], 1)

        @block.vector
        def _(e):
            e.memset(ri[:, 0], PADROW)
            e.memset(ri[:, 1], N)
            e.memset(hb[:, :, :], N).then_inc(s["clear"], 1)
            e.wait_ge(s["clear"], 1)
            e.memset(hb[0:1, 0, 0:1], -1).then_inc(s["clear"], 1)
            e.memset(g["bds"][:, :, :], 0.0).then_inc(s["wts"], 1)
            e.memset(g["vecs"][:, :], 0.0).then_inc(s["wts"], 1)
            e.wait_ge(s["wts"], 2)
            e.memset(V["eps"], LN_EPS)
            e.memset(V["a0"], 1.0).then_inc(s["wts"], 1)
            e.memset(MSG[:, :], 1.0)
            e.wait_ge(s["idx"], 16 * 10)
            e.tensor_copy(rf[:, 0:2], ri[:, :]).then_inc(s["rowsf"], 1)
            e.wait_ge(s["rowsf"], 1)
            e.tensor_copy(rf[:, 2, :, 1:P], rf[:, 1, :, 0:P - 1])
            e.tensor_copy(rf[:, 3, :, 0:P - 1], rf[:, 1, :, 1:P])
            e.tensor_copy(rf[:, 2, :, 0:1], hb[:, 0].unsqueeze(2))
            e.tensor_copy(rf[:, 3, :, P - 1:P], hb[:, 1].unsqueeze(2)).then_inc(s["shf"], 1)
            e.wait_ge(s["shf"], 1)
            e.tensor_tensor(fb[:, 0], rf[:, 1], rf[:, 2], ALU.is_equal).then_inc(s["flags"], 1)
            e.tensor_scalar(real[:, :, :], rf[:, 1], float(N), None, ALU.is_lt).then_inc(s["lastf"], 1)
            e.tensor_tensor(rf[:, 4], rf[:, 1], rf[:, 3], ALU.not_equal).then_inc(s["lastf"], 1)
            e.wait_ge(s["lastf"], 2)
            e.tensor_tensor(rf[:, 4], rf[:, 4], real[:, :, :], ALU.mult).then_inc(s["lastf"], 1)
            e.wait_ge(s["lastf"], 3)
            e.tensor_copy(fb[:, 1], rf[:, 4]).then_inc(s["lastb"], 1)
            for n, t in enumerate((g["srcE"], g["dstE"], g["lastE"])):
                e.wait_ge(s["tr"], n + 1)
                e.tensor_copy(t[:, :].rearrange("p (h r) -> p h r", h=2), pt[:, :, 0:HR]).then_inc(s["trc"], 1)
            e.wait_ge(s["trc"], 3)
            e.tensor_copy(g["srcI"][:, :], g["srcE"][:, :])
            e.tensor_copy(g["dstI"][:, :], g["dstE"][:, :])
            e.tensor_scalar(g["inI"][:, :], g["dstE"][:, :], float(N - 1), None, ALU.min)
            for n, (t, scale, add, far) in enumerate(((g["slotI"], TW // 2, F // 2, SLOTS + 8), (g["outI"], 1, 0, N + 8))):
                e.tensor_scalar(et[:, :], g["dstE"][:, :], float(scale), float(add - far), ALU.mult, ALU.add).then_inc(s["slot"], 1)
                e.wait_ge(s["slot"], 3 * n + 1)
                e.tensor_tensor(et[:, :], et[:, :], g["lastE"][:, :], ALU.mult).then_inc(s["slot"], 1)
                e.wait_ge(s["slot"], 3 * n + 2)
                e.tensor_scalar(t[:, :], et[:, :], float(far), None, ALU.add).then_inc(s["slot"], 1)
                e.wait_ge(s["slot"], 3 * n + 3)
            e.wait_ge(s["p3t"], 1)
            for h, p in ((0, pd), (1, pd2)):
                e.tensor_scalar(p3[:, :, h * HR:(h + 1) * HR], p[:, :, 0:HR], float(KS - 1), 0.0, ALU.mult, ALU.max).then_inc(s["p3"], 1)
            e.wait_ge(s["p3"], 2)
            for k in range(KS):
                after(e, s["bk"], k)
                e.tensor_scalar(bt[:, 0], p3, float(KS - 1), float(-k), ALU.min, ALU.add).then_inc(s["base"], 1)
                e.wait_ge(s["base"], 3 * k + 1)
                e.scalar_tensor_tensor(bt[:, 1], bt[:, 0], -1.0, bt[:, 0], ALU.mult, ALU.max).then_inc(s["base"], 1)
                e.wait_ge(s["base"], 3 * k + 2)
                e.tensor_scalar(bt[:, 0], bt[:, 1], -1.0, 1.0, ALU.mult, ALU.add).then_inc(s["base"], 1)
                e.wait_ge(s["base"], 3 * k + 3)
                e.tensor_scalar(g["basis"][:, :, :, k], bt[:, 0], 0.0, None, ALU.max).then_inc(s["bk"], 1)
            e.wait_ge(s["wT"], 1)
            e.tensor_copy(w1bT[:, :], pw[0:DH, 0, 0:DH]).then_inc(s["wTc"], 1)
            e.wait_ge(s["wc"], 1)
            e.tensor_copy(wc[:, :], pw[0:DH, 1, 0:DI]).then_inc(s["wcc"], 1)
            e.wait_ge(s["wc"], 2)
            e.tensor_copy(bcv[:, :], pw[0:DI, 0, 0:1]).then_inc(s["wcc"], 1)
            sg, mu = (g["vecs"][:, VECS.index(n):VECS.index(n) + 3] for n in ("sg0", "mu0"))
            e.wait_ge(s["vec"], 16 * len(placed))
            e.tensor_tensor(sg, sg, sg, ALU.mult).then_inc(s["sg"], 1)
            e.wait_ge(s["sg"], 1)
            e.tensor_scalar(sg, sg, 1e-14, 2.0, ALU.add, ALU.mult).then_inc(s["sg"], 1)
            e.wait_ge(s["sg"], 2)
            e.reciprocal(sg, sg).then_inc(s["sg"], 1)
            e.wait_ge(s["sg"], 4)
            e.scalar_tensor_tensor(mu, mu, -1.0, sg, ALU.mult, ALU.mult)
            e.wait_ge(s["bcast"], 16 * 8)
            e.tensor_tensor_scan(first[:, :], same[:, :], same[:, :], 1.0, ALU.mult, ALU.min)


def degrees(nc, g):
    a, sb, psum, MSG, ident = g["a"], g["sb"], g["psum"], g["MSG"], g["ident"]
    scan_phase(nc, g, "cnt", [MSG])
    with ExitStack() as c:
        s = sems(c, nc, "deg", "fix eidx flat rows tr cnt pairs sd rd stg0 stg1 sent0 sent1")
        cr = sb(c, "cr", [HR, 2, P])
        pt = psum(c, "pt", [P, 2, P])
        sd, eidx = sb(c, "sdc", [P, ROWS]), sb(c, "eidx", [P, ROWS])
        pairs = sb(c, "pairs", [P, BLOCKS, Q, 2])
        st, pv = sb(c, "st", [P, 2, Q], I32), sb(c, "pv", [P, 2, Q, 2])
        block = c.enter_context(nc.Block())

        @block.sync
        def _(e):
            e.dma_start(eidx[:, :], a["eidx"]).then_inc(s["eidx"], 16)
            e.wait_ge(s["fix"], 1)
            for q in range(Q):
                e.dma_start(g["cntflat"][q * EC:(q + 1) * EC].rearrange("(o n) -> o n", o=1), MSG[32 * q:32 * q + 1, :]).then_inc(s["flat"], 16)
            e.wait_ge(s["flat"], 16 * Q)
            for h in range(2):
                e.dma_start(cr[:, h, :], g["cntflat"][h * HR * P:(h + 1) * HR * P].rearrange("(r c) -> r c", c=P)).then_inc(s["rows"], 16)

        @block.scalar
        def _(e):
            e.wait_ge(s["cnt"], 1)
            e.activation(sd[:, :], g["cntE"][:, :], ACT.Sqrt).then_inc(s["sd"], 1)

        @block.tensor
        def _(e):
            e.wait_ge(s["rows"], 32)
            for h in range(2):
                mm = e.transpose(pt[:, h, 0:HR], cr[:, h, :], ident[0:HR, 0:HR])
            mm.then_inc(s["tr"], 1)

        @block.vector
        def _(e):
            e.scalar_tensor_tensor(MSG[:, :], g["first"][:, :], g["carry"][:, 0:1], MSG[:, :], ALU.mult, ALU.add).then_inc(s["fix"], 1)
            e.wait_ge(s["tr"], 1)
            e.tensor_scalar(g["cntE"][:, :].rearrange("p (h r) -> p h r", h=2), pt[:, :, 0:HR], 1.0, None, ALU.max).then_inc(s["cnt"], 1)
            e.wait_ge(s["cnt"], 1)
            e.reciprocal(g["rcE"][:, :], g["cntE"][:, :])
            e.wait_ge(s["eidx"], 16)
            byblock = pairs[:, :, :, :].rearrange("p b q w -> p w q b")
            e.tensor_copy(byblock[:, 0], eidx[:, :].rearrange("p (q b) -> p q b", q=Q)).then_inc(s["pairs"], 1)
            e.tensor_copy(byblock[:, 1], g["cntE"][:, :].rearrange("p (q b) -> p q b", q=Q)).then_inc(s["pairs"], 1)
            e.wait_ge(s["sd"], 1)
            e.reciprocal(g["dinvD"][:, :], sd[:, :])

        @block.gpsimd
        def _(e):
            slots = g["table"].rearrange("n (h w) -> (n h) w", w=2)
            e.wait_ge(s["pairs"], 2)

            def step(i, k, j):
                after(e, s[f"sent{k}"], 64 * (j - 1))
                e.tensor_copy(pv[:, k], pairs[:, bass.ds(i, 1)].rearrange("p b q w -> p (b q) w")).then_inc(s[f"stg{k}"], 1)
                e.tensor_copy(st[:, k, :], tiles(g["slotI"], i)).then_inc(s[f"stg{k}"], 1)
                e.wait_ge(s[f"stg{k}"], 1)
                after(e, s[f"stg{k}"], 2 * j)
                for q in range(Q):
                    e.indirect_dma_start(slots, bass.IndirectOffsetOnAxis(ap=st[:, k, q:q + 1], axis=0), pv[:, k, q, :], None,
                                         bounds_check=SLOTS - 1, oob_is_err=False).then_inc(s[f"sent{k}"], 16)
            each_block(e, step)
            for k in range(2):
                e.wait_ge(s[f"sent{k}"], 64 * (BLOCKS // 2))


def layer0(nc, g):
    a, V, BD, sb, psum, ident = g["a"], g["V"], g["BD"], g["sb"], g["psum"], g["ident"]
    with ExitStack() as c:
        s = sems(c, nc, "l0", "const " + GATHER + " sts0 sts1 sent row0 row1 att0 att1 " + ln_sems("e")
                 + " xt gau g2 g3 ex m mw hi r1 mid lo sc eq cb ld0 ld ld2 ld3 addi sum av pad zi")
        xd = psum(c, "xd", [P, P])
        cen, var, pw = psum(c, "cen", [P, P]), psum(c, "var", [P, P]), psum(c, "pw", [P, P])
        pe_, pc = psum(c, "pe", [P, Q, 3 * F]), psum(c, "pc", [P, Q])
        before = sb(c, "before", [P, P])
        gx, st, ss = sb(c, "gx", [P, 2, Q, F]), sb(c, "st", [P, 2, Q], I32), sb(c, "ss", [P, 2, Q], I32)
        x, sq, sd, h, m = (sb(c, n, [P, P]) for n in ("x", "sq", "sd", "h", "m"))
        att, gq, gs = sb(c, "att", [P, 2, P, 3]), sb(c, "gq", [P, 3, P]), sb(c, "gs", [P, P])
        row, S = sb(c, "row", [P, 2, Q * P]), sb(c, "S", [P, Q, Q * P], BF16)
        one, rest = sb(c, "one", [P, 1], BF16), sb(c, "rest", [P, 1, Q, F])
        mw3 = sb(c, "mw3", [P, Q, 3, F], BF16)
        junk, sc, cb, ld = sb(c, "junk", [P, Q, P]), sb(c, "sc", [P, Q]), sb(c, "cb", [P, 2, Q]), sb(c, "ld", [P, Q])
        av, ai = sb(c, "av", [P, 2, Q, TW]), sb(c, "ai", [P, 2, Q], I32)
        zi = sb(c, "zi", [P, Q], I32)
        t = {"x": x[:, :], "cen": cen[:, :], "sq": sq[:, :], "var": var[:, :], "sd": sd[:, :], "rs": sd[:, :], "h": h[:, :]}
        block = c.enter_context(nc.Block())

        @block.sync
        def _(e):
            e.dma_start(before[:, :], a["before"]).then_inc(s["const"], 16)

            def load(i, k, j):
                after(e, s["gau"], i - 1)
                after(e, s["lo"], i - 1)
                for q in range(Q):
                    e.dma_start(att[32 * q:32 * q + 32, k, :, :].rearrange("p c d -> p (c d)"),
                                g["attr3"][bass.ds(i * P + q * EC, P), :].rearrange("c d -> (c d)").partition_broadcast(32)).then_inc(s[f"att{k}"], 16)
                for q in range(Q):
                    e.dma_start(row[:, k, q * P:(q + 1) * P], g["srcflat"][bass.ds(i * P + q * EC, P)].partition_broadcast(P)).then_inc(s[f"row{k}"], 16)
            each_block(e, load)

        @block.gpsimd
        def _(e):
            lag = 4

            def fetch(i, k, j):
                after(e, s["xt"], i - 1)
                stage_indices(e, s, st, k, j, g["inI"], i)
                for q in range(Q):
                    e.indirect_dma_start(gx[:, k, q, :], None, a["x"], bass.IndirectOffsetOnAxis(ap=st[:, k, q:q + 1], axis=0)).then_inc(s[f"got{k}"], 16)

            def add(i, k, r):
                after(e, s["sent"], 64 * i)
                after(e, s["av"], i + 1)
                after(e, s["addi"], i + 1)
                e.tensor_tensor(ss[:, k, :], ai[:, k, :], zi[:, :], ALU.add).then_inc(s[f"sts{k}"], 1)
                e.wait_ge(s[f"sts{k}"], 1)
                after(e, s[f"sts{k}"], r)
                for q in range(Q):
                    e.indirect_dma_start(g["table"], bass.IndirectOffsetOnAxis(ap=ss[:, k, q:q + 1], axis=0), av[:, k, q, :], None,
                                         compute_op=ALU.add).then_inc(s["sent"], 16)

            e.memset(zi[:, :], 0).then_inc(s["zi"], 1)
            for k in range(2):
                e.memset(ss[:, k, :], 0).then_inc(s[f"sts{k}"], lag // 2)
            e.wait_ge(s["zi"], 1)
            for n in range(2 * lag):
                if n >= lag:
                    add(n - lag, n % 2, n // 2 + 1)
                fetch(n, n % 2, n // 2 + 1)
            with e.Fori(lag + 1, BLOCKS // 2 + 1) as r:
                for k in range(2):
                    add(2 * r - 2 - lag + k, k, r)
                    fetch(2 * r - 2 + k, k, r)
            for n in range(BLOCKS, BLOCKS + lag):
                add(n - lag, n % 2, n // 2 + 1)
            e.wait_ge(s["sent"], 64 * BLOCKS)

        @block.tensor
        def _(e):
            def enter(i, k, j):
                after(e, s[f"got{k}"], 64 * j)
                after(e, s["xe"], i)
                e.transpose(xd[:, :], gx[:, k, :, :], ident).then_inc(s["xt"], 1)

            def weights(i, k, j):
                after(e, s["m"], i + 1)
                after(e, s["lo"], i)
                e.matmul(pw[:, :], m[:, :], BD["W0"], start=True, stop=True).then_inc(s["mw"], 1)

            def sums(i, k, j):
                after(e, s["lo"], i + 1)
                after(e, s["eq"], Q * (i + 1))
                after(e, s["av"], i)
                after(e, s["cb"], Q * (i + 1))
                for r in range(Q):
                    for q in range(Q):
                        e.matmul(pe_[:, r, :], S[:, q, r * P:(r + 1) * P], mw3[:, q].rearrange("p w f -> p (w f)"), start=(q == 0), stop=(q == Q - 1))
                for r in range(1, Q):
                    for q in range(r):
                        mm = e.matmul(pc[:, r:r + 1], S[:, q, r * P:(r + 1) * P], one[:, :], start=(q == 0), stop=(q == r - 1))
                mm.then_inc(s["sum"], 1)
            staged(e, (1, lambda i, k, j: ln_centre(e, s, "e", t, i, g)),
                   (2, weights),
                   (0, enter),
                   (1, lambda i, k, j: ln_mean(e, s, "e", t, i, g)),
                   (2, sums))

        @block.scalar
        def _(e):
            def enter(i, k, j):
                after(e, s["xt"], i + 1)
                after(e, s["cene"], i)
                e.copy(x[:, :], xd[:, :]).then_inc(s["xe"], 1)

            def squares(i, k, j):
                after(e, s[f"att{k}"], 64 * j)
                after(e, s["g3"], i)
                after(e, s["ex"], i)
                for d in range(3):
                    mm = e.activation(gq[:, d, :], att[:, k, :, d], ACT.Square, bias=V[f"mu{d}"], scale=V[f"sg{d}"])
                mm.then_inc(s["gau"], 1)

            def gaussian(i, k, j):
                after(e, s["g3"], i + 1)
                after(e, s["m"], i)
                e.activation(gs[:, :], gq[:, 0, :], ACT.Exp, scale=-1.0).then_inc(s["ex"], 1)

            def weights(i, k, j):
                after(e, s["mw"], i + 1)
                after(e, s["sum"], i)
                e.copy(mw3[:, :, 0, :], pw[:, :].rearrange("p (q f) -> p q f", q=Q)).then_inc(s["hi"], 1)

            def middle(i, k, j):
                after(e, s["r1"], i + 1)
                e.copy(mw3[:, :, 1, :], rest[:, 0]).then_inc(s["mid"], 1)

            staged(e, (1, lambda i, k, j: ln_square(e, s, "e", t, i)),
                   (2, weights),
                   (0, enter),
                   (2, middle),
                   (1, gaussian),
                   (1, lambda i, k, j: ln_root(e, s, "e", t, i, g)),
                   (0, squares))

        @block.vector
        def _(e):
            e.memset(av[:, :, :, :], 0.0).then_inc(s["pad"], 1)
            e.memset(cb[:, 1, :], 0.0).then_inc(s["pad"], 1)
            e.memset(one[:, :], 1.0).then_inc(s["pad"], 1)
            e.wait_ge(s["const"], 16)
            e.wait_ge(s["pad"], 3)

            def exponent(i, k, j):
                after(e, s["gau"], i + 1)
                after(e, s["ex"], i)
                e.tensor_tensor(gq[:, 1, :], gq[:, 0, :], gq[:, 1, :], ALU.add).then_inc(s["g2"], 1)
                after(e, s["g2"], i + 1)
                e.tensor_tensor(gq[:, 0, :], gq[:, 1, :], gq[:, 2, :], ALU.add).then_inc(s["g3"], 1)

            def messages(i, k, j):
                ln_vector(e, s, "e", t, i)
                after(e, s["ex"], i + 1)
                after(e, s["he"], i + 1)
                after(e, s["mw"], i)
                e.tensor_tensor(m[:, :], h[:, :], gs[:, :], ALU.mult).then_inc(s["m"], 1)

            def shared(i, k, j):
                after(e, s["ld3"], i)
                copy(e, sc[:, :], tiles(g["srcE"], i)).then_inc(s["sc"], 1)
                after(e, s[f"row{k}"], 64 * j)
                after(e, s["sc"], i + 1)
                after(e, s["sum"], i)
                for q in range(Q):
                    e.tensor_scalar(S[:, q, :], row[:, k, :], sc[:, q:q + 1], None, ALU.is_equal).then_inc(s["eq"], 1)

                for q in range(Q):
                    if q == 0:
                        after(e, s["ld"], i)
                    after(e, s["eq"], Q * i + q + 1)
                    e.scalar_tensor_tensor(junk[:, q, :], before[:, :], 1.0, S[:, q, q * P:(q + 1) * P], ALU.mult, ALU.mult,
                                           accum_out=cb[:, 0, q:q + 1]).then_inc(s["cb"], 1)

            def split(i, k, j):
                after(e, s["hi"], i + 1)
                e.tensor_tensor(rest[:, 0], pw[:, :].rearrange("p (q f) -> p q f", q=Q), mw3[:, :, 0, :], ALU.subtract).then_inc(s["r1"], 1)

            def last_part(i, k, j):
                after(e, s["mid"], i + 1)
                e.tensor_tensor(mw3[:, :, 2, :], rest[:, 0], mw3[:, :, 1, :], ALU.subtract).then_inc(s["lo"], 1)

            def sums(i, k, j):
                after(e, s["sum"], i + 1)
                after(e, s["sent"], 64 * (i - 1))
                e.tensor_reduce(av[:, k, :, 0:F], pe_[:, :, :].rearrange("p q (w f) -> p q f w", w=3), AX.X, ALU.add).then_inc(s["av"], 1)
                e.tensor_tensor(cb[:, 1, 1:Q], pc[:, 1:Q], cb[:, 0, 1:Q], ALU.add).then_inc(s["ld0"], 1)
                e.tensor_copy(cb[:, 1, 0:1], cb[:, 0, 0:1]).then_inc(s["ld0"], 1)
                e.tensor_tensor(sc[:, :], sc[:, :], g["trashE"][:, :], ALU.subtract).then_inc(s["ld2"], 1)
                after(e, s["ld0"], 2 * (i + 1))
                e.tensor_scalar(ld[:, :], cb[:, 1, :], 0.5, None, ALU.is_lt).then_inc(s["ld"], 1)
                after(e, s["ld"], i + 1)
                after(e, s["ld2"], i + 1)
                e.tensor_tensor(ld[:, :], sc[:, :], ld[:, :], ALU.mult).then_inc(s["ld3"], 1)
                after(e, s["ld3"], i + 1)
                e.tensor_tensor(ai[:, k, :], ld[:, :], g["trashE"][:, :], ALU.add).then_inc(s["addi"], 1)
            staged(e, (3, sums), (2, split), (2, shared), (2, last_part), (1, exponent), (1, messages))


def place(nc, g):
    V, sb, psum, ident, HS, HDW = g["V"], g["sb"], g["psum"], g["ident"], g["HS"], g["HDW"]
    with ExitStack() as c:
        s = sems(c, nc, "pl", GATHER + " tb0 tb1 xs0 xs1 xo0 xo1 yo0 yo1 et zt tc gc ptr hc " + ln_sems("e") + " " + ln_sems("z"))
        pxe, pxz = psum(c, "pxe", [P, 2, P]), psum(c, "pxz", [P, NB])
        cene, vare = psum(c, "cene", [P, 2, BANK]), psum(c, "vare", [P, 2 * P])
        cenz, varz = psum(c, "cenz", [P, 2, BANK]), psum(c, "varz", [P, NB])
        gx, st = sb(c, "gx", [P, 2, 2, Q, TW]), sb(c, "st", [P, 2, 2, Q], I32)
        gc = sb(c, "gc", [P, 2, Q, F])
        tb, tc = sb(c, "tb", [NP, 2, Q, 4, TW]), sb(c, "tc", [NP, 4, Q, F])
        xe, sqe, sde, he = sb(c, "xe", [P, 2, 2 * P]), sb(c, "sqe", [P, 2 * P]), sb(c, "sde", [P, 2, 2 * P]), sb(c, "he", [P, 2 * P])
        xz, sqz, sdz, hz = sb(c, "xz", [P, 2, NB]), sb(c, "sqz", [P, NB]), sb(c, "sdz", [P, 2, NB]), sb(c, "hz", [P, 2, NB])
        tab = g["table"][0:N, :].rearrange("(q b p n) w -> b p q (n w)", q=Q, b=BLOCKS, p=NP)

        def te(k):
            return {"x": xe[:, k], "cen": cene[:, k, 0:2 * P], "sq": sqe[:, :], "var": vare[:, :], "sd": sde[:, k], "rs": sde[:, k], "h": he[:, :]}

        def tz(k):
            return {"x": xz[:, k], "cen": cenz[:, k, 0:NB], "sq": sqz[:, :], "var": varz[:, :], "sd": sdz[:, k], "rs": sdz[:, k], "h": hz[:, k]}
        block = c.enter_context(nc.Block())

        @block.gpsimd
        def _(e):
            def step(i, k, j):
                after(e, s["ptr"], i - 1)
                e.tensor_copy(st[:, k, 0, :], tiles(g["srcI"], i)).then_inc(s[f"stg{k}"], 1)
                e.tensor_copy(st[:, k, 1, :], tiles(g["dstI"], i)).then_inc(s[f"stg{k}"], 1)
                e.wait_ge(s[f"stg{k}"], 1)
                after(e, s[f"stg{k}"], 2 * j)
                for w in range(2):
                    for q in range(Q):
                        e.indirect_dma_start(gx[:, k, w, q, :], None, g["table"],
                                             bass.IndirectOffsetOnAxis(ap=st[:, k, w, q:q + 1], axis=0)).then_inc(s[f"got{k}"], 16)
            each_block(e, step)

        @block.sync
        def _(e):
            def load(i, k, j):
                after(e, s["tc"], i - 1)
                e.dma_start(tb[:, k].rearrange("p q n w -> p q (n w)"), tab[bass.ds(i, 1)].rearrange("b p q w -> (b p) q w")).then_inc(s[f"tb{k}"], 16)

            def store(i, k, j):
                after(e, s["xe"], i + 1)
                e.dma_start(g["xsd"][bass.ds(i, 1)].rearrange("b p c -> (b p) c"), xe[:, k]).then_inc(s[f"xs{k}"], 16)
                after(e, s["xz"], i + 1)
                e.dma_start(g["x0f"][bass.ds(i, 1)].rearrange("b p c -> (b p) c"), xz[:, k]).then_inc(s[f"xo{k}"], 16)
                after(e, s["hz"], i + 1)
                e.dma_start(g["yf"][bass.ds(i, 1)].rearrange("b p c -> (b p) c"), hz[:, k]).then_inc(s[f"yo{k}"], 16)
            staged(e, (0, load), (2, store))
            for k in range(2):
                for n in ("xs", "xo", "yo"):
                    e.wait_ge(s[f"{n}{k}"], 16 * (BLOCKS // 2))

        @block.tensor
        def _(e):
            def dense(i, k, j):
                after(e, s["tc"], i + 1)
                after(e, s["xz"], i)
                for n in range(4):
                    mm = e.transpose(pxz[:, n * NP:(n + 1) * NP], tc[:, n, :, :], ident[0:NP, 0:NP])
                mm.then_inc(s["zt"], 1)

            def edges(i, k, j):
                after(e, s["gc"], i + 1)
                after(e, s["xe"], i)
                for w in range(2):
                    mm = e.transpose(pxe[:, w, :], gc[:, w, :, :], ident)
                mm.then_inc(s["et"], 1)
            staged(e, (1, lambda i, k, j: ln_centre(e, s, "e", te(k), i, g, 2)),
                   (1, lambda i, k, j: ln_centre(e, s, "z", tz(k), i, g, 2)),
                   (0, dense),
                   (1, lambda i, k, j: ln_mean(e, s, "e", te(k), i, g)),
                   (0, edges),
                   (1, lambda i, k, j: ln_mean(e, s, "z", tz(k), i, g)))

        @block.scalar
        def _(e):
            def rows(i, k, j):
                after(e, s[f"tb{k}"], 16 * j)
                after(e, s["zt"], i)
                e.copy(tc[:, :, :, :], tb[:, k, :, :, 0:F].rearrange("p q n f -> p n q f")).then_inc(s["tc"], 1)

            def dense(i, k, j):
                after(e, s["zt"], i + 1)
                after(e, s[f"xo{k}"], 16 * (j - 1))
                after(e, s["cenz"], i - 1)
                e.activation(xz[:, k], pxz[:, :], ACT.Identity, bias=V["b0"]).then_inc(s["xz"], 1)

            def edges(i, k, j):
                after(e, s["et"], i + 1)
                after(e, s[f"xs{k}"], 16 * (j - 1))
                e.activation(xe[:, k].rearrange("p (w c) -> p w c", w=2), pxe[:, :, :], ACT.Identity, bias=V["b0"]).then_inc(s["xe"], 1)
            staged(e, (0, rows),
                   (1, lambda i, k, j: ln_square(e, s, "e", te(k), i)),
                   (1, lambda i, k, j: ln_square(e, s, "z", tz(k), i)),
                   (0, dense),
                   (1, lambda i, k, j: ln_root(e, s, "e", te(k), i, g)),
                   (0, edges),
                   (1, lambda i, k, j: ln_root(e, s, "z", tz(k), i, g)))

        @block.vector
        def _(e):
            def take(i, k, j):
                after(e, s[f"got{k}"], 128 * j)
                after(e, s["et"], i)
                e.tensor_copy(gc[:, :, :, :], gx[:, k, :, :, 0:F]).then_inc(s["gc"], 1)

            def pointers(i, k, j):
                copy(e, tiles(g["ptrI"], i), gx[:, k, 0, :, F])
                after(e, s["gc"], i + 1)
                copy(e, tiles(g["cntS"], i), gx[:, k, 0, :, F + 1]).then_inc(s["ptr"], 1)

            def dense(i, k, j):
                after(e, s[f"yo{k}"], 16 * (j - 1))
                ln_vector(e, s, "z", tz(k), i)

            def edges(i, k, j):
                after(e, s["hc"], i)
                ln_vector(e, s, "e", te(k), i)

            def keep(i, k, j):
                after(e, s["he"], i + 1)
                copy(e, at(HS, i), he[:, 0:P])
                copy(e, HDW[:, bass.ds(i, 1)].rearrange("p b w c -> p (b w) c"), bc_first(he[:, P:2 * P], 2)).then_inc(s["hc"], 1)
            staged(e, (0, take), (0, pointers), (1, edges), (1, keep), (1, dense))

    with ExitStack() as c:
        s = sems(c, nc, "ds", "m z sd r")
        z = sb(c, "z", [P, 2, ROWS])
        block = c.enter_context(nc.Block())

        @block.vector
        def _(e):
            e.tensor_scalar(z[:, 0], g["cntS"][:, :], 1.0, None, ALU.max).then_inc(s["m"], 1)
            e.tensor_scalar(z[:, 1], g["cntS"][:, :], 0.5, None, ALU.is_gt).then_inc(s["z"], 1)
            e.wait_ge(s["sd"], 1)
            e.reciprocal(z[:, 0], z[:, 0]).then_inc(s["r"], 1)
            e.wait_ge(s["z"], 1)
            e.wait_ge(s["r"], 1)
            e.tensor_tensor(g["dinvS"][:, :], z[:, 0], z[:, 1], ALU.mult)

        @block.scalar
        def _(e):
            e.wait_ge(s["m"], 1)
            e.activation(z[:, 0], z[:, 0], ACT.Sqrt).then_inc(s["sd"], 1)


def spline(nc, g, l):
    a, V, BD, sb, psum, ident = g["a"], g["V"], g["BD"], g["sb"], g["psum"], g["ident"]
    HS, MSG, basis = g["HS"], g["MSG"], g["basis"]
    with ExitStack() as c:
        s = sems(c, nc, f"sp{l}", "w " + GATHER + " yi0 yi1 yo0 yo1 ex ev lk ey hs hsd t1 t4 cf tt ttc y prod red m mw "
                 "zh zr zv zl zy st ag")
        px, pt = psum(c, "px", [P, P]), psum(c, "ptm", [P, P])
        ptt = psum(c, "ptt", [P, Q, P])
        py = [psum(c, f"py{n}", [P, BANK]) for n in range(3)]
        bank = (0, 1, 2, 1)
        pm, pz = psum(c, "pm", [P, P]), psum(c, "pz", [P, NB])
        Wl = sb(c, "Wl", [P, 16, F])
        gx, st = sb(c, "gx", [P, 2, Q, F]), sb(c, "st", [P, 2, Q], I32)
        v, lk, hs = sb(c, "v", [P, P]), sb(c, "lk", [P, P]), sb(c, "hs", [P, P])
        T4, cf = sb(c, "T4", [P, Q, KS, F]), sb(c, "cf", [P, 2, Q, KS, KS])
        TT, prod, msg = sb(c, "TT", [P, 2, Q, P]), sb(c, "prod", [P, 2, 16, F]), sb(c, "msg", [P, Q, F])
        yz, zv = sb(c, "yz", [P, 2, NB]), sb(c, "zv", [P, 2, NB])
        A, C = V[f"a{l - 1}"], V[f"c{l - 1}"]
        block = c.enter_context(nc.Block())

        @block.gpsimd
        def _(e):
            def sources(i, k, j):
                gather(e, s, st, k, j, i, g["ptrI"], g["runs"], gx, s["ex"])

            def dense(i, k, j):
                after(e, s["zl"] if l < 3 else s["zv"], i + 1)
                e.tensor_tensor(zv[:, k], zv[:, k], yz[:, k], ALU.add).then_inc(s["zy"], 1)
            staged(e, *([(0, sources)] if l > 1 else []), (1, dense))

        @block.sync
        def _(e):
            Ws = a[f"W{l}"]
            for k2 in range(KS):
                e.dma_start(Wl[32 * k2:32 * k2 + 32], Ws[16 * k2:16 * k2 + 16].rearrange("k c o -> c k o")).then_inc(s["w"], 16)

            def load(i, k, j):
                after(e, s["zy"], i - 1)
                e.dma_start(yz[:, k], g["yf"][bass.ds(i + (l - 1) * BLOCKS, 1)].rearrange("b p c -> (b p) c")).then_inc(s[f"yi{k}"], 16)

            def store(i, k, j):
                after(e, s["zy"], i + 1)
                e.dma_start(g["yf"][bass.ds(i + l * BLOCKS, 1)].rearrange("b p c -> (b p) c"), zv[:, k]).then_inc(s[f"yo{k}"], 16)
            staged(e, (0, load), (1, store))
            for k in range(2):
                e.wait_ge(s[f"yo{k}"], 16 * (BLOCKS // 2))

        @block.tensor
        def _(e):
            e.wait_ge(s["w"], 64)

            def dense(i, k, j):
                after(e, s["zh"], i + 1)
                after(e, s["zv"], i)
                e.matmul(pz[:, :], BD[f"R{l}"], yz[:, k], start=True, stop=True).then_inc(s["zr"], 1)

            def sources(i, k, j):
                after(e, s[f"got{k}"], 64 * j)
                after(e, s["ev"], i)
                e.matmul(px[:, :], BD[f"R{l - 1}"], at(HS, i), start=True, stop=False)
                e.matmul(px[:, :], gx[:, k, :, :], ident, start=False, stop=True).then_inc(s["ex"], 1)

            def rows(i, k, j):
                after(e, s["hs"], i + 1)
                after(e, s["t4"], i)
                e.transpose(pt[:, :], hs[:, :], ident).then_inc(s["t1"], 1)

            def columns(i, k, j):
                after(e, s["t4"], i + 1)
                after(e, s["ttc"], i)
                for q in range(Q):
                    mm = e.transpose(ptt[:, q, :], T4[:, q].rearrange("p k f -> p (k f)"), ident)
                mm.then_inc(s["tt"], 1)

            def product(q):
                def step(i, k, j):
                    if q == 0:
                        after(e, s["ttc"], i + 1)
                    after(e, s["prod"], Q * i + (-3, 0, -1, 2)[q])
                    e.matmul(py[bank[q]][:, :], TT[:, k, q, :], Wl[:, :, :], start=True, stop=True).then_inc(s["y"], 1)
                return step

            def messages(i, k, j):
                after(e, s["red"], Q * (i + 1))
                after(e, s["mw"], i)
                e.transpose(pm[:, :], msg[:, :, :], ident).then_inc(s["m"], 1)
            tile = [(1, product(q)) for q in range(Q)]
            staged(e, tile[0], (2, messages), *([(0, sources)] if l > 1 else []), tile[1], tile[2], (0, rows), tile[3], (0, columns),
                   (0, dense))

        @block.scalar
        def _(e):
            def norm(i, k, j):
                after(e, s[f"yi{k}"], 16 * j)
                e.activation(yz[:, k], yz[:, k], ACT.Identity, bias=C, scale=A).then_inc(s["zh"], 1)

            def layer(i, k, j):
                after(e, s["ex"], i + 1)
                after(e, s["ey"], i)
                e.activation(v[:, :], px[:, :], ACT.Identity, bias=V[f"b{l - 1}"]).then_inc(s["ev"], 1)

            def states(i, k, j):
                after(e, s["ey"], i + 1)
                after(e, s["t1"], i)
                after(e, s["hsd"], i)
                e.activation(hs[:, :], lk[:, :], ACT.Identity, bias=C, scale=A).then_inc(s["hs"], 1)

            def columns(i, k, j):
                after(e, s["tt"], i + 1)
                after(e, s["y"], Q * (i - 1))
                e.copy(TT[:, k], ptt[:, :, :]).then_inc(s["ttc"], 1)

            def dense(i, k, j):
                after(e, s["zr"], i + 1)
                after(e, s["st"], i - 1)
                after(e, s[f"yo{k}"], 16 * (j - 1))
                e.activation(zv[:, k], pz[:, :], ACT.Identity, bias=V[f"b{l}"]).then_inc(s["zv"], 1)
            staged(e, *([(1, layer), (1, states)] if l > 1 else []), (1, columns), (0, norm), (1, dense))

        @block.vector
        def _(e):
            def layer(i, k, j):
                after(e, s["ev"], i + 1)
                after(e, s["hs"], i)
                e.scalar_tensor_tensor(lk[:, :], v[:, :], SLOPE, v[:, :], ALU.mult, ALU.max).then_inc(s["lk"], 1)

            def residual(i, k, j):
                after(e, s["lk"], i + 1)
                e.tensor_tensor(lk[:, :], lk[:, :], at(HS, i), ALU.add).then_inc(s["ey"], 1)

            def states(i, k, j):
                if l > 1:
                    after(e, s["hs"], i + 1)
                    copy(e, at(HS, i), hs[:, :]).then_inc(s["hsd"], 1)
                else:
                    after(e, s["t1"], i)
                    copy(e, hs[:, :], at(HS, i)).then_inc(s["hs"], 1)

            def factors(i, k, j):
                b0, b1 = (basis[:, d].rearrange("p (q b) k -> p q b k", q=Q)[:, :, bass.ds(i, 1)].rearrange("p q b k -> p (q b) k") for d in range(2))
                after(e, s["prod"], Q * (i - 1))
                e.tensor_tensor(cf[:, k], bc(b1, KS), bc_mid(b0, KS), ALU.mult).then_inc(s["cf"], 1)

            def spread(i, k, j):
                b2 = basis[:, 2].rearrange("p (q b) k -> p q b k", q=Q)[:, :, bass.ds(i, 1)].rearrange("p q b k -> p (q b) k")
                after(e, s["t1"], i + 1)
                after(e, s["tt"], i)
                e.tensor_tensor(T4[:, :, :, :], bc_mid(pt[:, :].rearrange("p (q f) -> p q f", q=Q), KS), bc(b2, F), ALU.mult).then_inc(s["t4"], 1)

            def leaky(i, k, j):
                after(e, s["zv"], i + 1)
                e.scalar_tensor_tensor(zv[:, k], zv[:, k], SLOPE, zv[:, k], ALU.mult, ALU.max).then_inc(s["zl"], 1)

            def statistics(i, k, j):
                after(e, s["zy"], i + 1)
                e.bn_stats(g["stats"][:, bass.ds(i, 1), :].rearrange("p b c -> p (b c)"), zv[:, k]).then_inc(s["st"], 1)

            def product(q):
                def step(i, k, j):
                    n = Q * i + q + 1
                    if q == 0:
                        after(e, s["cf"], i + 1)
                    after(e, s["y"], n)
                    after(e, s["red"], n - 2)
                    e.tensor_tensor(prod[:, q % 2], py[bank[q]][:, :].rearrange("p (k f) -> p k f", f=F),
                                    bc(cf[:, k, q].rearrange("p a b -> p (a b)"), F), ALU.mult).then_inc(s["prod"], 1)
                return step

            def reduction(q):
                def step(i, k, j):
                    if q == 0:
                        after(e, s["m"], i)
                    after(e, s["prod"], Q * i + q + 1)
                    e.tensor_reduce(msg[:, q, :], prod[:, q % 2].rearrange("p k f -> p f k"), AX.X, ALU.add).then_inc(s["red"], 1)
                return step

            def write(i, k, j):
                after(e, s["m"], i + 1)
                copy(e, at(MSG, i), pm[:, :]).then_inc(s["mw"], 1)
            by, total = [(1, product(q)) for q in range(Q)], [(1, reduction(q)) for q in range(Q)]
            if l > 1:
                staged(e, *([(1, leaky)] if l < 3 else []), by[0], total[0], (0, layer), by[1], (0, residual), total[1], by[2], (0, states),
                       (2, write), (0, spread), total[2], (0, factors), (1, statistics), by[3], total[3])
            else:
                staged(e, (1, leaky), (0, states), by[0], total[0], by[1], (2, write), total[1],
                       by[2], (0, spread), total[2], (0, factors), (1, statistics), by[3], total[3])
            e.wait_ge(s["st"], BLOCKS)
            e.bn_aggr(g["agg"][:, 0:2], g["stats"][:, :, :].rearrange("p b (t c) -> p (b t) c", c=3)).then_inc(s["ag"], 1)


def run_end(nc, g, l):
    V, BD, sb, psum, ident = g["V"], g["BD"], g["sb"], g["psum"], g["ident"]
    HDW, MSG, agg = g["HDW"], g["MSG"], g["agg"]
    with ExitStack() as c:
        s = sems(c, nc, f"re{l}", "mt t ag r0 r1 x v lk y ym st norm p q f n")
        pt, px, pg = psum(c, "pt", [P, 2, BANK]), psum(c, "px", [P, 2, BANK]), psum(c, "pg", [P, 2])
        mt, ag = sb(c, "mt", [P, 2, P]), sb(c, "ag", [P, 2, Q, F])
        v, ym = sb(c, "v", [P, 2, 2, P]), sb(c, "ym", [P, 2, 2, P])
        stats, sums = sb(c, "st2", [P, 2, BLOCKS, 6]), sb(c, "sums", [P, 2, 2])
        f = sb(c, "f", [P, 8])
        block = c.enter_context(nc.Block())

        def hdw(i):
            return HDW[:, bass.ds(i, 1)].rearrange("p b w c -> p (b w) c")

        @block.sync
        def _(e):
            def store(i, k, j):
                after(e, s["ag"], i + 1)
                e.dma_start(g["runs"][0:EP, :].rearrange("(q b p) f -> b p q f", q=Q, b=BLOCKS)[bass.ds(i, 1)].rearrange("b p q f -> (b p) q f"),
                            ag[:, k]).then_inc(s[f"r{k}"], 16)
            each_block(e, store)
            for k in range(2):
                e.wait_ge(s[f"r{k}"], 16 * (BLOCKS // 2))

        @block.tensor
        def _(e):
            def rows(i, k, j):
                after(e, s["mt"], i + 1)
                after(e, s["ag"], i - 1)
                e.transpose(pt[:, k, 0:P], mt[:, k, :], ident).then_inc(s["t"], 1)

            def states(i, k, j):
                after(e, s["ag"], i + 1)
                after(e, s["v"], i - 1)
                e.matmul(px[:, k, 0:2 * P], BD[f"R{l}"], hdw(i), start=True, stop=False, skip_group_check=True)
                e.matmul(px[:, k, 0:P], ag[:, k, :, :], ident, start=False, stop=True, skip_group_check=True).then_inc(s["x"], 1)
            staged(e, (0, rows), (1, states))
            e.wait_ge(s["f"], 1)
            e.matmul(pg[:, :], g["groups"], f[:, 0:2], start=True, stop=True).then_inc(s["p"], 1)

        @block.scalar
        def _(e):
            def body(i, k, j):
                after(e, s["x"], i + 1)
                after(e, s["y"], i - 1)
                e.activation(v[:, k].rearrange("p w c -> p (w c)"), px[:, k, 0:2 * P], ACT.Identity, bias=V[f"b{l}"]).then_inc(s["v"], 1)
            each_block(e, body)
            e.wait_ge(s["q"], 3)
            e.activation(f[:, 4:5], f[:, 4:5], ACT.Sqrt, bias=V["eps"]).then_inc(s["q"], 1)

        @block.gpsimd
        def _(e):
            def states(i, k, j):
                after(e, s["lk"] if l < 3 else s["v"], i + 1)
                e.tensor_tensor(hdw(i), v[:, k], hdw(i), ALU.add).then_inc(s["y"], 1)

            def ends(i, k, j):
                after(e, s["y"], i + 1)
                after(e, s["st"], 2 * (i - 1))
                e.tensor_tensor(ym[:, k], hdw(i), bc_first(at(g["last"], i), 2), ALU.mult).then_inc(s["ym"], 1)
            staged(e, (0, states), (1, ends))

        @block.vector
        def _(e):
            def carried(i, k, j):
                after(e, s["t"], i - 1)
                e.scalar_tensor_tensor(mt[:, k, :], at(g["first"], i), g["carry"][:, 0:1], at(MSG, i), ALU.mult, ALU.add).then_inc(s["mt"], 1)

            def means(i, k, j):
                after(e, s["t"], i + 1)
                after(e, s[f"r{k}"], 16 * (j - 1))
                after(e, s["x"], i - 1)
                e.tensor_tensor(ag[:, k], pt[:, k, 0:P].rearrange("p (q f) -> p q f", q=Q), bc(tiles(g["rcE"], i), F), ALU.mult).then_inc(s["ag"], 1)

            def leaky(i, k, j):
                after(e, s["v"], i + 1)
                e.scalar_tensor_tensor(v[:, k], v[:, k], SLOPE, v[:, k], ALU.mult, ALU.max).then_inc(s["lk"], 1)

            def statistics(i, k, j):
                after(e, s["ym"], i + 1)
                for w in range(2):
                    e.bn_stats(stats[:, w, bass.ds(i, 1), :].rearrange("p b c -> p (b c)"), ym[:, k, w, :]).then_inc(s["st"], 1)
            staged(e, *([(3, leaky)] if l < 3 else []), (1, means), (0, carried), (5, statistics))
            e.wait_ge(s["st"], 2 * BLOCKS)
            for w in range(2):
                e.bn_aggr(sums[:, w, :], stats[:, w].rearrange("p b (t c) -> p (b t) c", c=3)).then_inc(s["n"], 1)
            e.wait_ge(s["n"], 2)
            for w, (mean, var) in enumerate(((sums[:, 0, 0:1], sums[:, 0, 1:2]), (sums[:, 1, 0:1], sums[:, 1, 1:2]))):
                e.scalar_tensor_tensor(var, mean, mean, var, ALU.mult, ALU.add).then_inc(s["n"], 1)
            e.wait_ge(s["n"], 4)
            e.tensor_tensor(f[:, 2:4], sums[:, 0, :], sums[:, 1, :], ALU.subtract).then_inc(s["n"], 1)
            e.scalar_tensor_tensor(f[:, 1:2], agg[:, 0:1], agg[:, 0:1], agg[:, 1:2], ALU.mult, ALU.add).then_inc(s["n"], 1)
            e.tensor_copy(f[:, 0:1], agg[:, 0:1]).then_inc(s["n"], 1)
            e.wait_ge(s["n"], 7)
            e.tensor_scalar(f[:, 2:4], f[:, 2:4], float(EC), None, ALU.mult).then_inc(s["n"], 1)
            e.wait_ge(s["n"], 8)
            e.scalar_tensor_tensor(f[:, 0:2], f[:, 0:2], float(N // Q), f[:, 2:4], ALU.mult, ALU.add).then_inc(s["f"], 1)
            e.wait_ge(s["p"], 1)
            e.tensor_scalar(f[:, 4:6], pg[:, :], 1.0 / N, None, ALU.mult).then_inc(s["q"], 1)
            e.wait_ge(s["q"], 1)
            e.tensor_tensor(f[:, 6:7], f[:, 4:5], f[:, 4:5], ALU.mult).then_inc(s["n"], 1)
            e.tensor_copy(f[:, 7:8], f[:, 4:5]).then_inc(s["q"], 1)
            e.wait_ge(s["n"], 9)
            e.wait_ge(s["q"], 2)
            e.tensor_tensor(f[:, 4:5], f[:, 5:6], f[:, 6:7], ALU.subtract).then_inc(s["q"], 1)
            e.wait_ge(s["q"], 4)
            e.reciprocal(f[:, 5:6], f[:, 4:5]).then_inc(s["n"], 1)
            e.wait_ge(s["n"], 10)
            e.tensor_tensor(V[f"a{l}"], V[f"g{l}"], f[:, 5:6], ALU.mult).then_inc(s["n"], 1)
            e.wait_ge(s["n"], 11)
            e.tensor_tensor(f[:, 6:7], f[:, 7:8], V[f"a{l}"], ALU.mult).then_inc(s["n"], 1)
            e.wait_ge(s["n"], 12)
            e.tensor_tensor(V[f"c{l}"], V[f"be{l}"], f[:, 6:7], ALU.subtract).then_inc(s["n"], 1)
            e.wait_ge(s["n"], 13)
            flat = HDW[:, :, :, :].rearrange("p b w c -> p (b w c)")
            e.tensor_scalar(flat, flat, V[f"a{l}"], V[f"c{l}"], ALU.mult, ALU.add).then_inc(s["norm"], 1)


def xsd_block(g, i):
    return g["xsd"][bass.ds(i, 1)].rearrange("b p c -> (b p) c")


def hops_start(nc, g):
    V, BD, sb, psum, ident, HS, HDW, MSG = g["V"], g["BD"], g["sb"], g["psum"], g["ident"], g["HS"], g["HDW"], g["MSG"]
    with ExitStack() as c:
        s = sems(c, nc, "hp", GATHER + " xi0 xi1 xo0 xo1 ex ev ey hn hc t1 hm m mw " + ln_sems("e"))
        px, pt, pm = psum(c, "px", [P, P]), psum(c, "pt", [P, P]), psum(c, "pm", [P, P])
        cen, var = psum(c, "cen", [P, 2, BANK]), psum(c, "var", [P, 2 * P])
        gx, st = sb(c, "gx", [P, 2, Q, F]), sb(c, "st", [P, 2, Q], I32)
        v, hn, hm = sb(c, "v", [P, P]), sb(c, "hn", [P, P]), sb(c, "hm", [P, Q, F])
        x, sq, sd, h = sb(c, "x", [P, 2, 2 * P]), sb(c, "sq", [P, 2 * P]), sb(c, "sd", [P, 2, 2 * P]), sb(c, "h", [P, 2, 2 * P])
        xi = sb(c, "xi", [P, 2, 2 * P])

        def te(k):
            return {"x": x[:, k], "cen": cen[:, k, 0:2 * P], "sq": sq[:, :], "var": var[:, :], "sd": sd[:, k], "rs": sd[:, k], "h": h[:, k]}
        block = c.enter_context(nc.Block())

        @block.gpsimd
        def _(e):
            each_block(e, lambda i, k, j: gather(e, s, st, k, j, i, g["ptrI"], g["runs"], gx, s["ex"]))

        @block.sync
        def _(e):
            def load(i, k, j):
                after(e, s["xe"], i - 1)
                e.dma_start(xi[:, k], xsd_block(g, i)).then_inc(s[f"xi{k}"], 16)

            def store(i, k, j):
                after(e, s["xe"], i + 1)
                e.dma_start(xsd_block(g, i), x[:, k]).then_inc(s[f"xo{k}"], 16)
            each_block_ahead(e, load, store)
            for k in range(2):
                e.wait_ge(s[f"xo{k}"], 16 * (BLOCKS // 2))

        @block.tensor
        def _(e):
            def sources(i, k, j):
                after(e, s[f"got{k}"], 64 * j)
                after(e, s["ev"], i)
                e.matmul(px[:, :], BD["R3"], at(HS, i), start=True, stop=False)
                e.matmul(px[:, :], gx[:, k, :, :], ident, start=False, stop=True).then_inc(s["ex"], 1)

            def rows(i, k, j):
                after(e, s["he"], i + 1)
                after(e, s["hm"], i)
                e.transpose(pt[:, :], h[:, k, 0:P], ident).then_inc(s["t1"], 1)

            def messages(i, k, j):
                after(e, s["hm"], i + 1)
                after(e, s["mw"], i)
                e.transpose(pm[:, :], hm[:, :, :], ident).then_inc(s["m"], 1)
            staged(e, (1, lambda i, k, j: ln_centre(e, s, "e", te(k), i, g, 2)),
                   (0, sources),
                   (2, rows),
                   (1, lambda i, k, j: ln_mean(e, s, "e", te(k), i, g)),
                   (2, messages))

        @block.scalar
        def _(e):
            def layer(i, k, j):
                after(e, s["ex"], i + 1)
                after(e, s["ey"], i)
                e.activation(v[:, :], px[:, :], ACT.Identity, bias=V["b3"]).then_inc(s["ev"], 1)

            def norm(i, k, j):
                after(e, s["ey"], i + 1)
                after(e, s["xe"], i)
                e.activation(hn[:, :], v[:, :], ACT.Identity, bias=V["c3"], scale=V["a3"]).then_inc(s["hn"], 1)
            staged(e, (1, lambda i, k, j: ln_square(e, s, "e", te(k), i)),
                   (0, layer),
                   (0, norm),
                   (1, lambda i, k, j: ln_root(e, s, "e", te(k), i, g)))

        @block.vector
        def _(e):
            def layer(i, k, j):
                after(e, s["ev"], i + 1)
                after(e, s["hn"], i)
                e.tensor_tensor(v[:, :], v[:, :], at(HS, i), ALU.add).then_inc(s["ey"], 1)

            def messages(i, k, j):
                after(e, s["t1"], i + 1)
                after(e, s["m"], i)
                e.tensor_tensor(hm[:, :, :], pt[:, :].rearrange("p (q f) -> p q f", q=Q), bc(tiles(g["dinvS"], i), F), ALU.mult).then_inc(s["hm"], 1)

            def residual(i, k, j):
                after(e, s[f"xi{k}"], 16 * j)
                after(e, s[f"xo{k}"], 16 * (j - 1))
                e.tensor_tensor(x[:, k, P:2 * P], xi[:, k, P:2 * P], HDW[:, bass.ds(i, 1), 0, :].rearrange("p b c -> p (b c)"), ALU.add)
                after(e, s["hn"], i + 1)
                e.tensor_tensor(x[:, k, 0:P], xi[:, k, 0:P], hn[:, :], ALU.add).then_inc(s["xe"], 1)

            def states(i, k, j):
                after(e, s["t1"], i - 1)
                after(e, s["hc"], i - 1)
                ln_vector(e, s, "e", te(k), i)

            def keep(i, k, j):
                after(e, s["he"], i + 1)
                copy(e, at(HS, i), h[:, k, 0:P])
                copy(e, HDW[:, bass.ds(i, 1), 0, :].rearrange("p b c -> p (b c)"), h[:, k, P:2 * P]).then_inc(s["hc"], 1)

            def write(i, k, j):
                after(e, s["m"], i + 1)
                copy(e, at(MSG, i), pm[:, :]).then_inc(s["mw"], 1)
            staged(e, (3, write), (0, layer), (2, messages), (0, residual), (1, states), (1, keep))


def hop_end(nc, g, n):
    sb, psum, ident, HDW, MSG = g["sb"], g["psum"], g["ident"], g["HDW"], g["MSG"]
    with ExitStack() as c:
        s = sems(c, nc, f"he{n}", "mt t ag r0 r1 x y")
        pt, px = psum(c, "pt", [P, 2, BANK]), psum(c, "px", [P, 2, BANK])
        mt, ag = sb(c, "mt", [P, 2, P]), sb(c, "ag", [P, 2, Q, F])
        block = c.enter_context(nc.Block())

        @block.sync
        def _(e):
            def store(i, k, j):
                after(e, s["ag"], i + 1)
                e.dma_start(g["runs"][0:EP, :].rearrange("(q b p) f -> b p q f", q=Q, b=BLOCKS)[bass.ds(i, 1)].rearrange("b p q f -> (b p) q f"),
                            ag[:, k]).then_inc(s[f"r{k}"], 16)
            each_block(e, store)
            for k in range(2):
                e.wait_ge(s[f"r{k}"], 16 * (BLOCKS // 2))

        @block.tensor
        def _(e):
            def rows(i, k, j):
                after(e, s["mt"], i + 1)
                after(e, s["ag"], i - 1)
                e.transpose(pt[:, k, 0:P], mt[:, k], ident).then_inc(s["t"], 1)

            def states(i, k, j):
                after(e, s["ag"], i + 1)
                after(e, s["y"], i - 1)
                e.transpose(px[:, k, 0:P], ag[:, k, :, :], ident).then_inc(s["x"], 1)
            staged(e, (0, rows), (1, states))

        @block.vector
        def _(e):
            def carried(i, k, j):
                after(e, s["t"], i - 1)
                e.scalar_tensor_tensor(mt[:, k], at(g["first"], i), g["carry"][:, 0:1], at(MSG, i), ALU.mult, ALU.add).then_inc(s["mt"], 1)

            def sums(i, k, j):
                after(e, s["t"], i + 1)
                after(e, s[f"r{k}"], 16 * (j - 1))
                after(e, s["x"], i - 1)
                e.tensor_tensor(ag[:, k], pt[:, k, 0:P].rearrange("p (q f) -> p q f", q=Q), bc(tiles(g["dinvD"], i), F), ALU.mult).then_inc(s["ag"], 1)

            def states(i, k, j):
                after(e, s["x"], i + 1)
                d = HDW[:, bass.ds(i, 1), 0, :].rearrange("p b c -> p (b c)")
                e.tensor_tensor(d, px[:, k, 0:P], d, ALU.add).then_inc(s["y"], 1)
            staged(e, (0, carried), (1, sums), (3, states))


def hop_gather(nc, g, n):
    sb, psum, ident, HS, MSG = g["sb"], g["psum"], g["ident"], g["HS"], g["MSG"]
    with ExitStack() as c:
        s = sems(c, nc, f"hg{n}", GATHER + " t hs hm m mw")
        pt, pm = psum(c, "pt", [P, P]), psum(c, "pm", [P, P])
        gx, st, hm = sb(c, "gx", [P, 2, Q, F]), sb(c, "st", [P, 2, Q], I32), sb(c, "hm", [P, Q, F])
        block = c.enter_context(nc.Block())

        @block.gpsimd
        def _(e):
            def step(i, k, j):
                after(e, s["hm"], i - 1)
                gather(e, s, st, k, j, i, g["ptrI"], g["runs"], gx, s["t"])
            each_block(e, step)

        @block.tensor
        def _(e):
            def step(i, k, j):
                after(e, s[f"got{k}"], 64 * j)
                after(e, s["hs"], i)
                e.transpose(pt[:, :], gx[:, k, :, :], ident).then_inc(s["t"], 1)
                after(e, s["hm"], i + 1)
                after(e, s["mw"], i)
                e.transpose(pm[:, :], hm[:, :, :], ident).then_inc(s["m"], 1)
            each_block(e, step)

        @block.vector
        def _(e):
            def step(i, k, j):
                after(e, s[f"got{k}"], 64 * j)
                after(e, s["m"], i)
                e.tensor_tensor(hm[:, :, :], gx[:, k], bc(tiles(g["dinvS"], i), F), ALU.mult).then_inc(s["hm"], 1)
                after(e, s["t"], i + 1)
                e.tensor_tensor(at(HS, i), pt[:, :], at(HS, i), ALU.add).then_inc(s["hs"], 1)
                after(e, s["m"], i + 1)
                copy(e, at(MSG, i), pm[:, :]).then_inc(s["mw"], 1)
            each_block(e, step)


def dense_end(nc, g):
    V, BD, sb, psum, ident = g["V"], g["BD"], g["sb"], g["psum"], g["ident"]
    with ExitStack() as c:
        s = sems(c, nc, "de", "yi0 yi1 xi0 xi1 oo0 oo1 y3 ab ga gb o ov o2 ot oc xc zero " + ln_sems("1") + " " + ln_sems("2"))
        cen1, var1, cen2, var2 = (psum(c, n, [P, NB]) for n in ("cen1", "var1", "cen2", "var2"))
        pa, pb, po = psum(c, "pa", [P, NB]), psum(c, "pb", [P, NB]), psum(c, "po", [P, NB])
        pt = psum(c, "pt", [NP, 4, P])
        yi, y, xi, x, xc = (g["MSG"][:, 2 * n * NB:2 * (n + 1) * NB].rearrange("p (k c) -> p k c", k=2) for n in range(5))
        h1, h2 = g["MSG"][:, 10 * NB:11 * NB], g["MSG"][:, 11 * NB:12 * NB]
        sq1, sd1, sq2, sd2 = (sb(c, n, [P, NB]) for n in ("sq1", "sd1", "sq2", "sd2"))
        ga, gb, o = sb(c, "ga", [P, NB]), sb(c, "gb", [P, NB]), sb(c, "o", [P, NB])
        zero = sb(c, "zero", [P, 1])
        ot = sb(c, "ot", [NP, 2, Q, 4, F])

        def t1(k):
            return {"x": y[:, k], "cen": cen1[:, :], "sq": sq1[:, :], "var": var1[:, :], "sd": sd1[:, :], "rs": sd1[:, :], "h": h1}

        def t2(k):
            return {"x": x[:, k], "cen": cen2[:, :], "sq": sq2[:, :], "var": var2[:, :], "sd": sd2[:, :], "rs": sd2[:, :], "h": h2}
        block = c.enter_context(nc.Block())
        outv = g["out"].rearrange("(q b p n) f -> b p q (n f)", q=Q, b=BLOCKS, p=NP)

        @block.sync
        def _(e):
            def load(i, k, j):
                after(e, s["x1"], i - 1)
                e.dma_start(yi[:, k], g["yf"][bass.ds(i + 3 * BLOCKS, 1)].rearrange("b p c -> (b p) c")).then_inc(s[f"yi{k}"], 16)
                e.dma_start(xi[:, k], g["x0f"][bass.ds(i, 1)].rearrange("b p c -> (b p) c")).then_inc(s[f"xi{k}"], 16)

            def store(i, k, j):
                after(e, s["oc"], i + 1)
                e.dma_start(outv[bass.ds(i, 1)].rearrange("b p q w -> (b p) q w"), ot[:, k].rearrange("p q n f -> p q (n f)")).then_inc(s[f"oo{k}"], 16)
            staged(e, (0, load), (4, store))
            for k in range(2):
                e.wait_ge(s[f"oo{k}"], 16 * (BLOCKS // 2))

        @block.tensor
        def _(e):
            def rows(i, k, j):
                after(e, s["o2"], i + 1)
                after(e, s["oc"], i)
                for n in range(4):
                    mm = e.transpose(pt[:, n, :], o[:, n * NP:(n + 1) * NP], ident)
                mm.then_inc(s["ot"], 1)

            def hidden(i, k, j):
                after(e, s["h2"], i + 1)
                after(e, s["gb"], i)
                e.matmul(pa[:, :], BD["w2aA"], h2, start=True, stop=True)
                e.matmul(pb[:, :], BD["w2aB"], h2, start=True, stop=True).then_inc(s["ab"], 1)

            def result(i, k, j):
                after(e, s["ga"], i + 1)
                after(e, s["gb"], i + 1)
                after(e, s["ov"], i)
                e.matmul(po[:, :], BD["w2bA"], ga[:, :], start=True, stop=False)
                e.matmul(po[:, :], BD["w2bB"], gb[:, :], start=False, stop=True).then_inc(s["o"], 1)
            staged(e, (0, lambda i, k, j: ln_centre(e, s, "1", t1(k), i, g)),
                   (0, lambda i, k, j: ln_mean(e, s, "1", t1(k), i, g)),
                   (1, lambda i, k, j: ln_centre(e, s, "2", t2(k), i, g)),
                   (3, rows),
                   (2, hidden),
                   (1, lambda i, k, j: ln_mean(e, s, "2", t2(k), i, g)),
                   (2, result))

        @block.scalar
        def _(e):
            def norm(i, k, j):
                after(e, s[f"yi{k}"], 16 * j)
                after(e, s["x2"], i - 1)
                e.activation(y[:, k], yi[:, k], ACT.Identity, bias=V["c3"], scale=V["a3"]).then_inc(s["y3"], 1)

            def rows(i, k, j):
                after(e, s["ot"], i + 1)
                after(e, s[f"oo{k}"], 16 * (j - 1))
                e.copy(ot[:, k].rearrange("p q n f -> p n q f"), pt[:, :, :].rearrange("p n (q f) -> p n q f", q=Q)).then_inc(s["oc"], 1)

            def hidden(i, k, j):
                after(e, s["ab"], i + 1)
                after(e, s["o"], i)
                e.activation(ga[:, :], pa[:, :], ACT.Relu, bias=V["b2aA"]).then_inc(s["ga"], 1)
                e.activation(gb[:, :], pb[:, :], ACT.Relu, bias=V["b2aB"]).then_inc(s["gb"], 1)

            def result(i, k, j):
                after(e, s["o"], i + 1)
                after(e, s["ot"], i)
                e.activation(o[:, :], po[:, :], ACT.Identity, bias=V["b2b"]).then_inc(s["ov"], 1)
            staged(e, (0, norm),
                   (1, lambda i, k, j: ln_square(e, s, "1", t1(k), i)),
                   (1, lambda i, k, j: ln_root(e, s, "1", t1(k), i, g)),
                   (2, lambda i, k, j: ln_square(e, s, "2", t2(k), i)),
                   (4, rows),
                   (3, hidden),
                   (2, lambda i, k, j: ln_root(e, s, "2", t2(k), i, g)),
                   (3, result))

        @block.vector
        def _(e):
            def hops(i, k, j):
                after(e, s["h1"], i + 1)
                after(e, s["xc"], i - 1)
                e.scalar_tensor_tensor(x[:, k], h1, 0.25, y[:, k], ALU.mult, ALU.add).then_inc(s["x2"], 1)

            def second(i, k, j):
                after(e, s["ab"], i)
                ln_vector(e, s, "2", t2(k), i)
            staged(e, (1, lambda i, k, j: ln_vector(e, s, "1", t1(k), i)),
                   (1, hops),
                   (2, second))

        @block.gpsimd
        def _(e):
            e.memset(zero[:, :], 0.0).then_inc(s["zero"], 1)
            e.wait_ge(s["zero"], 1)

            def enter(i, k, j):
                after(e, s[f"xi{k}"], 16 * j)
                after(e, s["y3"], i + 1)
                e.tensor_tensor(y[:, k], xi[:, k], y[:, k], ALU.add).then_inc(s["x1"], 1)

            def result(i, k, j):
                after(e, s["ov"], i + 1)
                e.tensor_tensor(o[:, :], o[:, :], xc[:, k], ALU.add).then_inc(s["o2"], 1)

            def keep(i, k, j):
                after(e, s["x2"], i + 1)
                after(e, s["o2"], i - 1)
                e.tensor_tensor(xc[:, k], x[:, k], zero[:, :].broadcast_to([P, NB]), ALU.add).then_inc(s["xc"], 1)
            staged(e, (0, enter), (3, result), (1, keep))


def edge_mlp(nc, g):
    V, BD, sb, psum, ident, HS, HDW, MSG = g["V"], g["BD"], g["sb"], g["psum"], g["ident"], g["HS"], g["HDW"], g["MSG"]
    with ExitStack() as c:
        s = sems(c, nc, "em", GATHER + " xi0 xi1 xo0 xo1 at0 at1 pad t hs hc att atc j h1 m mw " + ln_sems("e"))
        px, pat = psum(c, "px", [P, P]), psum(c, "pat", [P, P])
        cen, var = psum(c, "cen", [P, 2, BANK]), psum(c, "var", [P, 2 * P])
        pj, pm = psum(c, "pj", [P, 3, P]), psum(c, "pm", [P, 2, P])
        gx, st = sb(c, "gx", [P, 2, Q, F]), sb(c, "st", [P, 2, Q], I32)
        hs, x, xi = sb(c, "hs", [P, P]), sb(c, "x", [P, 2, 2 * P]), sb(c, "xi", [P, 2, 2 * P])
        sq, sd, h = sb(c, "sq", [P, 2 * P]), sb(c, "sd", [P, 2, 2 * P]), sb(c, "h", [P, 2, 2 * P])
        atr, atf, h1 = sb(c, "atr", [P, 2, Q, F]), sb(c, "atf", [P, 2, P]), sb(c, "h1", [P, 3, P])

        def te(k):
            return {"x": x[:, k], "cen": cen[:, k, 0:2 * P], "sq": sq[:, :], "var": var[:, :], "sd": sd[:, k], "rs": sd[:, k], "h": h[:, k]}
        block = c.enter_context(nc.Block())

        @block.gpsimd
        def _(e):
            each_block(e, lambda i, k, j: gather(e, s, st, k, j, i, g["ptrI"], g["runs"], gx, s["t"]))

        @block.sync
        def _(e):
            e.wait_ge(s["pad"], 2)

            def load(i, k, j):
                after(e, s["xe"], i - 1)
                e.dma_start(xi[:, k], xsd_block(g, i)).then_inc(s[f"xi{k}"], 16)
                after(e, s["att"], i - 1)
                e.dma_start(atr[:, k, :, 0:DE], g["attr16"].rearrange("(q b p) d -> b p q d", q=Q, b=BLOCKS)[bass.ds(i, 1)]
                            .rearrange("b p q d -> (b p) q d")).then_inc(s[f"at{k}"], 16)

            def store(i, k, j):
                after(e, s["xe"], i + 1)
                e.dma_start(xsd_block(g, i), x[:, k]).then_inc(s[f"xo{k}"], 16)
            each_block_ahead(e, load, store)
            for k in range(2):
                e.wait_ge(s[f"xo{k}"], 16 * (BLOCKS // 2))

        @block.tensor
        def _(e):
            def sources(i, k, j):
                after(e, s[f"got{k}"], 64 * j)
                after(e, s["hs"], i)
                e.transpose(px[:, :], gx[:, k, :, :], ident).then_inc(s["t"], 1)

            def attributes(i, k, j):
                after(e, s[f"at{k}"], 16 * j)
                after(e, s["atc"], i)
                e.transpose(pat[:, :], atr[:, k, :, :], ident).then_inc(s["att"], 1)

            def hidden(i, k, j):
                after(e, s["he"], i + 1)
                after(e, s["atc"], i + 1)
                after(e, s["h1"], i)
                for n in range(3):
                    e.matmul(pj[:, n, :], BD[f"w1x{n}"], h[:, k, 0:P], start=True, stop=False)
                    mm = e.matmul(pj[:, n, :], BD[f"w1e{n}"], atf[:, k], start=False, stop=True)
                mm.then_inc(s["j"], 1)

            def messages(i, k, j):
                after(e, s["h1"], i + 1)
                after(e, s["mw"], i)
                for w, name in enumerate(("wcA", "wcB")):
                    for n in range(3):
                        mm = e.matmul(pm[:, w, :], BD[f"{name}{n}"], h1[:, n, :], start=(n == 0), stop=(n == 2))
                mm.then_inc(s["m"], 1)
            staged(e, (1, lambda i, k, j: ln_mean(e, s, "e", te(k), i, g)),
                   (0, sources),
                   (2, hidden),
                   (1, attributes),
                   (0, lambda i, k, j: ln_centre(e, s, "e", te(k), i, g, 2)),
                   (2, messages))

        @block.scalar
        def _(e):
            def attributes(i, k, j):
                after(e, s["att"], i + 1)
                after(e, s["j"], i - 1)
                e.copy(atf[:, k], pat[:, :]).then_inc(s["atc"], 1)

            def hidden(i, k, j):
                after(e, s["j"], i + 1)
                after(e, s["m"], i)
                e.activation(h1[:, :, :], pj[:, :, :], ACT.Relu).then_inc(s["h1"], 1)
            staged(e, (1, lambda i, k, j: ln_root(e, s, "e", te(k), i, g)),
                   (2, hidden),
                   (1, attributes),
                   (0, lambda i, k, j: ln_square(e, s, "e", te(k), i)))

        @block.vector
        def _(e):
            e.memset(atr[:, :, :, :], 0.0).then_inc(s["pad"], 1)
            e.wait_ge(s["pad"], 1)
            e.memset(atr[:, :, :, DE:DE + 1], 1.0).then_inc(s["pad"], 1)

            def d(i):
                return HDW[:, bass.ds(i, 1), 0, :].rearrange("p b c -> p (b c)")

            def sources(i, k, j):
                after(e, s["t"], i + 1)
                after(e, s["xe"], i)
                e.tensor_tensor(hs[:, :], px[:, :], at(HS, i), ALU.add).then_inc(s["hs"], 1)

            def residual(i, k, j):
                after(e, s[f"xi{k}"], 16 * j)
                after(e, s[f"xo{k}"], 16 * (j - 1))
                e.scalar_tensor_tensor(x[:, k, P:2 * P], d(i), 0.25, xi[:, k, P:2 * P], ALU.mult, ALU.add)
                after(e, s["hs"], i + 1)
                e.scalar_tensor_tensor(x[:, k, 0:P], hs[:, :], 0.25, xi[:, k, 0:P], ALU.mult, ALU.add).then_inc(s["xe"], 1)

            def states(i, k, j):
                after(e, s["j"], i - 1)
                after(e, s["hc"], i - 1)
                ln_vector(e, s, "e", te(k), i)

            def keep(i, k, j):
                after(e, s["he"], i + 1)
                copy(e, d(i), h[:, k, P:2 * P]).then_inc(s["hc"], 1)

            def write(i, k, j):
                after(e, s["m"], i + 1)
                copy(e, at(MSG, i), pm[:, 0, :])
                copy(e, at(HS, i), pm[:, 1, :]).then_inc(s["mw"], 1)
            staged(e, (3, write), (0, sources), (0, residual), (1, states), (1, keep))


def node_mlp(nc, g):
    V, BD, sb, psum, ident, HDW = g["V"], g["BD"], g["sb"], g["psum"], g["ident"], g["HDW"]
    with ExitStack() as c:
        s = sems(c, nc, "nm", "bias xi0 xi1 mt t ag p g0 o ov o2 ot oc stg0 stg1 sent0 sent1")
        pt, ph = psum(c, "pt", [P, 2, P]), psum(c, "ph", [P, 2, P])
        po, pr = psum(c, "po", [P, P]), psum(c, "pr", [P, P])
        mt, ag, x = sb(c, "mt", [P, 2, P]), sb(c, "ag", [P, 2, Q, F]), sb(c, "x", [P, 2, 2 * P])
        gh, o, o2 = sb(c, "gh", [P, 2, P]), sb(c, "o", [P, P]), sb(c, "o2", [P, P])
        ot, st, bias = sb(c, "ot", [P, 2, Q, F]), sb(c, "st", [P, 2, Q], I32), sb(c, "bias", [P, 2])
        block = c.enter_context(nc.Block())

        @block.sync
        def _(e):
            def load(i, k, j):
                after(e, s["o2"], i - 1)
                e.dma_start(x[:, k], xsd_block(g, i)).then_inc(s[f"xi{k}"], 16)
            each_block(e, load)

        @block.gpsimd
        def _(e):
            def step(i, k, j):
                after(e, s["oc"], i + 1)
                after(e, s[f"sent{k}"], 64 * (j - 1))
                stage_indices(e, s, st, k, j, g["outI"], i)
                for q in range(Q):
                    e.indirect_dma_start(g["out"], bass.IndirectOffsetOnAxis(ap=st[:, k, q:q + 1], axis=0), ot[:, k, q, :], None,
                                         bounds_check=N - 1, oob_is_err=False).then_inc(s[f"sent{k}"], 16)
            each_block(e, step)
            for k in range(2):
                e.wait_ge(s[f"sent{k}"], 64 * (BLOCKS // 2))

        @block.tensor
        def _(e):
            def means(i, k, j):
                after(e, s["mt"], 2 * (i + 1))
                after(e, s["ag"], i)
                for w in range(2):
                    mm = e.transpose(pt[:, w, :], mt[:, w, :], ident)
                mm.then_inc(s["t"], 1)

            def hidden(i, k, j):
                after(e, s["ag"], i + 1)
                after(e, s["g0"], 2 * i)
                d = HDW[:, bass.ds(i, 1), 0, :].rearrange("p b c -> p (b c)")
                for w, name in enumerate(("w2aA", "w2aB")):
                    e.matmul(ph[:, w, :], BD[name], d, start=True, stop=False)
                    mm = e.matmul(ph[:, w, :], ag[:, w, :, :], ident, start=False, stop=True)
                mm.then_inc(s["p"], 1)

            def result(i, k, j):
                after(e, s["g0"], 2 * (i + 1))
                after(e, s["ov"], i)
                e.matmul(po[:, :], BD["w2bA"], gh[:, 0, :], start=True, stop=False)
                e.matmul(po[:, :], BD["w2bB"], gh[:, 1, :], start=False, stop=True).then_inc(s["o"], 1)

            def rows(i, k, j):
                after(e, s["o2"], i + 1)
                after(e, s["oc"], i)
                e.transpose(pr[:, :], o2[:, :], ident).then_inc(s["ot"], 1)
            staged(e, (1, hidden), (0, means), (2, rows), (1, result))

        @block.scalar
        def _(e):
            e.wait_ge(s["bias"], 2)

            def hidden(i, k, j):
                after(e, s["p"], i + 1)
                after(e, s["o"], i)
                for w in range(2):
                    e.activation(gh[:, w, :], ph[:, w, :], ACT.Relu, bias=bias[:, w:w + 1]).then_inc(s["g0"], 1)

            def result(i, k, j):
                after(e, s["o"], i + 1)
                after(e, s["o2"], i)
                e.activation(o[:, :], po[:, :], ACT.Identity, bias=V["b2b"]).then_inc(s["ov"], 1)

            def rows(i, k, j):
                after(e, s["ot"], i + 1)
                after(e, s[f"sent{k}"], 64 * (j - 1))
                e.copy(ot[:, k], pr[:, :].rearrange("p (q f) -> p q f", q=Q)).then_inc(s["oc"], 1)
            staged(e, (1, hidden), (2, rows), (1, result))

        @block.vector
        def _(e):
            e.tensor_tensor(bias[:, 0:1], V["b2aA"], V["bcA"], ALU.add).then_inc(s["bias"], 1)
            e.tensor_tensor(bias[:, 1:2], V["b2aB"], V["bcB"], ALU.add).then_inc(s["bias"], 1)

            def carried(i, k, j):
                after(e, s["t"], i)
                for w, m in enumerate((g["MSG"], g["HS"])):
                    e.scalar_tensor_tensor(mt[:, w, :], at(g["first"], i), g["carry"][:, w:w + 1], at(m, i), ALU.mult, ALU.add).then_inc(s["mt"], 1)

            def means(i, k, j):
                after(e, s["t"], i + 1)
                after(e, s["p"], i)
                r = tiles(g["rcE"], i)
                for w in range(2):
                    ins = e.tensor_tensor(ag[:, w], pt[:, w, :].rearrange("p (q f) -> p q f", q=Q), bc(r, F), ALU.mult)
                ins.then_inc(s["ag"], 1)

            def result(i, k, j):
                after(e, s["ov"], i + 1)
                after(e, s[f"xi{k}"], 16 * j)
                after(e, s["ot"], i)
                e.tensor_tensor(o2[:, :], o[:, :], x[:, k, P:2 * P], ALU.add).then_inc(s["o2"], 1)
            staged(e, (0, carried), (0, means), (1, result))


def build(nc, a, out):
    top = ExitStack()
    with top:
        def dram(name, shape, dt=F32):
            return nc.dram_tensor(name, shape, dt, kind="Internal").ap()

        used = {}

        def unique(name):
            used[name] = used.get(name, 0) + 1
            return name if used[name] == 1 else f"{name}_{used[name]}"

        def sb(c, name, shape, dt=F32):
            return c.enter_context(nc.sbuf_tensor(unique(name), shape, dt))

        def psum(c, name, shape):
            return c.enter_context(nc.psum_tensor(unique(name), shape, F32))

        g = {"a": a, "out": out, "sb": sb, "psum": psum,
             "table": dram("table", [TN, TW]),
             "runs": dram("runs", [EP + P, F]),
             "srcflat": dram("srcflat", [EP]), "cntflat": dram("cntflat", [EP]),
             "sameflat": dram("sameflat", [EP], BF16), "lastflat": dram("lastflat", [EP], BF16),
             "attr3": dram("attr3", [EP, 3]), "attr16": dram("attr16", [EP, DE]),
             "x0f": dram("x0f", [BLOCKS, P, NB]),
             "yf": dram("yf", [4 * BLOCKS, P, NB]),
             "xsd": dram("xsd", [BLOCKS, P, 2 * P])}
        for n in ("same", "last", "first"):
            g[n] = sb(top, n, [P, EC], BF16)
        g["HS"], g["MSG"] = sb(top, "HS", [P, EC]), sb(top, "MSG", [P, EC])
        g["HDW"] = sb(top, "HDW", [P, BLOCKS, 2, P])
        g["basis"] = sb(top, "basis", [P, 3, ROWS, KS])
        for n in ("srcE", "dstE", "lastE", "cntE", "cntS", "rcE", "dinvD", "dinvS"):
            g[n] = sb(top, n, [P, ROWS])
        for n in ("srcI", "dstI", "inI", "ptrI", "slotI", "outI"):
            g[n] = sb(top, n, [P, ROWS], I32)
        g["consts"] = sb(top, "consts", [P, len(CONSTS), P])
        for j, n in enumerate(CONSTS):
            g[n] = g["consts"][:, j, :]
        g["trashE"], g["carry"] = sb(top, "trashE", [P, Q]), sb(top, "carry", [P, 2])
        g["stats"], g["agg"] = sb(top, "stats", [P, BLOCKS, 6]), sb(top, "agg", [P, 2])
        g["bds"], g["vecs"] = sb(top, "bds", [P, len(BDS), P]), sb(top, "vecs", [P, len(VECS)])
        g["BD"] = {n: g["bds"][:, j, :] for j, n in enumerate(BDS)}
        g["V"] = {n: g["vecs"][:, j:j + 1] for j, n in enumerate(VECS)}

        setup(nc, g)
        degrees(nc, g)
        layer0(nc, g)
        place(nc, g)
        for l in (1, 2, 3):
            spline(nc, g, l)
            scan_phase(nc, g, f"scan{l}", [g["MSG"]])
            run_end(nc, g, l)
        dense_end(nc, g)
        hops_start(nc, g)
        for n in (1, 2, 3):
            scan_phase(nc, g, f"hscan{n}", [g["MSG"]])
            hop_end(nc, g, n)
            if n < 3:
                hop_gather(nc, g, n)
        edge_mlp(nc, g)
        scan_phase(nc, g, "mscan", [g["MSG"], g["HS"]])
        node_mlp(nc, g)


_NAMES = {"x": "x", "src": "src", "dst": "dst", "attr16": "edge_attr_16", "attr3": "edge_attr_3",
          "mu": "L0_gnn_mu", "sg": "L0_gnn_sigma", "b0": "L0_gnn_b"}
_NAMES |= {f"{n}{l}": f"L1_gnn_{n}{l}" for n in ("W", "R", "b", "g", "be") for l in (1, 2, 3)}
_NAMES |= {n: f"L3_gnn_{n}" for n in ("w1a", "b1a", "w1b", "b1b", "w2a", "b2a", "w2b", "b2b")}


def constants():
    import numpy as np
    p, q = np.arange(P)[:, None], np.arange(P)[None, :]
    eye, group = (p == q), (p // F == q // F)
    mean = np.where(group, np.float32(1 / F), np.float32(0))
    consts = np.stack([eye, eye - mean, mean, p % F == q % F, q == p + F], axis=1).astype(np.float32)
    pos = (np.arange(Q)[None, :] * P + p).astype(np.float32)
    eidx = (np.arange(ROWS)[None, :] * P + p).astype(np.float32)
    return {"consts": consts, "trash": pos + np.float32(N), "eidx": eidx, "before": (q < p).astype(np.float32)}


def kernel(**inputs):
    import numpy as np
    import concourse.bacc as bacc
    from concourse.bass_utils import run_bass_kernel_spmd as run

    nc = bacc.Bacc("TRN2", target_bir_lowering=False, num_devices=1)
    arrays = {n: np.ascontiguousarray(inputs[full]) for n, full in _NAMES.items()}
    arrays["W0T"] = np.ascontiguousarray(np.asarray(inputs["L0_gnn_W"]).T)
    arrays |= constants()
    args = {n: nc.dram_tensor(f"in_{n}", v.shape, mybir.dt.from_np(v.dtype), kind="ExternalInput").ap() for n, v in arrays.items()}
    out = nc.dram_tensor("out_x", (N, F), F32, kind="ExternalOutput").ap()
    build(nc, args, out)
    r = run(nc, [{f"in_{n}": v for n, v in arrays.items()}], core_ids=[0])
    return r.results[0]["out_x"]
```
